# Optimizing a Trainium2 kernel written in Bass

```python
import numpy as np
import jax
import jax.numpy as jnp

def _softmax(x, axis=-1):
    return jax.nn.softmax(x, axis=axis)

def _gelu(x):
    return jax.nn.gelu(x, approximate=True)

def _silu(x):
    return jax.nn.silu(x)

def _sigmoid(x):
    return jax.nn.sigmoid(x)

def _layernorm(x, axis=-1, eps=1e-05):
    m = jnp.mean(x, axis=axis, keepdims=True)
    v = jnp.var(x, axis=axis, keepdims=True)
    return (x - m) / jnp.sqrt(v + eps)

def _scatter_add(tgt, idx, src, axis=0):
    return tgt.at[idx].add(src)

def _segment_sum(src, seg, n):
    return jax.ops.segment_sum(src, seg, n)
kernel_name = 'mk_hybrid_d2_jaxref_r8_a70ec0'

def setup_inputs(seed: int=0):
    np.random.seed(seed)
    _w = jnp.asarray

    def _L0_attn_a_setup():
        import jax, jax.numpy as jnp
        import numpy as np
        HIDDEN = 256
        NUM_HEADS = 16
        HEAD_DIM = HIDDEN // NUM_HEADS
        SCALE = HEAD_DIM ** (-0.5)
        key = jax.random.key(seed)
        ks = jax.random.split(key, 5)
        B, S = (2, 256)
        init = HIDDEN ** (-0.5)
        return {'hidden_states': jax.random.normal(ks[0], (B, S, HIDDEN), dtype=jnp.float32), 'Wq': jax.random.normal(ks[1], (HIDDEN, HIDDEN), dtype=jnp.float32) * init, 'Wk': jax.random.normal(ks[2], (HIDDEN, HIDDEN), dtype=jnp.float32) * init, 'Wv': jax.random.normal(ks[3], (HIDDEN, HIDDEN), dtype=jnp.float32) * init, 'Wo': jax.random.normal(ks[4], (HIDDEN, HIDDEN), dtype=jnp.float32) * init}
    _L0_attn_a_in = _L0_attn_a_setup()

    def _L0_attn_b_setup():
        import jax, jax.numpy as jnp
        import numpy as np
        IN_FEATURES = 256
        HEAD_NUM = 64
        D = IN_FEATURES // HEAD_NUM
        SCALE = float(np.sqrt(D))
        key = jax.random.key(seed)
        ks = jax.random.split(key, 9)
        F = IN_FEATURES
        x = jax.random.normal(ks[0], (4, 128, F), dtype=jnp.float32)
        w = lambda k: jax.random.normal(k, (F, F), dtype=jnp.float32) * 0.02
        b = lambda k: jax.random.normal(k, (F,), dtype=jnp.float32) * 0.01
        return {'x': x, 'Wq': w(ks[1]), 'bq': b(ks[2]), 'Wk': w(ks[3]), 'bk': b(ks[4]), 'Wv': w(ks[5]), 'bv': b(ks[6]), 'Wo': w(ks[7]), 'bo': b(ks[8])}
    _L0_attn_b_in = _L0_attn_b_setup()

    def _L0_ffn_setup():
        import jax, jax.numpy as jnp
        import numpy as np
        key = jax.random.key(seed)
        k1, k2, k3, k4 = jax.random.split(key, 4)
        B, S, D_IN, D_OUT = (4, 512, 256, 256)
        x = jax.random.normal(k1, (B, S, D_IN), dtype=jnp.float32)
        weight = jax.random.normal(k2, (D_OUT, D_IN), dtype=jnp.float32) * 0.02
        scale_weight = jax.random.uniform(k3, (D_OUT,), dtype=jnp.float32, minval=0.5, maxval=1.5)
        bias = jax.random.normal(k4, (D_OUT,), dtype=jnp.float32) * 0.02
        return {'x': x, 'weight': weight, 'scale_weight': scale_weight, 'bias': bias}
    _L0_ffn_in = _L0_ffn_setup()

    def _L1_attn_a_setup():
        import jax, jax.numpy as jnp
        import numpy as np
        DIM = 256
        HEADS = 16
        HEAD_DIM = DIM // HEADS
        CHUNK = 128
        B, N = (4, 256)

        def _rmsnorm(x, w, eps):
            return x * jax.lax.rsqrt(jnp.mean(x * x, axis=-1, keepdims=True) + eps) * w

        def _weight_quant(w):
            scale = 1.0 / jnp.clip(jnp.mean(jnp.abs(w)), 1e-05, None)
            q = jnp.clip(jnp.round(w * scale), -1.0, 1.0) / scale
            return w + jax.lax.stop_gradient(q - w)

        def _forward(x, qkv_w, qkv_norm_w, proj_w, proj_norm_w, norm_w, s):
            Bb, Nn, C = x.shape
            H, D, T = (HEADS, HEAD_DIM, CHUNK)
            nc = Nn // T
            eps = jnp.finfo(x.dtype).eps
            scale = D ** (-0.5)
            h = _rmsnorm(x, qkv_norm_w, eps)
            qkv = h @ _weight_quant(qkv_w).T
            qkv = qkv.reshape(Bb, Nn, 3, H, D)
            q, k, v = (qkv[:, :, 0], qkv[:, :, 1], qkv[:, :, 2])

            def chunks(t):
                return t.reshape(Bb, nc, T, H, D).transpose(1, 0, 3, 2, 4)
            qc, kc, vc = (chunks(q), chunks(k), chunks(v))
            tt = jnp.arange(T, dtype=x.dtype)
            lam_t = jnp.exp(-s[:, None] * tt)
            lam_rev = jnp.exp(-s[:, None] * (T - tt))
            diff = tt[:, None] - tt[None, :]
            mask = jnp.where(diff >= 0, jnp.exp(-s[:, None, None] * diff), 0.0)
            lam_T = jnp.exp(-s * T)[:, None, None]

            def step(S, qkv_c):
                qi, ki, vi = qkv_c
                scores = jnp.einsum('bhtd,bhsd,hts->bhts', qi, ki, mask)
                intra = jnp.einsum('bhts,bhsd->bhtd', scores, vi)
                cross = jnp.einsum('bhtd,ht,bhde->bhte', qi, lam_t, S)
                o = scale * (intra + cross)
                kv = jnp.einsum('bhtd,ht,bhte->bhde', ki, lam_rev, vi)
                return (lam_T * S + kv, o)
            S0 = jnp.zeros((Bb, H, D, D), x.dtype)
            _, outs = jax.lax.scan(step, S0, (qc, kc, vc))
            out = outs.transpose(1, 0, 3, 2, 4).reshape(Bb, Nn, C)
            out = _rmsnorm(out, norm_w, 1e-06)
            out = _rmsnorm(out, proj_norm_w, eps) @ _weight_quant(proj_w).T
            return out
        key = jax.random.key(seed)
        ks = jax.random.split(key, 3)
        x = jax.random.normal(ks[0], (B, N, DIM), jnp.float32)
        bound = float(1.0 / np.sqrt(DIM))
        qkv_w = jax.random.uniform(ks[1], (3 * DIM, DIM), jnp.float32, -bound, bound)
        proj_w = jax.random.uniform(ks[2], (DIM, DIM), jnp.float32, -bound, bound)
        return {'x': x, 'qkv_w': qkv_w, 'qkv_norm_w': jnp.ones((DIM,), jnp.float32), 'proj_w': proj_w, 'proj_norm_w': jnp.ones((DIM,), jnp.float32), 'norm_w': jnp.ones((DIM,), jnp.float32), 's': jnp.full((HEADS,), 0.02, jnp.float32)}
    _L1_attn_a_in = _L1_attn_a_setup()

    def _L1_attn_b_setup():
        import jax, jax.numpy as jnp
        import numpy as np
        DIM = 256
        H = 16
        D = DIM // H // 2
        LAYER_NUM = 12
        LAM_INIT = 0.8 - 0.6 * float(np.exp(-0.3 * LAYER_NUM))
        SCALE = D ** (-0.5)
        EPS = 1e-05

        def _split_qk(y, b, n):
            y = y.reshape(b, n, H, D, 2)
            y = y.transpose(0, 1, 4, 2, 3)
            return y.reshape(b, n, 2 * H, D)
        key = jax.random.key(seed)
        ks = jax.random.split(key, 10)
        B, N = (4, 512)
        return {'x': jax.random.normal(ks[0], (B, N, DIM), dtype=jnp.float32), 'Wq': jax.random.normal(ks[1], (DIM, DIM), dtype=jnp.float32) * DIM ** (-0.5), 'Wk': jax.random.normal(ks[2], (DIM, DIM), dtype=jnp.float32) * DIM ** (-0.5), 'Wv': jax.random.normal(ks[3], (DIM, DIM), dtype=jnp.float32) * DIM ** (-0.5), 'Wo': jax.random.normal(ks[4], (DIM, DIM), dtype=jnp.float32) * DIM ** (-0.5), 'bo': jax.random.normal(ks[5], (DIM,), dtype=jnp.float32) * 0.01, 'lq1': jax.random.normal(ks[6], (D,), dtype=jnp.float32) * 0.1, 'lq2': jax.random.normal(ks[7], (D,), dtype=jnp.float32) * 0.1, 'lk1': jax.random.normal(ks[8], (D,), dtype=jnp.float32) * 0.1, 'lk2': jax.random.normal(ks[9], (D,), dtype=jnp.float32) * 0.1}
    _L1_attn_b_in = _L1_attn_b_setup()

    def _L1_ffn_setup():
        import jax, jax.numpy as jnp
        import numpy as np
        B, S, D, H = (4, 256, 256, 1024)

        def fwht(x):
            orig_shape = x.shape
            n = orig_shape[-1]
            x = x.reshape(-1, n)
            h = 1
            while h < n:
                xb = x.reshape(-1, n // (2 * h), 2, h)
                a = xb[:, :, 0, :]
                b = xb[:, :, 1, :]
                x = jnp.stack([a + b, a - b], axis=2).reshape(-1, n)
                h *= 2
            scale = jnp.asarray(1.0 / np.sqrt(n), dtype=x.dtype)
            return (x * scale).reshape(orig_shape)
        key = jax.random.key(seed)
        kx, k1, k2, k3 = jax.random.split(key, 4)
        x = jax.random.normal(kx, (B, S, D), dtype=jnp.float32)
        W1 = jax.random.normal(k1, (H, D), dtype=jnp.float32) * (1.0 / np.sqrt(D))
        W2 = jax.random.normal(k2, (D, H), dtype=jnp.float32) * (1.0 / np.sqrt(H))
        W3 = jax.random.normal(k3, (H, D), dtype=jnp.float32) * (1.0 / np.sqrt(D))
        return {'x': x, 'W1': W1, 'W2': W2, 'W3': W3}
    _L1_ffn_in = _L1_ffn_setup()
    _d = {'L0_attn_a_hidden_states': _L0_attn_a_in['hidden_states'], 'L0_attn_a_Wq': _L0_attn_a_in['Wq'], 'L0_attn_a_Wk': _L0_attn_a_in['Wk'], 'L0_attn_a_Wv': _L0_attn_a_in['Wv'], 'L0_attn_a_Wo': _L0_attn_a_in['Wo'], 'L0_attn_b_Wq': _L0_attn_b_in['Wq'], 'L0_attn_b_bq': _L0_attn_b_in['bq'], 'L0_attn_b_Wk': _L0_attn_b_in['Wk'], 'L0_attn_b_bk': _L0_attn_b_in['bk'], 'L0_attn_b_Wv': _L0_attn_b_in['Wv'], 'L0_attn_b_bv': _L0_attn_b_in['bv'], 'L0_attn_b_Wo': _L0_attn_b_in['Wo'], 'L0_attn_b_bo': _L0_attn_b_in['bo'], 'L0_ffn_weight': _L0_ffn_in['weight'], 'L0_ffn_scale_weight': _L0_ffn_in['scale_weight'], 'L0_ffn_bias': _L0_ffn_in['bias'], 'L1_attn_a_qkv_w': _L1_attn_a_in['qkv_w'], 'L1_attn_a_qkv_norm_w': _L1_attn_a_in['qkv_norm_w'], 'L1_attn_a_proj_w': _L1_attn_a_in['proj_w'], 'L1_attn_a_proj_norm_w': _L1_attn_a_in['proj_norm_w'], 'L1_attn_a_norm_w': _L1_attn_a_in['norm_w'], 'L1_attn_a_s': _L1_attn_a_in['s'], 'L1_attn_b_Wq': _L1_attn_b_in['Wq'], 'L1_attn_b_Wk': _L1_attn_b_in['Wk'], 'L1_attn_b_Wv': _L1_attn_b_in['Wv'], 'L1_attn_b_Wo': _L1_attn_b_in['Wo'], 'L1_attn_b_bo': _L1_attn_b_in['bo'], 'L1_attn_b_lq1': _L1_attn_b_in['lq1'], 'L1_attn_b_lq2': _L1_attn_b_in['lq2'], 'L1_attn_b_lk1': _L1_attn_b_in['lk1'], 'L1_attn_b_lk2': _L1_attn_b_in['lk2'], 'L1_ffn_W1': _L1_ffn_in['W1'], 'L1_ffn_W2': _L1_ffn_in['W2'], 'L1_ffn_W3': _L1_ffn_in['W3']}
    _x0 = _d['L0_attn_a_hidden_states']
    _d['L0_attn_a_hidden_states'] = jax.random.normal(jax.random.fold_in(jax.random.key(seed), 1), (8, 256, 256), dtype=_x0.dtype)
    del _x0
    return _d

def reference(L0_attn_a_hidden_states, L0_attn_a_Wq, L0_attn_a_Wk, L0_attn_a_Wv, L0_attn_a_Wo, L0_attn_b_Wq, L0_attn_b_bq, L0_attn_b_Wk, L0_attn_b_bk, L0_attn_b_Wv, L0_attn_b_bv, L0_attn_b_Wo, L0_attn_b_bo, L0_ffn_weight, L0_ffn_scale_weight, L0_ffn_bias, L1_attn_a_qkv_w, L1_attn_a_qkv_norm_w, L1_attn_a_proj_w, L1_attn_a_proj_norm_w, L1_attn_a_norm_w, L1_attn_a_s, L1_attn_b_Wq, L1_attn_b_Wk, L1_attn_b_Wv, L1_attn_b_Wo, L1_attn_b_bo, L1_attn_b_lq1, L1_attn_b_lq2, L1_attn_b_lk1, L1_attn_b_lk2, L1_ffn_W1, L1_ffn_W2, L1_ffn_W3):

    def _L0_attn_a_ref(hidden_states, Wq, Wk, Wv, Wo):
        import jax, jax.numpy as jnp
        import numpy as np
        HIDDEN = 256
        NUM_HEADS = 16
        HEAD_DIM = HIDDEN // NUM_HEADS
        SCALE = HEAD_DIM ** (-0.5)
        B, S, _ = hidden_states.shape
        q = (hidden_states @ Wq.T).reshape(B, S, NUM_HEADS, HEAD_DIM).transpose(0, 2, 1, 3)
        k = (hidden_states @ Wk.T).reshape(B, S, NUM_HEADS, HEAD_DIM).transpose(0, 2, 1, 3)
        v = (hidden_states @ Wv.T).reshape(B, S, NUM_HEADS, HEAD_DIM).transpose(0, 2, 1, 3)
        scores = jnp.einsum('bhqd,bhkd->bhqk', q, k) * SCALE
        probs = jax.nn.softmax(scores, axis=-1)
        attn = jnp.einsum('bhqk,bhkd->bhqd', probs, v)
        attn = attn.transpose(0, 2, 1, 3).reshape(B, S, HIDDEN)
        return attn @ Wo.T

    def _L0_attn_b_ref(x, Wq, bq, Wk, bk, Wv, bv, Wo, bo):
        import jax, jax.numpy as jnp
        import numpy as np
        IN_FEATURES = 256
        HEAD_NUM = 64
        D = IN_FEATURES // HEAD_NUM
        SCALE = float(np.sqrt(D))
        B, S, F = x.shape
        d = D
        h = F // d
        q = x @ Wq + bq
        k = x @ Wk + bk
        v = x @ Wv + bv

        def to_heads(t):
            return t.reshape(B, S, d, h).transpose(0, 2, 1, 3)
        q, k, v = (to_heads(q), to_heads(k), to_heads(v))
        scores = jnp.einsum('bdsh,bdth->bdst', q, k) / SCALE
        weights = jax.nn.softmax(scores, axis=-1)
        feats = jnp.einsum('bdst,bdth->bdsh', weights, v)
        feats = feats.transpose(0, 2, 1, 3).reshape(B, S, F)
        return feats @ Wo + bo

    def _L0_ffn_ref(x, weight, scale_weight, bias):
        import jax, jax.numpy as jnp
        import numpy as np
        w = weight * scale_weight[:, None]
        out = jnp.einsum('bsi,oi->bso', x, w) + bias
        return out

    def _L1_attn_a_ref(x, qkv_w, qkv_norm_w, proj_w, proj_norm_w, norm_w, s):
        import jax, jax.numpy as jnp
        import numpy as np
        DIM = 256
        HEADS = 16
        HEAD_DIM = DIM // HEADS
        CHUNK = 128
        B, N = (4, 256)

        def _rmsnorm(x, w, eps):
            return x * jax.lax.rsqrt(jnp.mean(x * x, axis=-1, keepdims=True) + eps) * w

        def _weight_quant(w):
            scale = 1.0 / jnp.clip(jnp.mean(jnp.abs(w)), 1e-05, None)
            q = jnp.clip(jnp.round(w * scale), -1.0, 1.0) / scale
            return w + jax.lax.stop_gradient(q - w)

        def _forward(x, qkv_w, qkv_norm_w, proj_w, proj_norm_w, norm_w, s):
            Bb, Nn, C = x.shape
            H, D, T = (HEADS, HEAD_DIM, CHUNK)
            nc = Nn // T
            eps = jnp.finfo(x.dtype).eps
            scale = D ** (-0.5)
            h = _rmsnorm(x, qkv_norm_w, eps)
            qkv = h @ _weight_quant(qkv_w).T
            qkv = qkv.reshape(Bb, Nn, 3, H, D)
            q, k, v = (qkv[:, :, 0], qkv[:, :, 1], qkv[:, :, 2])

            def chunks(t):
                return t.reshape(Bb, nc, T, H, D).transpose(1, 0, 3, 2, 4)
            qc, kc, vc = (chunks(q), chunks(k), chunks(v))
            tt = jnp.arange(T, dtype=x.dtype)
            lam_t = jnp.exp(-s[:, None] * tt)
            lam_rev = jnp.exp(-s[:, None] * (T - tt))
            diff = tt[:, None] - tt[None, :]
            mask = jnp.where(diff >= 0, jnp.exp(-s[:, None, None] * diff), 0.0)
            lam_T = jnp.exp(-s * T)[:, None, None]

            def step(S, qkv_c):
                qi, ki, vi = qkv_c
                scores = jnp.einsum('bhtd,bhsd,hts->bhts', qi, ki, mask)
                intra = jnp.einsum('bhts,bhsd->bhtd', scores, vi)
                cross = jnp.einsum('bhtd,ht,bhde->bhte', qi, lam_t, S)
                o = scale * (intra + cross)
                kv = jnp.einsum('bhtd,ht,bhte->bhde', ki, lam_rev, vi)
                return (lam_T * S + kv, o)
            S0 = jnp.zeros((Bb, H, D, D), x.dtype)
            _, outs = jax.lax.scan(step, S0, (qc, kc, vc))
            out = outs.transpose(1, 0, 3, 2, 4).reshape(Bb, Nn, C)
            out = _rmsnorm(out, norm_w, 1e-06)
            out = _rmsnorm(out, proj_norm_w, eps) @ _weight_quant(proj_w).T
            return out
        return _forward(x, qkv_w, qkv_norm_w, proj_w, proj_norm_w, norm_w, s)

    def _L1_attn_b_ref(x, Wq, Wk, Wv, Wo, bo, lq1, lq2, lk1, lk2):
        import jax, jax.numpy as jnp
        import numpy as np
        DIM = 256
        H = 16
        D = DIM // H // 2
        LAYER_NUM = 12
        LAM_INIT = 0.8 - 0.6 * float(np.exp(-0.3 * LAYER_NUM))
        SCALE = D ** (-0.5)
        EPS = 1e-05

        def _split_qk(y, b, n):
            y = y.reshape(b, n, H, D, 2)
            y = y.transpose(0, 1, 4, 2, 3)
            return y.reshape(b, n, 2 * H, D)
        b, n, _ = x.shape
        q = _split_qk(x @ Wq.T, b, n) * SCALE
        k = _split_qk(x @ Wk.T, b, n)
        v = (x @ Wv.T).reshape(b, n, H, 2 * D).transpose(0, 2, 1, 3)
        att = jnp.einsum('bnqd,bnkd->bnqk', q, k)
        att = jnp.nan_to_num(att)
        att = jax.nn.softmax(att.astype(jnp.float32), axis=-1)
        lam = jnp.exp(jnp.sum(lq1 * lk1)) - jnp.exp(jnp.sum(lq2 * lk2)) + LAM_INIT
        diff = att[:, :, :H, :H] - lam * att[:, :, H:, H:]
        out = jnp.einsum('bnah,bhnd->bnad', diff, v)
        out = out * jax.lax.rsqrt(jnp.mean(out * out, axis=-1, keepdims=True) + EPS)
        out = out * (1.0 - LAM_INIT)
        out = out.reshape(b, n, DIM)
        return out @ Wo.T + bo

    def _L1_ffn_ref(x, W1, W2, W3):
        import jax, jax.numpy as jnp
        import numpy as np
        B, S, D, H = (4, 256, 256, 1024)

        def fwht(x):
            orig_shape = x.shape
            n = orig_shape[-1]
            x = x.reshape(-1, n)
            h = 1
            while h < n:
                xb = x.reshape(-1, n // (2 * h), 2, h)
                a = xb[:, :, 0, :]
                b = xb[:, :, 1, :]
                x = jnp.stack([a + b, a - b], axis=2).reshape(-1, n)
                h *= 2
            scale = jnp.asarray(1.0 / np.sqrt(n), dtype=x.dtype)
            return (x * scale).reshape(orig_shape)
        up_gate = jnp.einsum('bsd,hd->bsh', x, W1)
        up_lin = jnp.einsum('bsd,hd->bsh', x, W3)
        hidden = jax.nn.silu(up_gate) * up_lin
        hidden = fwht(hidden)
        out = jnp.einsum('bsh,dh->bsd', hidden, W2)
        return out
    x = L0_attn_a_hidden_states
    x = x + _L0_attn_a_ref(_layernorm(x, axis=-1), L0_attn_a_Wq, L0_attn_a_Wk, L0_attn_a_Wv, L0_attn_a_Wo)
    x = x + _L0_ffn_ref(_layernorm(x, axis=-1), L0_ffn_weight, L0_ffn_scale_weight, L0_ffn_bias)
    x = x + _L0_attn_b_ref(_layernorm(x, axis=-1), L0_attn_b_Wq, L0_attn_b_bq, L0_attn_b_Wk, L0_attn_b_bk, L0_attn_b_Wv, L0_attn_b_bv, L0_attn_b_Wo, L0_attn_b_bo)
    x = x + _L0_ffn_ref(_layernorm(x, axis=-1), L0_ffn_weight, L0_ffn_scale_weight, L0_ffn_bias)
    x = x + _L1_attn_a_ref(_layernorm(x, axis=-1), L1_attn_a_qkv_w, L1_attn_a_qkv_norm_w, L1_attn_a_proj_w, L1_attn_a_proj_norm_w, L1_attn_a_norm_w, L1_attn_a_s)
    x = x + _L1_ffn_ref(_layernorm(x, axis=-1), L1_ffn_W1, L1_ffn_W2, L1_ffn_W3)
    x = x + _L1_attn_b_ref(_layernorm(x, axis=-1), L1_attn_b_Wq, L1_attn_b_Wk, L1_attn_b_Wv, L1_attn_b_Wo, L1_attn_b_bo, L1_attn_b_lq1, L1_attn_b_lq2, L1_attn_b_lk1, L1_attn_b_lk2)
    x = x + _L1_ffn_ref(_layernorm(x, axis=-1), L1_ffn_W1, L1_ffn_W2, L1_ffn_W3)
    return x

_drawn_inputs = setup_inputs


def setup_inputs(seed=0):
    import zlib

    import numpy as np

    out = dict(_drawn_inputs(seed))
    spreads = {'L1_attn_a_qkv_norm_w': (1.0, 0.2),
     'L1_attn_a_proj_norm_w': (1.0, 0.2),
     'L1_attn_a_norm_w': (1.0, 0.2),
     'L1_attn_a_s': (0.019999999552965164, 0.6)}
    factors = {'L0_attn_b_Wq': 8.0,
     'L0_attn_b_bq': 8.0,
     'L0_attn_b_Wk': 8.0,
     'L0_attn_b_bk': 200.0,
     'L0_attn_b_Wv': 5.269,
     'L0_attn_b_bv': 8.0,
     'L0_attn_b_Wo': 4.663,
     'L0_attn_b_bo': 14.101,
     'L1_attn_b_bo': 8.0,
     'L1_attn_b_lq1': 54.369,
     'L1_attn_b_lq2': 64.0,
     'L1_attn_b_lk1': 43.814,
     'L1_attn_b_lk2': 64.0}
    for name, (base, spread) in spreads.items():
        noise = np.random.default_rng([zlib.crc32(name.encode()), seed]).standard_normal(out[name].shape)
        drawn = base * np.exp(spread * noise) if base else spread * noise
        out[name] = jnp.asarray(drawn.astype(out[name].dtype))
    for name, factor in factors.items():
        out[name] = (out[name] * factor).astype(out[name].dtype)
    return out
```

```python
from contextlib import ExitStack

import concourse.bass as bass
from concourse import mybir

F32 = mybir.dt.float32
F32R = mybir.dt.float32r
ALU = mybir.AluOpType
ACT = mybir.ActivationFunctionType
AX = mybir.AxisListType

P = 128
B = 8
S = 256
C = 256
CT = C // P
TT = S // P
HID = 1024
HT = HID // P
LN_EPS = 1e-5
F32_EPS = 2.0 ** -23
LAM_INIT = 0.8 - 0.6 * 2.718281828459045 ** (-0.3 * 12)
ROUND_MAGIC = 1.5 * 2.0 ** 23
F32_MAX = 3.4028234663852886e38
SQRT_MAX = 1.8446742e19


HALVES, DEPTH1 = 32, 8
PRODS = DEPTH1 + 4


class Stage:

    def __init__(self, name, kind, slots=0, rows=0, groups=0, depth=0, n_max=0, n_exp=0, n_out=0, scale=1.0):
        self.name, self.kind = name, kind
        self.slots, self.rows, self.groups, self.depth = slots, rows, groups, depth
        self.n_max, self.n_exp, self.n_out, self.scale = n_max, n_exp, n_out, scale


ATTN_A0 = dict(slots=2, rows=64, groups=8, depth=16, n_max=8, n_exp=8, n_out=4, scale=0.25)
RET1 = dict(slots=2, rows=64, groups=8, depth=16, n_max=0, n_exp=8, n_out=4)
ATTN_B0 = dict(n_max=2, n_exp=2, n_out=4, scale=0.5)
STAGES = [
    Stage("attn_a0", "narrow", **ATTN_A0),
    Stage("ffn0", "ffn0"),
    Stage("attn_b0", "wide", **ATTN_B0),
    Stage("ffn0", "ffn0"),
    Stage("ret1", "narrow", **RET1),
    Stage("ffn1", "ffn1"),
    Stage("attn_b1", "tokens", scale=8.0 ** -0.5),
    Stage("ffn1", "ffn1"),
]


def increments(st):
    n = dict(stats=TT, meanvar=TT, vareps=1, rstd=1, xn=TT, xT=1, xh=1, xl=1, y=1, xres=1)
    if st.name == "ret1":
        n.update(rstd_sq=1, ms2=1, ms2e=1, r2=1, rr=1, xh=CT)
    if st.name in ("ffn0", "attn_b0", "attn_b1"):
        n.update(xbias=1)
    if st.kind == "ffn1":
        n.update(y=0, up=HT // 2, silu=HT // 2, hid=HT // 2, hh=HT // 2, hl=HT // 2, down=HT // 2, xres=TT)
    if st.kind in ("narrow", "wide"):
        n.update(qp=1, kp=1, vp=1, qh=1, ql=1, kh=1, kl=1, vev=1)
        n.update(scoresT=st.n_exp, probs=st.n_exp, pv=st.n_exp, outT=st.n_out, out_tok=st.n_out,
                 normed=st.n_out, aT=1, ah=1, al=1)
        if st.n_max:
            n.update(scores=st.n_max, rowmax=st.n_max, maxT=1, maxh=1, maxl=1, recip=st.n_out)
    if st.kind == "wide":
        n.update(qh=4, ql=4, kh=CT, kl=CT, pv=4)
    if st.kind == "narrow":
        n.update(qstore=48, kstore=48, qload=16 * st.slots, kload=16 * st.slots)
        if st.n_max:
            n.update(maxrows=32 * st.slots, maxzero=st.slots)
    if st.kind == "tokens":
        n.update(qp=1, kp=1, vp=1, qev=1, kev=1, vev=1, prod=TT * PRODS, summed=TT * PRODS, clamped=TT, smax=TT, less=TT,
                 probs=TT, psum=TT, recip=TT, lamrec=TT, part1=TT, part2=TT, normed=TT, outT=TT,
                 clip=1, sq=1, ssq=1, ssqe=1, hpow=1, inrange=1, hr=1, hn=1, aT=1, ah=1, al=1)
    if st.name == "ret1":
        n.update(n1=1, n2=1, sq1=1, sq2=1, e1=1, e2=1, rn1=1, rn2=1, nw=1)
        n.update(ah=CT)
    if st is STAGES[-1]:
        n.update(stored=16)
    return n


class Signals:

    def __init__(self, ctx, nc):
        self.per = [increments(st) for st in STAGES]
        names = list(dict.fromkeys(k for n in self.per for k in n))
        self.sem = {k: ctx.enter_context(nc.semaphore(f"s_{k}")) for k in names}
        self.base, total = [], {k: 1 for k in names}
        for n in self.per:
            self.base.append(dict(total))
            for k, v in n.items():
                total[k] += B * v
        self.total = total


def build(nc, T, out):
    ctx = ExitStack()
    with ctx:
        def sb(name, shape, dt=F32):
            return ctx.enter_context(nc.sbuf_tensor(name, shape, dt))

        def sem(name):
            return ctx.enter_context(nc.semaphore(name))

        sig = Signals(ctx, nc)

        x = sb("x", [P, B, TT * C])
        ident = sb("ident", [P, P])
        caus = sb("caus", [P, S])
        diff = sb("diff", [P, S])
        negs = sb("negs", [P, 16])
        half_pow = sb("half_pow", [P, 32])
        mask = sb("mask", [P, 16, S])
        scratch = sb("scratch", [P, 5120])
        tmpw = scratch[:, 3072:5120]
        W = {}
        for n, cols in dict(a0_q=C, a0_k=C, a0_v=C, a0_o=C, f0=C, b0_q=C, b0_k=C, b0_v=C, b0_o=C, w1=HID, w3=HID).items():
            W[n] = (sb(f"{n}_h", [P, CT, cols], F32R), sb(f"{n}_l", [P, CT, cols], F32R))
        W["w2"] = (sb("w2_h", [P, HT, C], F32R), sb("w2_l", [P, HT, C], F32R))
        for n in "qkvo":
            W[f"b1_{n}"] = W[f"a0_{n}"]
            W[f"r1_{n}"] = W[f"b0_{n}"][:1]
        had = sb("had", [P, P], F32R)
        sel = sb("sel", [P, 4, P], F32R)
        bq, bk = sb("bq", [P, CT]), sb("bk", [P, CT])
        bv, bo0, bo1, bf = sb("bv", [P, C]), sb("bo0", [P, C]), sb("bo1", [P, C]), sb("bf", [P, C])
        rowbias = {"ffn0": bf, "attn_b0": bo0, "attn_b1": bo1}
        qkvn, projn, nwb = sb("qkvn", [P, CT]), sb("projn", [P, CT]), sb("nwb", [P, C])
        lamv = sb("lamv", [P, 4, 8])
        lamt = sb("lamt", [P, 8])
        lamp = sb("lamp", [P, 2, 8])
        absum = sb("absum", [P, 4])
        qscale = sb("qscale", [P, 4])
        ones = sb("ones", [P, P])

        bst = sb("bst", [P, TT, 6])
        mv = sb("mv", [P, TT, 2])
        ve, rstd = sb("ve", [P, TT]), sb("rstd", [P, TT])
        ms2, ms2e, r2, rr = sb("ms2", [P, TT]), sb("ms2e", [P, TT]), sb("r2", [P, TT]), sb("rr", [P, TT])
        xn = sb("xn", [P, TT, C])
        xT = (sb("xT_h", [P, CT, S], F32R), sb("xT_l", [P, CT, S], F32R))
        QT = (sb("QT_h", [P, CT, S], F32R), sb("QT_l", [P, CT, S], F32R))
        KT = (sb("KT_h", [P, CT, S], F32R), sb("KT_l", [P, CT, S], F32R))
        V = sb("V", [P, TT, 16, 32])
        Vw = sb("Vw", [P, TT, 4, 65])
        Qs = sb("Qs", [P, 8 * 2 * S], F32R)
        Ks = sb("Ks", [P, 8, S], F32R)
        mx = sb("mx", [P, TT, 32])
        MT = (sb("MT_h", [P, S], F32R), sb("MT_l", [P, S], F32R))
        pr = [sb(f"pr{i}", [P, TT * 512]) for i in range(2)]
        OS = sb("OS", [P, S])
        qt, kt_, vt = (scratch[:, 2048 + n * 512:2560 + n * 512].rearrange("p (t c) -> p t c", t=TT) for n in range(3))
        prods = [pr[0][:], pr[1][:], scratch[:, 0:1024], scratch[:, 1024:2048]]
        sc1 = scratch[:, 3584:4608]
        dif, dif2 = scratch[:, 4608:4864], scratch[:, 4864:5120]
        m1, r1, lr1 = sb("m1", [P, HALVES]), sb("r1", [P, HALVES]), sb("lr1", [P, HALVES // 2])
        rec = sb("rec", [P, TT, 4])
        ON = sb("ON", [P, TT, C])
        ON2 = sb("ON2", [P, TT, C])
        sq = xn
        swb = ON2[:, 0, :]
        ssq, ssqe, hr = sb("ssq", [P, 32]), sb("ssqe", [P, 32]), sb("hr", [P, 32])
        aT = xT
        sg, hf = (q[:].rearrange("p t c -> p (t c)") for q in (ON, ON2))
        hid = [tuple(Qs[:, 512 * n:512 * n + 512].rearrange("p (a t) -> p a t", a=2) for n in (2 * k, 2 * k + 1))
               for k in range(2)]
        r2t, hr0 = sb("r2t", [P, TT]), sb("hr0", [P, 32])
        absw = tmpw.rearrange("p (j n) -> p j n", j=4)

        qd = nc.dram_tensor("q_stack", [2, 3, P, S], F32, kind="Internal").ap()
        kd = nc.dram_tensor("k_stack", [2, 3, P, S], F32, kind="Internal").ap()

        SC = [ctx.enter_context(nc.psum_tensor(f"SC{i}", [P, 1024], F32)) for i in range(2)]
        OT = [ctx.enter_context(nc.psum_tensor(f"OT{i}", [P, 512], F32)) for i in range(2)]
        pa = ctx.enter_context(nc.psum_tensor("pa", [P, 512], F32))
        pb = ctx.enter_context(nc.psum_tensor("pb", [P, 512], F32))

        x_in, const_in, ready0 = sem("x_in"), sem("const_in"), sem("ready0")
        primed = sem("primed")
        passed = sem("passed")
        raw_in = [sem(f"raw_in{n}") for n in range(3)]
        w_split, w_step = sem("w_split"), sem("w_step")
        had_ps, w2_h_done, w2_l_done = sem("had_ps"), sem("w2_h_done"), sem("w2_l_done")
        dve_setup, act_setup, abs_ps, q_scales = sem("dve_setup"), sem("act_setup"), sem("abs_ps"), sem("q_scales")
        abs_in, abs_rows, abs_sum = sem("abs_in"), sem("abs_rows"), sem("abs_sum")
        mask_exp, mask_done, stack_clear = sem("mask_exp"), sem("mask_done"), sem("stack_clear")

        LOADS = [("a0_q", CT), ("a0_k", CT), ("a0_v", CT), ("a0_o", CT), ("f0", CT),
                 ("b0_q", CT), ("b0_k", CT), ("b0_v", CT), ("b0_o", CT),
                 ("r1_q", CT), ("r1_k", CT), ("r1_v", CT), ("r1_o", CT),
                 ("w1", CT), ("w3", CT), ("w2", HT),
                 ("b1_q", CT), ("b1_k", CT), ("b1_v", CT), ("b1_o", CT)]
        ORDER = [n for n, _ in LOADS]
        NEEDS = {"attn_a0": "a0_o", "ffn0": "f0", "attn_b0": "b0_o", "ret1": "r1_o", "ffn1": "w2", "attn_b1": "b1_o"}

        def raw_part(n):
            return 2 if n in ("w1", "w3", "w2") else ORDER.index(n) % 2

        def raw_view(n):
            t = dict(LOADS)[n]
            at, size = ((0, 512), (512, 512), (1024, 2048))[raw_part(n)]
            return scratch[:, at:at + size].rearrange("p (t n) -> p t n", t=t)

        def split_done(eng, name):
            eng.wait_ge(w_split, ORDER.index(NEEDS[name]) + 1)

        def in_stage(eng, s, i):
            per, base = sig.per[s], sig.base[s]

            apart = eng.engine in (mybir.EngineType.Pool, mybir.EngineType.SP)

            def wait(name, k, alone=apart):
                eng.wait_ge(sig.sem[name], i * per[name] + (base[name] + k))
                if alone:
                    eng.sem_inc(passed, 1)

            def prev(name, alone=apart):
                if name in per:
                    eng.wait_ge(sig.sem[name], i * per[name] + base[name])
                    if alone:
                        eng.sem_inc(passed, 1)
            return wait, prev

        def stage_start(eng, s):
            if s:
                eng.wait_ge(sig.sem["xres"], sig.base[s]["xres"])

        def three(pe, out_ap, left, right, first, last):
            terms = [(a, b) for a in range(len(left)) for b in range(len(right)) if a + b < 2]
            for n, (a, b) in enumerate(terms):
                ins = pe.matmul(out_ap, left[a], right[b], start=first and n == 0, stop=last and n == len(terms) - 1)
            return ins

        def product(pe, out_ap, left, right, tiles):
            for t in range(tiles):
                ins = three(pe, out_ap, left(t), right(t), t == 0, t == tiles - 1)
            return ins

        QM = tuple(Qs[:, n * 4 * S:(n + 1) * 4 * S].rearrange("p (h t) -> p h t", h=4) for n in range(2))

        def stack_q(st):
            return Qs[:, 0:st.groups * st.slots * S].rearrange("p (g s t) -> p g s t", g=st.groups, s=st.slots)

        n_const = 16 * (5 + 4 + 7 + 4)
        block = ctx.enter_context(nc.Block())

        @block.sync
        def _(sp):
            for b in range(B):
                sp.dma_start(x[:, b, :].rearrange("p (t c) -> p t c", t=TT),
                             T["hidden"][b].rearrange("(t p) c -> p t c", p=P)).then_inc(x_in, 16)
                if b < 2:
                    n = ORDER[b]
                    sp.dma_start(raw_view(n), T[n].rearrange("(t p) n -> p t n", p=P)).then_inc(raw_in[raw_part(n)], 16)
            small = [(ident[:], T["ident"]), (caus[:], T["caus"]), (diff[:], T["diff"]), (pr[0][:, 0:P], T["had"]),
                     (pr[0][:, P:5 * P], T["sel"])]
            for dst, src in small:
                sp.dma_start(dst, src).then_inc(const_in, 16)
            for dst, n in ((bq, "b0_bq"), (bk, "b0_bk"), (qkvn, "r1_qkvn"), (projn, "r1_projn")):
                sp.dma_start(dst[:], T[n]).then_inc(const_in, 16)
            for dst, n in ((bv, "b0_bv"), (bo0, "b0_bo"), (bo1, "b1_bo"), (bf, "f0_b"), (swb, "f0_s"), (nwb, "r1_nw"), (negs, "r1_s")):
                sp.dma_start(dst if n == "f0_s" else dst[:], T[n].rearrange("(a n) -> a n", a=1).to_broadcast([P, T[n].shape[0]])).then_inc(const_in, 16)
            for j, n in enumerate(("lq1", "lk1", "lq2", "lk2")):
                sp.dma_start(lamv[:, j, :], T[n].rearrange("(a n) -> a n", a=1).to_broadcast([P, 8])).then_inc(const_in, 16)

            for j, n in enumerate(("r1_q", "r1_k", "r1_v", "r1_o")):
                sp.dma_start(absw[:, j, :].rearrange("p (t n) -> p t n", t=CT), T[n].rearrange("(t p) n -> p t n", p=P)).then_inc(abs_in, 16)
            loaded = 2

            def load_until(name):
                nonlocal loaded
                while loaded <= ORDER.index(name):
                    n = ORDER[loaded]
                    sp.wait_ge(w_split, loaded - 1)
                    if n in ("w1", "w3", "w2"):
                        sp.wait_ge(w_split, loaded)
                    sp.dma_start(raw_view(n), T[n].rearrange("(t p) n -> p t n", p=P)).then_inc(raw_in[raw_part(n)], 16)
                    loaded += 1

            sp.wait_ge(primed, 1)
            for s, st in enumerate(STAGES):
                load_until(NEEDS[st.name])
                if st.kind == "narrow":
                    stage_start(sp, s)
                    sp.wait_ge(stack_clear, 1 + sum(t.kind in ("narrow", "wide") for t in STAGES[:s]))
                    R, D, Qg = st.rows, st.depth, stack_q(st)
                    with sp.Fori(0, B) as i:
                        wait, prev = in_stage(sp, s, i)
                        for parts, dram, low, store in ((QT, qd, "ql", "qstore"), (KT, kd, "kl", "kstore")):
                            wait(low, 1)
                            prev("qload" if dram is qd else "kload")
                            for t in range(3):
                                what = (0, 0, 1)[t] if dram is qd else (0, 1, 0)[t]
                                sp.dma_start(dram[:, t, :, :].rearrange("h p t -> p h t"),
                                             parts[what][:].bitcast(F32)).then_inc(sig.sem[store], 16)
                        prev("scoresT")
                        for slot in range(st.slots):
                            r0 = R * slot + 2
                            if slot == 0:
                                wait("qstore", 48)
                            sp.dma_start(Qg[r0:r0 + 3 * D, :, slot, :].bitcast(F32), qd[slot].rearrange("t (d j) n -> (t d) j n", j=P // D)).then_inc(sig.sem["qload"], 16)
                            if slot == 0:
                                wait("kstore", 48)
                            sp.dma_start(Ks[r0:r0 + 3 * D, :, :].bitcast(F32), kd[slot].rearrange("t (d j) n -> (t d) j n", j=P // D)).then_inc(sig.sem["kload"], 16)
                        if st.n_max:
                            wait("maxl", 1)
                            wait("scores", st.n_max)
                            for slot in range(st.slots):
                                for part_ in range(2):
                                    r = R * slot + part_
                                    sp.dma_start(Qg[r:r + 1, :, slot, :].bitcast(F32),
                                                 MT[part_][8 * slot:8 * slot + 8, :].bitcast(F32)).then_inc(sig.sem["maxrows"], 16)
                if s == len(STAGES) - 1:
                    with sp.Fori(0, B) as i:
                        wait, prev = in_stage(sp, s, i)
                        wait("xres", sig.per[s]["xres"])
                        sp.dma_start(out[bass.ds(i, 1)].rearrange("a (t p) c -> p (a t) c", p=P),
                                     x[:, bass.ds(i, 1), :].rearrange("p a (t c) -> p (a t) c", t=TT)).then_inc(sig.sem["stored"], 16)
                    sp.wait_ge(sig.sem["stored"], sig.total["stored"])
            sp.wait_ge(x_in, 16 * B)
            sp.wait_ge(const_in, n_const)

        @block.gpsimd
        def _(pool):
            steps = 0

            def step(ins):
                nonlocal steps
                steps += 1
                ins.then_inc(w_step, 1)
                pool.wait_ge(w_step, steps)

            step(pool.memset(half_pow[:], -0.5))
            step(pool.memset(ones[:], 1.0))
            step(pool.memset(V[:], 0.0))
            step(pool.memset(V[:, :, :, 16:17], 1.0))
            pool.memset(Vw[:, :, :, 64:65], 1.0).then_inc(ready0, 1)
            pool.wait_ge(const_in, n_const)
            step(pool.tensor_copy(had[:], pr[0][:, 0:P]))
            step(pool.tensor_copy(sel[:].rearrange("a b c -> a (b c)"), pr[0][:, P:5 * P]))
            step(pool.tensor_scalar(negs[:], negs[:], -1.0, None, ALU.mult))

            def prepare(upto, done):
                while done <= ORDER.index(upto):
                    n = ORDER[done]
                    v = raw_view(n)
                    same = [m for m in ORDER[:done + 1] if raw_part(m) == raw_part(n)]
                    pool.wait_ge(raw_in[raw_part(n)], 16 * len(same))
                    h = W[n][0]
                    if n == "f0":
                        for t in range(CT):
                            step(pool.tensor_tensor(v[:, t, :], v[:, t, :], swb[:], ALU.mult))
                    if n.startswith("r1"):
                        a = qscale[:, 3:4] if n == "r1_o" else qscale[:, 2:3]
                        pool.wait_ge(q_scales, 2 if n == "r1_o" else 1)
                        step(pool.tensor_scalar(v, v, a, 1.0, ALU.mult, ALU.min))
                        step(pool.tensor_scalar(v, v, -1.0, ROUND_MAGIC, ALU.max, ALU.add))
                        step(pool.tensor_scalar(v, v, -ROUND_MAGIC, None, ALU.add))
                        pool.tensor_copy(h[:], v).then_inc(w_split, 1)
                        pool.wait_ge(w_split, done + 1)
                        done += 1
                        continue
                    if n == "w2":
                        src, dst = v, tmpw.rearrange("p (t n) -> p t n", t=HT)
                        for stride in (1, 2, 4):
                            sv = src.rearrange("p (a two b) n -> p a two (b n)", two=2, b=stride)
                            dv = dst.rearrange("p (a two b) n -> p a two (b n)", two=2, b=stride)
                            step(pool.tensor_tensor(dv[:, :, 0, :], sv[:, :, 0, :], sv[:, :, 1, :], ALU.add))
                            step(pool.tensor_tensor(dv[:, :, 1, :], sv[:, :, 0, :], sv[:, :, 1, :], ALU.subtract))
                            src, dst = dst, src
                        v = src
                        step(pool.tensor_scalar(v, v, float(HID) ** -0.5, None, ALU.mult))
                    step(pool.tensor_copy(h[:], v))
                    pool.tensor_tensor(W[n][1][:], v, h[:].bitcast(F32), ALU.subtract).then_inc(w_split, 1)
                    pool.wait_ge(w_split, done + 1)
                    done += 1
                return done

            pool.wait_ge(primed, 1)
            done = 0
            for s, st in enumerate(STAGES):
                done = prepare(NEEDS[st.name], done)
                if st.name == "ret1":
                    for h in range(16):
                        pool.wait_ge(mask_exp, h + 1)
                        ins = pool.tensor_tensor(mask[:, h, :], mask[:, h, :], caus[:], ALU.mult)
                    ins.then_inc(mask_done, 1)
                stage_start(pool, s)
                if st.kind == "narrow":
                    pool.memset(Qs[:, 0:st.groups * st.slots * S].bitcast(F32), 0.0).then_inc(w_step, 1)
                    pool.memset(Ks[:].bitcast(F32), 0.0).then_inc(w_step, 1)
                    steps += 2
                    pool.wait_ge(w_step, steps)
                    for slot in range(st.slots):
                        step(pool.memset(Ks[st.rows * slot:st.rows * slot + 2, :, :].bitcast(F32), 1.0))
                    pool.sem_inc(stack_clear, 1)
                if st.kind == "wide":
                    for q in (QM[0].bitcast(F32), QM[1].bitcast(F32), MT[0][:].bitcast(F32), MT[1][:].bitcast(F32)):
                        step(pool.memset(q, 0.0))
                    pool.sem_inc(stack_clear, 1)
                with pool.Fori(0, B) as i:
                    wait, prev = in_stage(pool, s, i)
                    wait("meanvar", TT)
                    pool.tensor_scalar(ve[:], mv[:, :, 1], LN_EPS, None, ALU.add).then_inc(sig.sem["vareps"], 1)
                    wait("vareps", 1)
                    pool.tensor_tensor(rstd[:], ve[:], half_pow[:, 0:TT], ALU.pow).then_inc(sig.sem["rstd"], 1)
                    if st.name == "ret1":
                        wait("ms2", 1)
                        pool.tensor_scalar(ms2e[:], ms2[:], F32_EPS, None, ALU.add).then_inc(sig.sem["ms2e"], 1)
                        wait("ms2e", 1)
                        pool.tensor_tensor(r2[:], ms2e[:], half_pow[:, 0:TT], ALU.pow).then_inc(sig.sem["r2"], 1)
                    if st.name in rowbias:
                        wait("xn", TT)
                        xv = x[:, bass.ds(i, 1), :].rearrange("p a (t c) -> p (a t) c", t=TT)
                        bb = rowbias[st.name][:].rearrange("p (a c) -> p a c", a=1).to_broadcast([P, TT, C])
                        pool.tensor_tensor(xv, xv, bb, ALU.add).then_inc(sig.sem["xbias"], 1)
                    if st.kind == "narrow" and st.n_max:
                        prev("scoresT")
                        Qg = stack_q(st)
                        for slot in range(st.slots):
                            r = st.rows * slot
                            pool.memset(Qg[r:r + 2, :, slot, :].bitcast(F32), 0.0).then_inc(sig.sem["maxzero"], 1)
                            wait("maxzero", slot + 1)
                    if st.name == "attn_b1":
                        wait("ssq", 1)
                        pool.tensor_scalar(ssqe[:], ssq[:], 1e-5, None, ALU.add).then_inc(sig.sem["ssqe"], 1)
                        wait("ssqe", 1)
                        pool.tensor_tensor(hr0[:], ssqe[:], half_pow[:], ALU.pow).then_inc(sig.sem["hpow"], 1)
                        wait("hpow", 1)
                        pool.tensor_scalar(ssqe[:], ssq[:], F32_MAX / 16, None, ALU.is_lt).then_inc(sig.sem["inrange"], 1)
                        wait("inrange", 1)
                        pool.tensor_tensor(hr[:], hr0[:], ssqe[:], ALU.mult).then_inc(sig.sem["hr"], 1)
                    if st.name == "ret1":
                        for q, e, r, eps in (("sq1", "e1", "rn1", 1e-6), ("sq2", "e2", "rn2", F32_EPS)):
                            wait(q, 1)
                            pool.tensor_scalar(ssqe[:, 0:TT], ssq[:, 0:TT], 1.0 / C, eps, ALU.mult, ALU.add).then_inc(sig.sem[e], 1)
                            wait(e, 1)
                            pool.tensor_tensor(hr[:, 0:TT], ssqe[:, 0:TT], half_pow[:, 0:TT], ALU.pow).then_inc(sig.sem[r], 1)

        def evac_out(act, st, wait, prev, o):
            rows = 65 if st.kind == "wide" else P
            wait("pv", o + 1 if st.kind == "wide" else 2 * o + 2)
            if o:
                wait("out_tok", o)
            else:
                prev("out_tok")
            act.activation(OS[0:rows, :], OT[o % 2][0:rows, 0:S], ACT.Copy).then_inc(sig.sem["outT"], 1)

        @block.scalar
        def _(act):
            for signal in sig.sem.values():
                act.sem_inc(signal, 1)
            act.sem_inc(primed, 1)
            act.wait_ge(const_in, n_const)
            act.wait_ge(dve_setup, 2)
            act.activation(lamp[:, :, 2:3], lamp[:, :, 0:1], ACT.Exp).then_inc(act_setup, 1)
            for s, st in enumerate(STAGES):
                stage_start(act, s)
                if st.name == "ret1":
                    act.wait_ge(w_step, 7)
                    for h in range(16):
                        act.activation(mask[:, h, :], diff[:], ACT.Exp, scale=negs[:, h:h + 1]).then_inc(mask_exp, 1)
                if st.kind == "ffn1" and s == 5:
                    for t in range(0, HT, 2):
                        act.wait_ge(had_ps, t // 2 + 1)
                        act.activation(W["w2"][0][:, t:t + 2, :].rearrange("p a n -> p (a n)"), OT[t // 2 % 2][:], ACT.Copy)\
                           .then_inc(w2_h_done, 1)
                if st.kind == "wide":
                    act.wait_ge(stack_clear, 2)
                with act.Fori(0, B) as i:
                    wait, prev = in_stage(act, s, i)
                    wait("xT", 1)
                    prev("up" if st.kind == "ffn1" else "y")
                    if st.name == "ret1":
                        for t in range(CT):
                            act.activation(xT[0][:, t, :], pa[:, t * S:(t + 1) * S], ACT.Copy, scale=qkvn[:, t:t + 1])\
                               .then_inc(sig.sem["xh"], 1)
                    else:
                        act.activation(xT[0][:].rearrange("p a n -> p (a n)"), pa[:], ACT.Copy).then_inc(sig.sem["xh"], 1)
                    if st.kind == "ffn1":
                        for r in range(HT // 2):
                            wait("up", r + 1)
                            if r:
                                wait("hid", r)
                            else:
                                prev("hid")
                            act.activation(sg[:], SC[r % 2][:, 0:512], ACT.Silu).then_inc(sig.sem["silu"], 1)
                            wait("hid", r + 1)
                            if r >= 2:
                                wait("down", r - 1)
                            else:
                                prev("down")
                            act.activation(hid[r % 2][0][:].rearrange("p a n -> p (a n)"), hf[:], ACT.Copy).then_inc(sig.sem["hh"], 1)
                    if st.kind == "tokens":
                        for dst, p, ps, done in ((qt, "qp", pb, "qev"), (kt_, "kp", pa, "kev"), (vt, "vp", pb, "vev")):
                            wait(p, 1)
                            prev("prod")
                            act.activation(dst.rearrange("p t c -> p (t c)"), ps[:], ACT.Copy).then_inc(sig.sem[done], 1)
                        for t in range(TT):
                            wait("less", t + 1)
                            act.activation(sc1, sc1, ACT.Exp, scale=st.scale).then_inc(sig.sem["probs"], 1)
                            if t == 0:
                                prev("clip")
                            wait("summed", (TT * DEPTH1 + 4, TT * PRODS)[t])
                            act.activation(ON[:, t, :], OT[t][:, 0:C], ACT.Copy).then_inc(sig.sem["outT"], 1)
                        wait("aT", 1)
                        act.activation(aT[0][:].rearrange("p a n -> p (a n)"), pa[:], ACT.Copy).then_inc(sig.sem["ah"], 1)
                    if st.kind in ("narrow", "wide"):
                        for parts, p, ps, h, bias, free in ((QT, "qp", pb, "qh", bq, "qstore"), (KT, "kp", pa, "kh", bk, "kstore")):
                            wait(p, 1)
                            if st.kind == "narrow":
                                prev(free)
                                flat = parts[0][:].rearrange("p a n -> p (a n)")
                                act.activation(flat, ps[:], ACT.Copy, scale=qscale[:, 0:1] if st.name == "ret1" else 1.0)\
                                   .then_inc(sig.sem[h], 1)
                            elif parts is QT:
                                prev("scoresT")
                                for n in range(4):
                                    t, r0 = n // 2, 64 * (n % 2)
                                    act.activation(QM[0][r0:r0 + 64, n, :], ps[r0:r0 + 64, t * S:(t + 1) * S], ACT.Identity,
                                                   bias=bias[r0:r0 + 64, t:t + 1]).then_inc(sig.sem[h], 1)
                            else:
                                prev("scoresT")
                                for t in range(CT):
                                    act.activation(parts[0][:, t, :], ps[:, t * S:(t + 1) * S], ACT.Identity, bias=bias[:, t:t + 1])\
                                       .then_inc(sig.sem[h], 1)
                        if st.kind == "narrow":
                            wait("vp", 1)
                            prev("pv")
                            act.activation(V[:, :, :, 0:16], pb[:].rearrange("p (t h d) -> p t h d", t=TT, h=16), ACT.Copy,
                                           scale=qscale[:, 0:1] if st.name == "ret1" else 1.0).then_inc(sig.sem["vev"], 1)
                        if st.n_max:
                            nh = 4 if st.kind == "wide" else st.groups * st.slots
                            wait("maxT", 1)
                            prev("maxrows" if st.kind == "narrow" else "scoresT")
                            act.activation(MT[0][0:nh, :], pa[0:nh, 0:S], ACT.Copy, scale=-1.0).then_inc(sig.sem["maxh"], 1)
                        per_out = max(1, st.n_exp // st.n_out)
                        for r in range(st.n_exp):
                            if st.n_max:
                                wait("scoresT", r + 1)
                                if r >= 2:
                                    wait("pv", (r - 1) * (2 if st.kind == "wide" else 1))
                                else:
                                    prev("pv")
                                act.activation(pr[r % 2][:], SC[r % 2][:], ACT.Exp, scale=st.scale).then_inc(sig.sem["probs"], 1)
                            if st.kind == "wide":
                                outs = range(2 * (r - 1), 2 * r)
                            else:
                                outs = [(r - 2) // 2] if r % 2 == 0 and r >= 2 else []
                            for o in outs:
                                if o >= 0:
                                    evac_out(act, st, wait, prev, o)
                        for o in (range(2, 4) if st.kind == "wide" else [st.n_out - 1]):
                            evac_out(act, st, wait, prev, o)
                        wait("aT", 1)
                        wait("vp", 1)
                        if st.name == "ret1":
                            for t in range(CT):
                                act.activation(aT[0][:, t, :], pa[:, t * S:(t + 1) * S], ACT.Copy, scale=projn[:, t:t + 1])\
                                   .then_inc(sig.sem["ah"], 1)
                        else:
                            act.activation(aT[0][:].rearrange("p a n -> p (a n)"), pa[:], ACT.Copy).then_inc(sig.sem["ah"], 1)

        @block.vector
        def _(dve):
            dve.wait_ge(primed, 1)
            dve.wait_ge(const_in, n_const)
            dve.tensor_tensor(sq[:, 0, 0:16].rearrange("p (a b) -> p a b", a=2), lamv[:, 0:4:2, :], lamv[:, 1:4:2, :], ALU.mult).then_inc(dve_setup, 1)
            dve.wait_ge(dve_setup, 1)
            dve.tensor_reduce(lamp[:, :, 0:1], sq[:, 0, 0:16].rearrange("p (a b) -> p a b", a=2), AX.X, ALU.add).then_inc(dve_setup, 1)
            dve.wait_ge(act_setup, 1)
            dve.tensor_tensor(lamt[:, 0:1], lamp[:, 1, 2:3], lamp[:, 0, 2:3], ALU.subtract).then_inc(dve_setup, 1)
            dve.wait_ge(dve_setup, 3)
            dve.tensor_scalar(lamt[:, 1:2], lamt[:, 0:1], -LAM_INIT, None, ALU.add).then_inc(dve_setup, 1)
            for s, st in enumerate(STAGES):
                stage_start(dve, s)
                if st.name == "attn_a0":
                    dve.wait_ge(ready0, 1)
                if st.name == "ret1":
                    dve.wait_ge(mask_done, 1)
                if st.name == "ffn1" and s == 5:
                    for t in range(0, HT, 2):
                        dve.wait_ge(w2_h_done, t // 2 + 1)
                        dve.tensor_tensor(W["w2"][1][:, t:t + 2, :].rearrange("p a n -> p (a n)"), OT[t // 2 % 2][:],
                                          W["w2"][0][:, t:t + 2, :].rearrange("p a n -> p (a n)").bitcast(F32), ALU.subtract)\
                           .then_inc(w2_l_done, 1)
                if s == 0:
                    dve.wait_ge(abs_in, 64)
                    for j, n in enumerate(("q", "k", "v", "o")):
                        dve.tensor_reduce(absum[:, j:j + 1], absw[:, j, :], AX.X, ALU.add, apply_absolute_value=True).then_inc(abs_rows, 1)
                    dve.wait_ge(abs_ps, 1)
                    dve.tensor_reduce(qscale[:, 0:1], pb[:, 0:3], AX.X, ALU.add).then_inc(abs_sum, 1)
                    dve.tensor_copy(qscale[:, 1:2], pb[:, 3:4]).then_inc(abs_sum, 1)
                    dve.wait_ge(abs_sum, 2)
                    dve.tensor_scalar(qscale[:, 0:1], qscale[:, 0:1], 1.0 / (3 * C * C), 1e-5, ALU.mult, ALU.max).then_inc(abs_sum, 1)
                    dve.tensor_scalar(qscale[:, 1:2], qscale[:, 1:2], 1.0 / (C * C), 1e-5, ALU.mult, ALU.max).then_inc(abs_sum, 1)
                    dve.wait_ge(abs_sum, 4)
                    dve.reciprocal(qscale[:, 2:4], qscale[:, 0:2]).then_inc(q_scales, 2)
                    dve.wait_ge(x_in, 16 * B)
                with dve.Fori(0, B) as i:
                    wait, prev = in_stage(dve, s, i)
                    xi = x[:, bass.ds(i, 1), :].rearrange("p a (t c) -> p (a t) c", t=TT)
                    for t in range(TT):
                        dve.bn_stats(bst[:, t, :], x[:, bass.ds(i, 1), t * C:(t + 1) * C]).then_inc(sig.sem["stats"], 1)
                    wait("stats", TT, alone=True)
                    for t in range(TT):
                        dve.bn_aggr(mv[:, t, :], bst[:, t, :]).then_inc(sig.sem["meanvar"], 1)
                    wait("rstd", 1)
                    scale_of = rstd
                    if st.name == "ret1":
                        dve.tensor_tensor(r2t[:], rstd[:], rstd[:], ALU.mult).then_inc(sig.sem["rstd_sq"], 1)
                        wait("rstd_sq", 1)
                        dve.tensor_tensor(ms2[:], r2t[:], mv[:, :, 1], ALU.mult).then_inc(sig.sem["ms2"], 1)
                        wait("r2", 1)
                        dve.tensor_tensor(rr[:], r2[:], rstd[:], ALU.mult).then_inc(sig.sem["rr"], 1)
                        wait("rr", 1)
                        scale_of = rr
                    prev("xT")
                    for t in range(TT):
                        dve.tensor_scalar(xn[:, t, :], x[:, bass.ds(i, 1), t * C:(t + 1) * C], mv[:, t, 0:1], scale_of[:, t:t + 1],
                                          ALU.subtract, ALU.mult).then_inc(sig.sem["xn"], 1)
                    wait("xh", sig.per[s]["xh"])
                    if st.name == "ret1":
                        for t in range(CT):
                            ins = dve.scalar_tensor_tensor(out=xT[1][:, t, :], in0=pa[:, t * S:(t + 1) * S], scalar=qkvn[:, t:t + 1],
                                                           in1=xT[0][:, t, :].bitcast(F32), op0=ALU.mult, op1=ALU.subtract)
                        ins.then_inc(sig.sem["xl"], 1)
                    else:
                        dve.tensor_tensor(xT[1][:].rearrange("p a n -> p (a n)"), pa[:], xT[0][:].bitcast(F32).rearrange("p a n -> p (a n)"),
                                          ALU.subtract).then_inc(sig.sem["xl"], 1)
                    if st.kind == "ffn1":
                        for r in range(HT // 2):
                            wait("silu", r + 1)
                            if r:
                                wait("hl", r)
                            else:
                                prev("hl")
                            dve.tensor_tensor(hf[:], SC[r % 2][:, 512:1024], sg[:], ALU.mult).then_inc(sig.sem["hid"], 1)
                            wait("hh", r + 1)
                            dve.tensor_tensor(hid[r % 2][1][:].rearrange("p a n -> p (a n)"), hf[:],
                                              hid[r % 2][0][:].bitcast(F32).rearrange("p a n -> p (a n)"), ALU.subtract).then_inc(sig.sem["hl"], 1)
                    if st.kind in ("narrow", "wide"):
                        for parts, ps, h, l, bias in ((QT, pb, "qh", "ql", bq), (KT, pa, "kh", "kl", bk)):
                            wait(h, sig.per[s][h])
                            if st.kind == "wide" and parts is QT:
                                for n in range(4):
                                    t, r0 = n // 2, 64 * (n % 2)
                                    dve.scalar_tensor_tensor(out=QM[1][r0:r0 + 64, n, :], in0=ps[r0:r0 + 64, t * S:(t + 1) * S],
                                                             scalar=bias[r0:r0 + 64, t:t + 1], in1=QM[0][r0:r0 + 64, n, :].bitcast(F32),
                                                             op0=ALU.add, op1=ALU.subtract).then_inc(sig.sem[l], 1)
                            elif st.kind == "wide":
                                for t in range(CT):
                                    dve.scalar_tensor_tensor(out=parts[1][:, t, :], in0=ps[:, t * S:(t + 1) * S], scalar=bias[:, t:t + 1],
                                                             in1=parts[0][:, t, :].bitcast(F32), op0=ALU.add, op1=ALU.subtract)\
                                       .then_inc(sig.sem[l], 1)
                            else:
                                flat = [q[:].rearrange("p a n -> p (a n)") for q in parts]
                                a = qscale[:, 0:1] if st.name == "ret1" else 1.0
                                dve.scalar_tensor_tensor(out=flat[1], in0=ps[:], scalar=a, in1=flat[0].bitcast(F32),
                                                         op0=ALU.mult, op1=ALU.subtract).then_inc(sig.sem[l], 1)
                        if st.kind == "wide":
                            wait("vp", 1)
                            prev("pv")
                            for t in range(TT):
                                ins = dve.tensor_tensor(Vw[:, t, :, 0:64], pb[:, t * C:(t + 1) * C].rearrange("p (h d) -> p h d", h=4),
                                                        bv[:].rearrange("p (h d) -> p h d", h=4), ALU.add)
                            ins.then_inc(sig.sem["vev"], 1)
                        nr = st.n_max // 2
                        if st.n_max:
                            prev("maxT")
                        for r in range(st.n_max):
                            wait("scores", r + 1)
                            t, k = divmod(r, nr)
                            dve.tensor_reduce(mx[:, t, 4 * k:4 * k + 4], SC[r % 2][:].rearrange("p (h k) -> p h k", h=4), AX.X, ALU.max)\
                               .then_inc(sig.sem["rowmax"], 1)
                        if st.n_max:
                            nh = 4 * nr
                            wait("maxh", 1)
                            dve.scalar_tensor_tensor(out=MT[1][0:nh, :], in0=pa[0:nh, 0:S], scalar=-1.0, in1=MT[0][0:nh, :].bitcast(F32),
                                                     op0=ALU.mult, op1=ALU.subtract).then_inc(sig.sem["maxl"], 1)
                        def masked(r):
                            wait("scoresT", r + 1)
                            if r >= 2:
                                wait("pv", r - 1)
                            else:
                                prev("pv")
                            heads = mask[:, r:16:8, :]
                            pv_, sv = (q[:].rearrange("p (k h t) -> p k h t", k=2, h=2) for q in (pr[r % 2], SC[r % 2]))
                            dve.tensor_tensor(pv_[:, 0], sv[:, 0], heads, ALU.mult)
                            dve.tensor_tensor(pv_[:, 1, :, P:S], sv[:, 1, :, P:S], heads[:, :, 0:P], ALU.mult).then_inc(sig.sem["probs"], 1)
                        for o in range(st.n_out):
                            if not st.n_max:
                                if o == 0:
                                    masked(0)
                                    masked(1)
                                if o < st.n_out - 1:
                                    masked(2 * o + 2)
                                    masked(2 * o + 3)
                            wait("out_tok", o + 1)
                            ps = (pb, pa)[o % 2]
                            if o == 0:
                                prev("aT")
                            elif st.n_max:
                                wait("normed", o)
                            if st.kind == "wide":
                                pv_ = ps[:, 0:TT * 65].rearrange("p (t c) -> p t c", t=TT)
                                dve.reciprocal(rec[:, :, 0:1], pv_[:, :, 64:65]).then_inc(sig.sem["recip"], 1)
                                wait("recip", o + 1)
                                for t in range(TT):
                                    ins = dve.tensor_scalar(ON[:, t, 64 * o:64 * o + 64], pv_[:, t, 0:64], rec[:, t, 0:1], None, ALU.mult)
                                ins.then_inc(sig.sem["normed"], 1)
                                continue
                            pv_ = ps[:, 0:TT * P].rearrange("p (t h d) -> p t h d", t=TT, h=4)
                            if st.name == "ret1":
                                for t in range(TT):
                                    ins = dve.tensor_scalar(ON[:, t, 64 * o:64 * o + 64].rearrange("p (h d) -> p h d", h=4),
                                                            pv_[:, t, :, 0:16], 0.25, None, ALU.mult)
                                ins.then_inc(sig.sem["normed"], 1)
                                continue
                            dve.reciprocal(rec[:], pv_[:, :, :, 16]).then_inc(sig.sem["recip"], 1)
                            wait("recip", o + 1)
                            for t in range(TT):
                                ins = dve.tensor_tensor(ON[:, t, 64 * o:64 * o + 64].rearrange("p (h d) -> p h d", h=4), pv_[:, t, :, 0:16],
                                                        rec[:, t, :].rearrange("p (h d) -> p h d", d=1).to_broadcast([P, 4, 16]), ALU.mult)
                            ins.then_inc(sig.sem["normed"], 1)
                        if st.name == "ret1":
                            wait("normed", st.n_out)
                            for src, dst, q, r, n in ((ON, ON2, "sq1", "rn1", "n1"), (ON2, ON, "sq2", "rn2", "n2")):
                                for t in range(TT):
                                    ins = dve.tensor_tensor_reduce(out=sq[:, t, :], in0=src[:, t, :], in1=src[:, t, :], scale=1.0, scalar=0.0,
                                                                   op0=ALU.mult, op1=ALU.add, accum_out=ssq[:, t:t + 1])
                                ins.then_inc(sig.sem[q], 1)
                                wait(r, 1)
                                for t in range(TT):
                                    if q == "sq1":
                                        ins = dve.scalar_tensor_tensor(out=dst[:, t, :], in0=src[:, t, :], scalar=hr[:, t:t + 1], in1=nwb[:],
                                                                       op0=ALU.mult, op1=ALU.mult)
                                    else:
                                        ins = dve.tensor_scalar(dst[:, t, :], src[:, t, :], hr[:, t:t + 1], None, ALU.mult)
                                ins.then_inc(sig.sem[n], 1)
                                wait(n, 1)
                    if st.kind == "tokens":
                        wait("kev", 1)

                        def products(t, n0, pieces):
                            for u, (dst_of, in0, in1) in enumerate(pieces):
                                n = n0 + u
                                if n >= 4:
                                    wait("summed", n - 3)
                                dve.tensor_tensor(dst_of(prods[n % 4]), in0, in1, ALU.mult).then_inc(sig.sem["prod"], 1)

                        for t in range(TT):
                            qv, kv = (q[:, t, :].rearrange("p (d q) -> p d q", d=DEPTH1) for q in (qt, kt_))
                            products(t, DEPTH1 * t, [
                                (lambda b: b.rearrange("p (q k) -> p q k", q=HALVES),
                                 qv[:, d, :].rearrange("p (q a) -> p q a", a=1).to_broadcast([P, HALVES, HALVES]),
                                 kv[:, d, :].rearrange("p (a k) -> p a k", a=1).to_broadcast([P, HALVES, HALVES])) for d in range(DEPTH1)])
                        wait("vev", 1)
                        s3 = sc1.rearrange("p (q k) -> p q k", q=HALVES)
                        HD = HALVES // 2
                        d3, e3 = (q.rearrange("p (a h) -> p a h", a=HD) for q in (dif, dif2))
                        for t in range(TT):
                            wait("summed", DEPTH1 * (t + 1))
                            if t:
                                wait("part2", t)
                            dve.tensor_scalar(sc1, SC[t][:], F32_MAX, -F32_MAX, ALU.min, ALU.max).then_inc(sig.sem["clamped"], 1)
                            wait("clamped", t + 1)
                            dve.tensor_reduce(m1[:], s3, AX.X, ALU.max).then_inc(sig.sem["smax"], 1)
                            wait("smax", t + 1)
                            dve.tensor_tensor(s3, s3, m1[:].rearrange("p (q a) -> p q a", a=1).to_broadcast([P, HALVES, HALVES]),
                                              ALU.subtract).then_inc(sig.sem["less"], 1)
                            wait("probs", t + 1)
                            dve.tensor_reduce(r1[:], s3, AX.X, ALU.add).then_inc(sig.sem["psum"], 1)
                            wait("psum", t + 1)
                            dve.reciprocal(m1[:], r1[:]).then_inc(sig.sem["recip"], 1)
                            wait("recip", t + 1)
                            dve.tensor_scalar(lr1[:], m1[:, HD:HALVES], lamt[:, 1:2], None, ALU.mult).then_inc(sig.sem["lamrec"], 1)
                            wait("lamrec", t + 1)
                            if t:
                                wait("prod", TT * DEPTH1 + 4 * t)
                            dve.tensor_tensor(d3, s3[:, 0:HD, 0:HD], m1[:, 0:HD].rearrange("p (q a) -> p q a", a=1).to_broadcast([P, HD, HD]),
                                              ALU.mult).then_inc(sig.sem["part1"], 1)
                            dve.tensor_tensor(e3, s3[:, HD:HALVES, HD:HALVES], lr1[:].rearrange("p (q a) -> p q a", a=1).to_broadcast([P, HD, HD]),
                                              ALU.mult).then_inc(sig.sem["part2"], 1)
                            wait("part2", t + 1)
                            dve.tensor_tensor(dif, dif, dif2, ALU.add).then_inc(sig.sem["normed"], 1)
                            wait("normed", t + 1)
                            vv = vt[:, t, :].rearrange("p (h d) -> p h d", h=16)
                            products(t, TT * DEPTH1 + 4 * t, [
                                (lambda b: b.rearrange("p (h a d) -> p h a d", h=4, a=HD),
                                 d3[:, :, 4 * u:4 * u + 4].rearrange("p a (h o) -> p h a o", o=1).to_broadcast([P, 4, HD, 16]),
                                 vv[:, 4 * u:4 * u + 4, :].rearrange("p h (o d) -> p h o d", o=1).to_broadcast([P, 4, HD, 16])) for u in range(4)])
                        flat = ON[:].rearrange("p t c -> p (t c)")
                        wait("outT", TT)
                        clipped = ON2[:].rearrange("p t c -> p (t c)")
                        dve.tensor_scalar(clipped, flat, SQRT_MAX, -SQRT_MAX, ALU.min, ALU.max).then_inc(sig.sem["clip"], 1)
                        wait("clip", 1)
                        dve.scalar_tensor_tensor(out=sq[:].rearrange("p t c -> p (t c)"), in0=clipped, scalar=1.0 / 16, in1=clipped,
                                                 op0=ALU.mult, op1=ALU.mult).then_inc(sig.sem["sq"], 1)
                        wait("sq", 1)
                        dve.tensor_reduce(ssq[:], sq[:].rearrange("p t (h d) -> p (t h) d", d=16), AX.X, ALU.add).then_inc(sig.sem["ssq"], 1)
                        wait("hr", 1)
                        dve.scalar_tensor_tensor(out=ON2[:].rearrange("p t (h d) -> p (t h) d", d=16), in0=ON[:].rearrange("p t (h d) -> p (t h) d", d=16),
                                                 scalar=1.0 - LAM_INIT, in1=hr[:].rearrange("p (h d) -> p h d", d=1).to_broadcast([P, 32, 16]),
                                                 op0=ALU.mult, op1=ALU.mult).then_inc(sig.sem["hn"], 1)
                    if st.kind in ("narrow", "wide", "tokens"):
                        wait("ah", sig.per[s]["ah"])
                        if st.name == "ret1":
                            for t in range(CT):
                                ins = dve.scalar_tensor_tensor(out=aT[1][:, t, :], in0=pa[:, t * S:(t + 1) * S], scalar=projn[:, t:t + 1],
                                                               in1=aT[0][:, t, :].bitcast(F32), op0=ALU.mult, op1=ALU.subtract)
                            ins.then_inc(sig.sem["al"], 1)
                        else:
                            dve.tensor_tensor(aT[1][:].rearrange("p a n -> p (a n)"), pa[:], aT[0][:].bitcast(F32).rearrange("p a n -> p (a n)"),
                                              ALU.subtract).then_inc(sig.sem["al"], 1)
                    if st.kind == "ffn1":
                        wait("down", HT // 2)
                    else:
                        wait("y", 1)
                    if st.name in rowbias:
                        wait("xbias", 1)
                    if st.kind == "ffn1":
                        for t, ps in enumerate((pa, pb)):
                            xt = x[:, bass.ds(i, 1), t * C:(t + 1) * C]
                            dve.tensor_tensor(xt, xt, ps[:, 0:C].rearrange("p (a c) -> p a c", a=1), ALU.add).then_inc(sig.sem["xres"], 1)
                    elif st.name == "ret1":
                        xt = x[:, bass.ds(i, 1), :]
                        dve.scalar_tensor_tensor(out=xt, in0=pb[:].rearrange("p (a c) -> p a c", a=1), scalar=qscale[:, 1:2], in1=xt,
                                                 op0=ALU.mult, op1=ALU.add).then_inc(sig.sem["xres"], 1)
                    else:
                        xt = x[:, bass.ds(i, 1), :]
                        dve.tensor_tensor(xt, xt, pb[:].rearrange("p (a c) -> p a c", a=1), ALU.add).then_inc(sig.sem["xres"], 1)

        @block.tensor
        def _(pe):
            pe.wait_ge(abs_rows, 4)
            pe.wait_ge(ready0, 1)
            pe.matmul(pb[:, 0:4], ones[:], absum[:], start=True, stop=True).then_inc(abs_ps, 1)
            pe.wait_ge(q_scales, 2)
            pe.wait_ge(primed, 1)
            for s, st in enumerate(STAGES):
                stage_start(pe, s)
                split_done(pe, st.name)
                if st.name == "ffn1" and s == 5:
                    for t in range(0, HT, 2):
                        if t >= 4:
                            pe.wait_ge(w2_l_done, t // 2 - 1)
                        for u in range(2):
                            for n, q in enumerate(W["w2"]):
                                ins = pe.matmul(OT[t // 2 % 2][:, u * C:(u + 1) * C], had[:], q[:, t + u, :], start=n == 0, stop=n == 1)
                        ins.then_inc(had_ps, 1)
                    pe.wait_ge(w2_l_done, HT // 2)
                if st.name == "attn_a0":
                    pe.wait_ge(const_in, n_const)
                with pe.Fori(0, B) as i:
                    wait, prev = in_stage(pe, s, i)

                    def turn(src, ps, signal):
                        for c in range(CT):
                            for t in range(TT):
                                ins = pe.transpose(ps[:, c * S + t * P:c * S + t * P + P], src[:, t, c * P:c * P + P], ident[:])
                        ins.then_inc(sig.sem[signal], 1)

                    def channels_out(ps, w, signal):
                        for o in range(CT):
                            ins = product(pe, ps[:, o * S:(o + 1) * S], lambda t: [q[:, t, o * P:(o + 1) * P] for q in w],
                                          lambda t: [q[:, t, :] for q in xT], CT)
                        ins.then_inc(sig.sem[signal], 1)

                    def tokens_out(ps, act_, w, signal):
                        for o in range(TT):
                            ins = product(pe, ps[:, o * C:(o + 1) * C], lambda t: [q[:, t, o * P:(o + 1) * P] for q in act_],
                                          lambda t: [q[:, t, :] for q in w], CT)
                        ins.then_inc(sig.sem[signal], 1)

                    wait("xn", TT)
                    prev("xres")
                    turn(xn, pa, "xT")
                    wait("xl", 1)
                    if st.kind == "ffn0":
                        tokens_out(pb, xT, W["f0"], "y")
                    if st.kind == "ffn1":
                        def up(r):
                            if r >= 2:
                                wait("hid", r - 1)
                            for u in range(2):
                                o = 2 * r + u
                                for w, at in ((W["w1"], 0), (W["w3"], 512)):
                                    ins = product(pe, SC[r % 2][:, at + u * S:at + (u + 1) * S],
                                                  lambda t: [q[:, t, o * P:(o + 1) * P] for q in w], lambda t: [q[:, t, :] for q in xT], CT)
                            ins.then_inc(sig.sem["up"], 1)

                        def down(r):
                            wait("hl", r + 1)
                            for u in range(2):
                                for t, ps in enumerate((pa, pb)):
                                    ins = three(pe, ps[:, 0:C], [q[:, u, t * P:(t + 1) * P] for q in hid[r % 2]],
                                                [q[:, 2 * r + u, :] for q in W["w2"]], r == 0 and u == 0, r == HT // 2 - 1 and u == 1)
                            return ins.then_inc(sig.sem["down"], 1)

                        up(0)
                        for r in range(1, HT // 2):
                            up(r)
                            down(r - 1)
                        down(HT // 2 - 1)
                    if st.kind == "tokens":
                        tokens_out(pb, xT, W["b1_q"], "qp")
                        tokens_out(pa, xT, W["b1_k"], "kp")
                        wait("qev", 1)
                        tokens_out(pb, xT, W["b1_v"], "vp")

                        def sums(n, dst, width, first, last):
                            wait("prod", n + 1)
                            for c in range(0, 1024, width):
                                ins = pe.matmul(dst(c), ident[:], prods[n % 4][:, c:c + width],
                                                start=first and (c == 0 or width == 512), stop=last and (c == 1024 - width or width == 512))
                            ins.then_inc(sig.sem["summed"], 1)

                        for t in range(TT):
                            for d in range(DEPTH1):
                                sums(DEPTH1 * t + d, lambda c: SC[t][:, c:c + 512], 512, d == 0, d == DEPTH1 - 1)
                        for t in range(TT):
                            for u in range(4):
                                sums(TT * DEPTH1 + 4 * t + u, lambda c: OT[t][:, 0:C], C, u == 0, u == 3)
                        wait("hn", 1)
                        wait("kev", 1)
                        turn(ON2, pa, "aT")
                        wait("al", 1)
                        wait("vev", 1)
                        tokens_out(pb, aT, W["b1_o"], "y")
                    if st.kind in ("narrow", "wide"):
                        pre = {"attn_a0": "a0", "attn_b0": "b0", "ret1": "r1"}[st.name]
                        wq, wk, wv, wo = (W[f"{pre}_{n}"] for n in "qkvo")
                        channels_out(pb, wq, "qp")
                        channels_out(pa, wk, "kp")
                        wait("ql", sig.per[s]["ql"])
                        tokens_out(pb, xT, wv, "vp")
                        if st.kind == "narrow":
                            Qg = stack_q(st)
                            wait("qload", 16 * st.slots)
                            wait("kload", 16 * st.slots)
                            if st.n_max:
                                wait("maxzero", st.slots)
                        else:
                            wait("kl", CT)
                        nr = st.n_max // 2
                        for r in range(st.n_max):
                            if r >= 2:
                                wait("rowmax", r - 1)
                            t, k = divmod(r, nr)
                            for u in range(4):
                                n = 4 * k + u
                                dst = SC[r % 2][:, u * S:(u + 1) * S]
                                if st.kind == "narrow":
                                    ins = pe.matmul(dst, Qg[:, n % 8, n // 8, t * P:(t + 1) * P], Ks[:, n % 8, :], start=True, stop=True)
                                else:
                                    ins = three(pe, dst, [q[:, n, t * P:(t + 1) * P] for q in QM], [q[:, n // 2, :] for q in KT], True, True)
                            ins.then_inc(sig.sem["scores"], 1)
                        wait("kl", sig.per[s]["kl"])
                        if st.n_max:
                            nh = 4 * nr
                            wait("rowmax", st.n_max)
                            for t in range(TT):
                                ins = pe.transpose(pa[0:nh, t * P:(t + 1) * P], mx[:, t, 0:nh], ident[:])
                            ins.then_inc(sig.sem["maxT"], 1)
                            if st.kind == "narrow":
                                wait("maxrows", 32 * st.slots)
                            else:
                                wait("maxl", 1)
                        wait("vev", 1)

                        def scores_t(r):
                            if r >= 2:
                                wait("probs", r - 1)
                            for kt in range(TT):
                                dst = SC[r % 2][:, kt * 512:(kt + 1) * 512]
                                if st.kind == "narrow":
                                    ins = pe.matmul(dst.rearrange("p (s t) -> p s t", s=2), Ks[:, r, kt * P:(kt + 1) * P],
                                                    Qg[:, r, :, :], start=True, stop=True)
                                else:
                                    for u in range(2):
                                        n, d = 2 * r + u, dst[:, u * S:(u + 1) * S]
                                        three(pe, d, [q[:, r, kt * P:(kt + 1) * P] for q in KT], [q[:, n, :] for q in QM], True, False)
                                        pe.matmul(d, sel[:, n, :], MT[0][:], start=False, stop=False)
                                        ins = pe.matmul(d, sel[:, n, :], MT[1][:], start=False, stop=True)
                            ins.then_inc(sig.sem["scoresT"], 1)

                        def attend(r):
                            wait("probs", r + 1)
                            p = pr[r % 2][:].rearrange("p (k h t) -> p k h t", k=TT, h=2)
                            if st.kind == "wide":
                                for u in range(2):
                                    o = 2 * r + u
                                    if o >= 2:
                                        wait("outT", o - 1)
                                    for kt in range(TT):
                                        ins = pe.matmul(OT[o % 2][0:65, 0:S], Vw[:, kt, o, :], p[:, kt, u, :], start=kt == 0, stop=kt == 1)
                                    ins.then_inc(sig.sem["pv"], 1)
                                return
                            o = r // 2
                            if r % 2 == 0 and o >= 2:
                                wait("outT", o - 1)
                            for kt in range(TT):
                                for u in range(2):
                                    c = 32 * (2 * (r % 2) + u)
                                    head = 2 * r + u
                                    t0 = P * kt if st.name == "ret1" else 0
                                    ins = pe.matmul(OT[o % 2][c:c + 32, t0:S], V[:, kt, head, :], p[:, kt, u, t0:S],
                                                    start=kt == 0, stop=kt == 1, tile_position=(0, c), skip_group_check=True)
                            ins.then_inc(sig.sem["pv"], 1)

                        def to_tokens(o):
                            wait("outT", o + 1)
                            if o >= 2:
                                wait("normed", o - 1)
                            rows = 65 if st.kind == "wide" else P
                            for t in range(TT):
                                ins = pe.transpose((pb, pa)[o % 2][:, t * rows:(t + 1) * rows], OS[0:rows, t * P:(t + 1) * P], ident[0:rows, 0:rows])
                            ins.then_inc(sig.sem["out_tok"], 1)

                        scores_t(0)
                        scores_t(1)
                        for r in range(st.n_exp):
                            attend(r)
                            if r + 2 < st.n_exp:
                                scores_t(r + 2)
                            if st.kind == "narrow" and r % 2 == 0 and r >= 2:
                                to_tokens((r - 2) // 2)
                            if st.kind == "wide" and r == 0:
                                to_tokens(0)
                                to_tokens(1)
                        for o in (range(2, 4) if st.kind == "wide" else [st.n_out - 1]):
                            to_tokens(o)
                        src, key = {"ret1": (ON, "n2")}.get(st.name, (ON, "normed"))
                        wait(key, sig.per[s][key])
                        turn(src, pa, "aT")
                        wait("al", 1)
                        tokens_out(pb, aT, wo, "y")


_WEIGHTS = {
    "a0_q": "L0_attn_a_Wq", "a0_k": "L0_attn_a_Wk", "a0_v": "L0_attn_a_Wv", "a0_o": "L0_attn_a_Wo",
    "f0": "L0_ffn_weight", "f0_s": "L0_ffn_scale_weight", "f0_b": "L0_ffn_bias",
    "b0_q": "L0_attn_b_Wq", "b0_bq": "L0_attn_b_bq", "b0_k": "L0_attn_b_Wk", "b0_bk": "L0_attn_b_bk",
    "b0_v": "L0_attn_b_Wv", "b0_bv": "L0_attn_b_bv", "b0_o": "L0_attn_b_Wo", "b0_bo": "L0_attn_b_bo",
    "r1_qkvn": "L1_attn_a_qkv_norm_w", "r1_projn": "L1_attn_a_proj_norm_w", "r1_nw": "L1_attn_a_norm_w", "r1_s": "L1_attn_a_s",
    "b1_q": "L1_attn_b_Wq", "b1_k": "L1_attn_b_Wk", "b1_v": "L1_attn_b_Wv", "b1_o": "L1_attn_b_Wo", "b1_bo": "L1_attn_b_bo",
    "lq1": "L1_attn_b_lq1", "lq2": "L1_attn_b_lq2", "lk1": "L1_attn_b_lk1", "lk2": "L1_attn_b_lk2",
    "w1": "L1_ffn_W1", "w2": "L1_ffn_W2", "w3": "L1_ffn_W3",
}

_OUT = (8, 256, 256)


def _layouts(inputs):
    import numpy as np

    a = {k: np.asarray(inputs[v]) for k, v in _WEIGHTS.items()}
    half, d, j = np.meshgrid(np.arange(2), np.arange(16), np.arange(8), indexing="ij")
    qk16 = ((half * 8 + j) * 16 + d).ravel()
    d, half, j = np.meshgrid(np.arange(8), np.arange(2), np.arange(16), indexing="ij")
    qk8 = (j * 16 + 2 * d + half).ravel()
    g, half, d = np.meshgrid(np.arange(8), np.arange(2), np.arange(16), indexing="ij")
    v16 = ((half * 8 + g) * 16 + d).ravel()
    qkv = np.asarray(inputs["L1_attn_a_qkv_w"])
    proj = np.asarray(inputs["L1_attn_a_proj_w"])
    a["a0_q"], a["a0_k"] = a["a0_q"].T[:, qk16], a["a0_k"].T[:, qk16]
    a["a0_v"], a["a0_o"] = a["a0_v"].T[:, v16], a["a0_o"].T[v16]
    a["r1_q"], a["r1_k"], a["r1_v"] = qkv[:256].T[:, qk16], qkv[256:512].T[:, qk16], qkv[512:].T[:, v16]
    a["r1_o"] = proj.T[v16]
    a["r1_nw"], a["r1_projn"] = a["r1_nw"][v16], a["r1_projn"][v16]
    a["b1_q"], a["b1_k"] = a["b1_q"].T[:, qk8], a["b1_k"].T[:, qk8]
    for n in ("b1_v", "b1_o", "f0", "w1", "w2", "w3"):
        a[n] = a[n].T
    for n in ("b0_bq", "b0_bk", "r1_qkvn", "r1_projn"):
        a[n] = a[n].reshape(2, 128).T
    a["hidden"] = np.asarray(inputs["L0_attn_a_hidden_states"])
    a["ident"] = np.eye(128, dtype=np.float32)
    h = np.ones((1, 1), np.float32)
    while h.shape[0] < 128:
        h = np.block([[h, h], [h, -h]])
    a["had"] = h.astype(np.float32)
    t, k = np.arange(256)[None, :], np.arange(128)[:, None]
    a["caus"] = (t >= k).astype(np.float32)
    a["diff"] = np.maximum(t - k, 0).astype(np.float32)
    a["sel"] = np.repeat(np.eye(128, 4, dtype=np.float32), 128, axis=1)
    return {k: np.ascontiguousarray(v) for k, v in a.items()}


def kernel(**inputs):
    import numpy as _np
    import concourse.bacc as _bacc
    from concourse.bass_utils import run_bass_kernel_spmd as _run

    nc = _bacc.Bacc("TRN2", target_bir_lowering=False, num_devices=1)
    arrays, T = {}, {}
    for name, a in _layouts(inputs).items():
        arrays[f"in_{name}"] = a
        T[name] = nc.dram_tensor(f"in_{name}", a.shape, mybir.dt.from_np(a.dtype), kind="ExternalInput").ap()
    out = nc.dram_tensor("out_0_dram", _OUT, F32, kind="ExternalOutput").ap()
    build(nc, T, out)
    r = _run(nc, [arrays], core_ids=[0])
    return r.results[0]["out_0_dram"]
```

```python
from contextlib import ExitStack

import concourse.bass as bass
from concourse import mybir

F32 = mybir.dt.float32
F32R = mybir.dt.float32r
ALU = mybir.AluOpType
ACT = mybir.ActivationFunctionType
AX = mybir.AxisListType

P = 128
B = 8
S = 256
C = 256
CT = C // P
TT = S // P
HID = 1024
HT = HID // P
LN_EPS = 1e-5
F32_EPS = 2.0 ** -23
LAM_INIT = 0.8 - 0.6 * 2.718281828459045 ** (-0.3 * 12)
ROUND_MAGIC = 1.5 * 2.0 ** 23
F32_MAX = 3.4028234663852886e38
SQRT_MAX = 1.8446742e19


HALVES, DEPTH1 = 32, 8
PRODS = DEPTH1 + 4


class Stage:

    def __init__(self, name, kind, slots=0, rows=0, groups=0, depth=0, n_max=0, n_exp=0, n_out=0, scale=1.0):
        self.name, self.kind = name, kind
        self.slots, self.rows, self.groups, self.depth = slots, rows, groups, depth
        self.n_max, self.n_exp, self.n_out, self.scale = n_max, n_exp, n_out, scale


ATTN_A0 = dict(slots=2, rows=64, groups=8, depth=16, n_max=8, n_exp=8, n_out=4, scale=0.25)
RET1 = dict(slots=2, rows=64, groups=8, depth=16, n_max=0, n_exp=8, n_out=4)
ATTN_B0 = dict(n_max=2, n_exp=2, n_out=4, scale=0.5)
STAGES = [
    Stage("attn_a0", "narrow", **ATTN_A0),
    Stage("ffn0", "ffn0"),
    Stage("attn_b0", "wide", **ATTN_B0),
    Stage("ffn0", "ffn0"),
    Stage("ret1", "narrow", **RET1),
    Stage("ffn1", "ffn1"),
    Stage("attn_b1", "tokens", scale=8.0 ** -0.5),
    Stage("ffn1", "ffn1"),
]


def increments(st):
    n = dict(stats=TT, meanvar=TT, vareps=1, rstd=1, xn=TT, xT=1, xh=1, xl=1, y=1, xres=1)
    if st.name == "ret1":
        n.update(rstd_sq=1, ms2=1, ms2e=1, r2=1, rr=1, xh=CT)
    if st.name in ("ffn0", "attn_b0", "attn_b1"):
        n.update(xbias=1)
    if st.kind == "ffn1":
        n.update(y=0, up=HT // 2, silu=HT // 2, hid=HT // 2, hh=HT // 2, hl=HT // 2, down=HT // 2, xres=TT)
    if st.kind in ("narrow", "wide"):
        n.update(qp=1, kp=1, vp=1, qh=1, ql=1, kh=1, kl=1, vev=1)
        n.update(scoresT=st.n_exp, probs=st.n_exp, pv=st.n_exp, outT=st.n_out, out_tok=st.n_out,
                 normed=st.n_out, aT=1, ah=1, al=1)
        if st.n_max:
            n.update(scores=st.n_max, rowmax=st.n_max, maxT=1, maxh=1, maxl=1, recip=st.n_out)
    if st.kind == "wide":
        n.update(qh=4, ql=4, kh=CT, kl=CT, pv=4)
    if st.kind == "narrow":
        n.update(qstore=48, kstore=48, qload=16 * st.slots, kload=16 * st.slots)
        if st.n_max:
            n.update(maxrows=32 * st.slots, maxzero=st.slots)
    if st.kind == "tokens":
        n.update(qp=1, kp=1, vp=1, qev=1, kev=1, vev=1, prod=TT * PRODS, summed=TT * PRODS, clamped=TT, smax=TT, less=TT,
                 probs=TT, psum=TT, recip=TT, lamrec=TT, part1=TT, part2=TT, normed=TT, outT=TT,
                 clip=1, sq=1, ssq=1, ssqe=1, hpow=1, inrange=1, hr=1, hn=1, aT=1, ah=1, al=1)
    if st.name == "ret1":
        n.update(n1=1, n2=1, sq1=1, sq2=1, e1=1, e2=1, rn1=1, rn2=1, nw=1)
        n.update(ah=CT)
    if st is STAGES[-1]:
        n.update(stored=16)
    return n


class Signals:

    def __init__(self, ctx, nc):
        self.per = [increments(st) for st in STAGES]
        names = list(dict.fromkeys(k for n in self.per for k in n))
        self.sem = {k: ctx.enter_context(nc.semaphore(f"s_{k}")) for k in names}
        self.base, total = [], {k: 1 for k in names}
        for n in self.per:
            self.base.append(dict(total))
            for k, v in n.items():
                total[k] += B * v
        self.total = total


def build(nc, T, out):
    ctx = ExitStack()
    with ctx:
        def sb(name, shape, dt=F32):
            return ctx.enter_context(nc.sbuf_tensor(name, shape, dt))

        def sem(name):
            return ctx.enter_context(nc.semaphore(name))

        sig = Signals(ctx, nc)

        x = sb("x", [P, B, TT * C])
        ident = sb("ident", [P, P])
        caus = sb("caus", [P, S])
        diff = sb("diff", [P, S])
        negs = sb("negs", [P, 16])
        half_pow = sb("half_pow", [P, 32])
        with nc.sbuf_tensor("below", [P, 1024], F32), nc.sbuf_tensor("w2_staged", [P, 2, HT, C], F32R) as w2_staged:
            w2_raw = (w2_staged[:, 0], w2_staged[:, 1])
        scratch = sb("scratch", [P, 5120])
        tmpw = scratch[:, 3072:5120]
        W = {}
        for n, cols in dict(a0_q=C, a0_k=C, a0_v=C, a0_o=C, f0=C, b0_q=C, b0_k=C, b0_v=C, b0_o=C, w1=HID, w3=HID).items():
            W[n] = (sb(f"{n}_h", [P, CT, cols], F32R), sb(f"{n}_l", [P, CT, cols], F32R))
        with nc.sbuf_tensor("mask", [P, 16, S], F32) as mask:
            pass
        w2_tile = sb("w2", [P, 2, HT, C], F32R)
        W["w2"] = (w2_tile[:, 0], w2_tile[:, 1])
        for n in "qkvo":
            W[f"b1_{n}"] = W[f"a0_{n}"]
            W[f"r1_{n}"] = (sb(f"r1_{n}_w", [P, CT, C], F32R),)
        had = sb("had", [P, P], F32R)
        sel = sb("sel", [P, 4, P], F32R)
        had_raw = sb("had_raw", [P, P])
        bq, bk = sb("bq", [P, CT]), sb("bk", [P, CT])
        bv, bo0, bo1, bf = sb("bv", [P, C]), sb("bo0", [P, C]), sb("bo1", [P, C]), sb("bf", [P, C])
        rowbias = {"ffn0": bf, "attn_b0": bo0, "attn_b1": bo1}
        qkvn, projn, nwb = sb("qkvn", [P, CT]), sb("projn", [P, CT]), sb("nwb", [P, C])
        lamv = sb("lamv", [P, 4, 8])
        lamt = sb("lamt", [P, 8])
        lamp = sb("lamp", [P, 2, 8])
        absum = sb("absum", [P, 4])
        qscale = sb("qscale", [P, 4])
        ones = sb("ones", [P, P])

        bst = sb("bst", [P, TT, 6])
        mv = sb("mv", [P, TT, 2])
        ve, rstd = sb("ve", [P, TT]), sb("rstd", [P, TT])
        ms2, ms2e, r2, rr = sb("ms2", [P, TT]), sb("ms2e", [P, TT]), sb("r2", [P, TT]), sb("rr", [P, TT])
        xn = sb("xn", [P, TT, C])
        xT = (sb("xT_h", [P, CT, S], F32R), sb("xT_l", [P, CT, S], F32R))
        QT = (sb("QT_h", [P, CT, S], F32R), sb("QT_l", [P, CT, S], F32R))
        KT = (sb("KT_h", [P, CT, S], F32R), sb("KT_l", [P, CT, S], F32R))
        V = sb("V", [P, TT, 16, 32])
        Vw = sb("Vw", [P, TT, 4, 65])
        Qs = sb("Qs", [P, 8 * 2 * S], F32R)
        Ks = sb("Ks", [P, 8, S], F32R)
        mx = sb("mx", [P, TT, 32])
        MT = (sb("MT_h", [P, S], F32R), sb("MT_l", [P, S], F32R))
        pr = [sb(f"pr{i}", [P, TT * 512]) for i in range(2)]
        OS = sb("OS", [P, S])
        qt, kt_, vt = (scratch[:, 2048 + n * 512:2560 + n * 512].rearrange("p (t c) -> p t c", t=TT) for n in range(3))
        prods = [pr[0][:], pr[1][:], scratch[:, 0:1024], scratch[:, 1024:2048]]
        sc1 = scratch[:, 3584:4608]
        dif, dif2 = scratch[:, 4608:4864], scratch[:, 4864:5120]
        m1, r1, lr1 = sb("m1", [P, HALVES]), sb("r1", [P, HALVES]), sb("lr1", [P, HALVES // 2])
        rec = sb("rec", [P, TT, 4])
        ON = sb("ON", [P, TT, C])
        ON2 = sb("ON2", [P, TT, C])
        sq = sb("sq", [P, TT, C])
        sel_raw = sq[:].rearrange("p t c -> p (t c)")
        swb = ON2[:, 0, :]
        ssq, ssqe, hr = sb("ssq", [P, 32]), sb("ssqe", [P, 32]), sb("hr", [P, 32])
        aT = (sb("aT_h", [P, CT, S], F32R), sb("aT_l", [P, CT, S], F32R))
        sg, hf = (q[:].rearrange("p t c -> p (t c)") for q in (ON, ON2))
        hid = [tuple(Qs[:, 512 * n:512 * n + 512].rearrange("p (a t) -> p a t", a=2) for n in (2 * k, 2 * k + 1))
               for k in range(2)]
        r2t, hr0 = sb("r2t", [P, TT]), sb("hr0", [P, 32])
        absw = tmpw.rearrange("p (j n) -> p j n", j=4)

        qd = nc.dram_tensor("q_stack", [2, 3, P, S], F32, kind="Internal").ap()
        kd = nc.dram_tensor("k_stack", [2, 3, P, S], F32, kind="Internal").ap()

        SC = [ctx.enter_context(nc.psum_tensor(f"SC{i}", [P, 1024], F32)) for i in range(2)]
        OT = [ctx.enter_context(nc.psum_tensor(f"OT{i}", [P, 512], F32)) for i in range(2)]
        pa = ctx.enter_context(nc.psum_tensor("pa", [P, 512], F32))
        pb = ctx.enter_context(nc.psum_tensor("pb", [P, 512], F32))

        x0_in, x_in, first_in, const_in = sem("x0_in"), sem("x_in"), sem("first_in"), sem("const_in")
        negs_done, ones_done, zeroed, had_done = sem("negs_done"), sem("ones_done"), sem("zeroed"), sem("had_done")
        primed = sem("primed")
        passed = sem("passed")
        raw_first, raw_in = ([sem(f"{q}{n}") for n in range(3)] for q in ("raw_first", "raw_in"))
        w_split, w_step = sem("w_split"), sem("w_step")
        had_ps, w2_h_done, w2_l_done = sem("had_ps"), sem("w2_h_done"), sem("w2_l_done")
        dve_setup, act_setup, abs_ps, q_scales = sem("dve_setup"), sem("act_setup"), sem("abs_ps"), sem("q_scales")
        abs_in, abs_rows, abs_sum = sem("abs_in"), sem("abs_rows"), sem("abs_sum")
        mask_exp, mask_done, stack_clear = sem("mask_exp"), sem("mask_done"), sem("stack_clear")

        ORDER = ["a0_q", "a0_k", "a0_v", "a0_o", "f0", "b0_q", "b0_k", "b0_v", "b0_o", "w1", "w3", "r1_q", "r1_k", "r1_v", "r1_o",
                 "b1_q", "b1_k", "b1_v", "b1_o", "w2"]
        LARGE = ("w1", "w3", "w2")
        NEEDS = {"attn_a0": "a0_o", "ffn0": "f0", "attn_b0": "b0_o", "ret1": "r1_o", "ffn1": "w2", "attn_b1": "b1_o"}

        def raw_part(n):
            return 2 if n in LARGE else [m for m in ORDER if m not in LARGE].index(n) % 2

        def raw_view(n):
            at, size = ((0, 512), (512, 512), (1024, 2048))[raw_part(n)]
            return scratch[:, at:at + size].rearrange("p (t n) -> p t n", t=HT if n == "w2" else CT)

        def load_raw(eng, n, arrived):
            eng.dma_start(raw_view(n), T[n].rearrange("(t p) n -> p t n", p=P)).then_inc(arrived[raw_part(n)], 16)

        def split_done(eng, name):
            eng.wait_ge(w_split, ORDER.index(NEEDS[name]) + 1)

        quarter = [SC[n // 2][:, n % 2 * 512:n % 2 * 512 + 512] for n in range(4)]

        def front_psum(st):
            if st.kind in ("narrow", "wide"):
                return quarter
            return [q[:] for q in ((pa, pb, pa, pb) if st.kind == "tokens" else (OT[0],))]

        def sequences(eng, pieces, back, parts=(), between=None):
            for piece in pieces:
                piece(0)
            cuts = [0, *parts, B - 1]
            for n in range(len(cuts) - 1):
                with eng.Fori(cuts[n], cuts[n + 1]) as i:
                    back(i, lambda k: pieces[k](i + 1), False)
                if between and n < len(parts):
                    between(n)
            back(B - 1, lambda k: None, True)

        def is_first(b):
            return isinstance(b, int) and b == 0

        def in_stage(eng, s, i):
            per, base = sig.per[s], sig.base[s]

            apart = eng.engine in (mybir.EngineType.Pool, mybir.EngineType.SP)

            def wait(name, k, alone=apart):
                eng.wait_ge(sig.sem[name], i * per[name] + (base[name] + k))
                if alone:
                    eng.sem_inc(passed, 1)

            def prev(name, alone=apart):
                if name in per:
                    eng.wait_ge(sig.sem[name], i * per[name] + base[name])
                    if alone:
                        eng.sem_inc(passed, 1)
            return wait, prev

        def stage_start(eng, s):
            if s:
                eng.wait_ge(sig.sem["xres"], sig.base[s]["xres"])

        def three(pe, out_ap, left, right, first, last):
            terms = [(a, b) for a in range(len(left)) for b in range(len(right)) if a + b < 2]
            for n, (a, b) in enumerate(terms):
                ins = pe.matmul(out_ap, left[a], right[b], start=first and n == 0, stop=last and n == len(terms) - 1)
            return ins

        def product(pe, out_ap, left, right, tiles):
            for t in range(tiles):
                ins = three(pe, out_ap, left(t), right(t), t == 0, t == tiles - 1)
            return ins

        QM = tuple(Qs[:, n * 4 * S:(n + 1) * 4 * S].rearrange("p (h t) -> p h t", h=4) for n in range(2))

        def stack_q(st):
            return Qs[:, 0:st.groups * st.slots * S].rearrange("p (g s t) -> p g s t", g=st.groups, s=st.slots)

        def cleared(s):
            return 1 + sum(t.kind in ("narrow", "wide") for t in STAGES[:s])

        def tile_sums(t, last):
            return 2 * DEPTH1 + (4 if t == 0 else 8 if last else 8 + DEPTH1)

        n_const = 16 * (3 + 4 + 6 + 4)
        block = ctx.enter_context(nc.Block())

        @block.sync
        def _(sp):
            for b in range(B):
                sp.dma_start(x[:, b, :].rearrange("p (t c) -> p t c", t=TT),
                             T["hidden"][b].rearrange("(t p) c -> p t c", p=P)).then_inc(x_in if b else x0_in, 16)
                if b == 0:
                    load_raw(sp, "a0_q", raw_first)
                    load_raw(sp, "a0_k", raw_first)
                    for dst, src in ((ident[:], T["ident"]), (negs[:], T["r1_s"].rearrange("(a n) -> a n", a=1).to_broadcast([P, 16])),
                                     (diff[:], T["diff"])):
                        sp.dma_start(dst, src).then_inc(first_in, 16)
            for dst, src in ((caus[:], T["caus"]), (had_raw[:], T["had"]), (sel_raw, T["sel"])):
                sp.dma_start(dst, src).then_inc(const_in, 16)
            for dst, n in ((bq, "b0_bq"), (bk, "b0_bk"), (qkvn, "r1_qkvn"), (projn, "r1_projn")):
                sp.dma_start(dst[:], T[n]).then_inc(const_in, 16)
            for dst, n in ((bv[:], "b0_bv"), (bo0[:], "b0_bo"), (bo1[:], "b1_bo"), (bf[:], "f0_b"), (swb, "f0_s"), (nwb[:], "r1_nw")):
                sp.dma_start(dst, T[n].rearrange("(a n) -> a n", a=1).to_broadcast([P, C])).then_inc(const_in, 16)
            for j, n in enumerate(("lq1", "lk1", "lq2", "lk2")):
                sp.dma_start(lamv[:, j, :], T[n].rearrange("(a n) -> a n", a=1).to_broadcast([P, 8])).then_inc(const_in, 16)
            load_raw(sp, "w1", raw_first)
            for j, n in enumerate(("r1_q", "r1_k", "r1_v", "r1_o")):
                sp.dma_start(absw[:, j, :].rearrange("p (t n) -> p t n", t=CT), T[n].rearrange("(t p) n -> p t n", p=P)).then_inc(abs_in, 16)

            sp.wait_ge(primed, 1)
            for s, st in enumerate(STAGES):
                if st.kind == "narrow":
                    stage_start(sp, s)
                    sp.wait_ge(stack_clear, cleared(s))
                    D, Qg = st.depth, stack_q(st)

                    def stores(b):
                        wait, prev = in_stage(sp, s, b)
                        for parts, dram, low, store, load in ((QT, qd, "ql", "qstore", "qload"), (KT, kd, "kl", "kstore", "kload")):
                            wait(low, 1)
                            prev(load)
                            for t in range(3):
                                part = (0, 0, 1)[t] if dram is qd else (0, 1, 0)[t]
                                sp.dma_start(dram[:, t, :, :].rearrange("h p t -> p h t"),
                                             parts[part][:].bitcast(F32)).then_inc(sig.sem[store], 16)

                    def loads(b):
                        wait, prev = in_stage(sp, s, b)
                        prev("scoresT")
                        for slot in range(st.slots):
                            r0 = st.rows * slot + 2
                            if slot == 0:
                                wait("qstore", 48)
                            sp.dma_start(Qg[r0:r0 + 3 * D, :, slot, :].bitcast(F32),
                                         qd[slot].rearrange("t (d j) n -> (t d) j n", j=P // D)).then_inc(sig.sem["qload"], 16)
                            if slot == 0:
                                wait("kstore", 48)
                            sp.dma_start(Ks[r0:r0 + 3 * D, :, :].bitcast(F32),
                                         kd[slot].rearrange("t (d j) n -> (t d) j n", j=P // D)).then_inc(sig.sem["kload"], 16)

                    def back(i, ahead, last):
                        wait, prev = in_stage(sp, s, i)
                        if st.n_max:
                            wait("maxl", 1)
                            wait("scores", st.n_max)
                            for slot in range(st.slots):
                                for part in range(2):
                                    r = st.rows * slot + part
                                    sp.dma_start(Qg[r:r + 1, :, slot, :].bitcast(F32),
                                                 MT[part][8 * slot:8 * slot + 8, :].bitcast(F32)).then_inc(sig.sem["maxrows"], 16)
                        ahead(0)
                        ahead(1)

                    sequences(sp, [stores, loads], back)
                if s == len(STAGES) - 1:
                    with sp.Fori(0, B) as i:
                        wait, prev = in_stage(sp, s, i)
                        wait("xres", sig.per[s]["xres"])
                        sp.dma_start(out[bass.ds(i, 1)].rearrange("a (t p) c -> p (a t) c", p=P),
                                     x[:, bass.ds(i, 1), :].rearrange("p a (t c) -> p (a t) c", t=TT)).then_inc(sig.sem["stored"], 16)
                    sp.wait_ge(sig.sem["stored"], sig.total["stored"])

        @block.gpsimd
        def _(pool):
            steps = 0

            def step(ins):
                nonlocal steps
                steps += 1
                ins.then_inc(w_step, 1)
                pool.wait_ge(w_step, steps)

            step(pool.memset(half_pow[:], -0.5))
            pool.wait_ge(first_in, 48)
            pool.tensor_scalar(negs[:], negs[:], -1.0, None, ALU.mult).then_inc(negs_done, 1)

            def clear_stack():
                step(pool.memset(Qs[:].bitcast(F32), 0.0))
                pool.sem_inc(stack_clear, 1)

            def prepare(names):
                for n in names:
                    v = raw_view(n)
                    same = [m for m in ORDER if raw_part(m) == raw_part(n)]
                    if n == same[0]:
                        pool.wait_ge(raw_first[raw_part(n)], 16)
                    else:
                        pool.wait_ge(raw_in[raw_part(n)], 16 * same.index(n))
                    h = W[n][0]
                    low = len(W[n]) > 1 and W[n][1]
                    if n == "f0":
                        pool.wait_ge(const_in, n_const)
                        for t in range(CT):
                            step(pool.tensor_tensor(v[:, t, :], v[:, t, :], swb, ALU.mult))
                    if n.startswith("r1"):
                        a = qscale[:, 3:4] if n == "r1_o" else qscale[:, 2:3]
                        pool.wait_ge(q_scales, 2)
                        step(pool.tensor_scalar(v, v, a, 1.0, ALU.mult, ALU.min))
                        step(pool.tensor_scalar(v, v, -1.0, ROUND_MAGIC, ALU.max, ALU.add))
                        step(pool.tensor_scalar(v, v, -ROUND_MAGIC, None, ALU.add))
                    if n == "w2":
                        src, dst = v, tmpw.rearrange("p (t n) -> p t n", t=HT)
                        for stride in (1, 2, 4):
                            sv = src.rearrange("p (a two b) n -> p a two (b n)", two=2, b=stride)
                            dv = dst.rearrange("p (a two b) n -> p a two (b n)", two=2, b=stride)
                            step(pool.tensor_tensor(dv[:, :, 0, :], sv[:, :, 0, :], sv[:, :, 1, :], ALU.add))
                            step(pool.tensor_tensor(dv[:, :, 1, :], sv[:, :, 0, :], sv[:, :, 1, :], ALU.subtract))
                            src, dst = dst, src
                        v = src
                        h, low = w2_raw
                        step(pool.tensor_scalar(v, v, float(HID) ** -0.5, None, ALU.mult))
                    step(pool.tensor_copy(h[:], v))
                    if low:
                        step(pool.tensor_tensor(low[:], v, h[:].bitcast(F32), ALU.subtract))
                    pool.sem_inc(w_split, 1)
                    if n != same[-1]:
                        load_raw(pool, same[same.index(n) + 1], raw_in)

            def cut_mask():
                for h in range(16):
                    pool.wait_ge(mask_exp, h + 1)
                    step(pool.tensor_tensor(mask[:, h, :], mask[:, h, :], caus[:], ALU.mult))
                pool.sem_inc(mask_done, 1)

            def clear_wide():
                for q in (QM[0], QM[1], MT[0][:], MT[1][:]):
                    step(pool.memset(q.bitcast(F32), 0.0))
                pool.sem_inc(stack_clear, 1)

            jobs = {0: [lambda: prepare(ORDER[4:7]), lambda: prepare(ORDER[7:9]), cut_mask, lambda: prepare(ORDER[9:11])],
                    1: [clear_wide],
                    2: [lambda: prepare(ORDER[11:14]), lambda: prepare(ORDER[14:16]), lambda: prepare(ORDER[16:19]),
                        lambda: prepare(ORDER[19:])],
                    3: [clear_stack]}

            clear_stack()
            prepare(ORDER[:4])
            pool.wait_ge(primed, 1)
            for s, st in enumerate(STAGES):
                stage_start(pool, s)

                def rstd_of(b):
                    wait, prev = in_stage(pool, s, b)
                    wait("meanvar", TT)
                    pool.tensor_scalar(ve[:], mv[:, :, 1], LN_EPS, None, ALU.add).then_inc(sig.sem["vareps"], 1)
                    wait("vareps", 1)
                    pool.tensor_tensor(rstd[:], ve[:], half_pow[:, 0:TT], ALU.pow).then_inc(sig.sem["rstd"], 1)
                    if st.name == "ret1":
                        wait("ms2", 1)
                        pool.tensor_scalar(ms2e[:], ms2[:], F32_EPS, None, ALU.add).then_inc(sig.sem["ms2e"], 1)
                        wait("ms2e", 1)
                        pool.tensor_tensor(r2[:], ms2e[:], half_pow[:, 0:TT], ALU.pow).then_inc(sig.sem["r2"], 1)
                    if st.name in rowbias:
                        wait("xn", TT)
                        xv = x[:, bass.ds(b, 1), :].rearrange("p a (t c) -> p (a t) c", t=TT)
                        bb = rowbias[st.name][:].rearrange("p (a c) -> p a c", a=1).to_broadcast([P, TT, C])
                        pool.tensor_tensor(xv, xv, bb, ALU.add).then_inc(sig.sem["xbias"], 1)
                    if st.kind == "narrow" and st.n_max:
                        prev("scoresT")
                        Qg = stack_q(st)
                        for slot in range(st.slots):
                            r = st.rows * slot
                            pool.memset(Qg[r:r + 2, :, slot, :].bitcast(F32), 0.0).then_inc(sig.sem["maxzero"], 1)
                            wait("maxzero", slot + 1)

                def back(i, ahead, last):
                    wait, prev = in_stage(pool, s, i)
                    ahead(0)
                    if st.name == "attn_b1":
                        wait("ssq", 1)
                        pool.tensor_scalar(ssqe[:], ssq[:], 1e-5, None, ALU.add).then_inc(sig.sem["ssqe"], 1)
                        wait("ssqe", 1)
                        pool.tensor_tensor(hr0[:], ssqe[:], half_pow[:], ALU.pow).then_inc(sig.sem["hpow"], 1)
                        wait("hpow", 1)
                        pool.tensor_scalar(ssqe[:], ssq[:], F32_MAX / 16, None, ALU.is_lt).then_inc(sig.sem["inrange"], 1)
                        wait("inrange", 1)
                        pool.tensor_tensor(hr[:], hr0[:], ssqe[:], ALU.mult).then_inc(sig.sem["hr"], 1)
                    if st.name == "ret1":
                        for q, e, r, eps in (("sq1", "e1", "rn1", 1e-6), ("sq2", "e2", "rn2", F32_EPS)):
                            wait(q, 1)
                            pool.tensor_scalar(ssqe[:, 0:TT], ssq[:, 0:TT], 1.0 / C, eps, ALU.mult, ALU.add).then_inc(sig.sem[e], 1)
                            wait(e, 1)
                            pool.tensor_tensor(hr[:, 0:TT], ssqe[:, 0:TT], half_pow[:, 0:TT], ALU.pow).then_inc(sig.sem[r], 1)

                todo = jobs.get(s, [])
                sequences(pool, [rstd_of], back, range(1, len(todo) + 1), lambda n: todo[n]())

        def evac_out(act, st, wait, prev, o):
            rows = 65 if st.kind == "wide" else P
            wait("pv", o + 1 if st.kind == "wide" else 2 * o + 2)
            if o:
                wait("out_tok", o)
            else:
                prev("out_tok")
            act.activation(OS[0:rows, :], OT[o % 2][0:rows, 0:S], ACT.Copy).then_inc(sig.sem["outT"], 1)

        @block.scalar
        def _(act):
            for signal in sig.sem.values():
                act.sem_inc(signal, 1)
            act.sem_inc(primed, 1)
            act.wait_ge(negs_done, 1)
            for h in range(16):
                act.activation(mask[:, h, :], diff[:], ACT.Exp, scale=negs[:, h:h + 1]).then_inc(mask_exp, 1)
            for s, st in enumerate(STAGES):
                stage_start(act, s)
                if s == 1:
                    act.wait_ge(dve_setup, 2)
                    act.activation(lamp[:, :, 2:3], lamp[:, :, 0:1], ACT.Exp).then_inc(act_setup, 1)
                if st.kind == "ffn1" and s == 5:
                    for t in range(0, HT, 2):
                        act.wait_ge(had_ps, t // 2 + 1)
                        act.activation(W["w2"][0][:, t:t + 2, :].rearrange("p a n -> p (a n)"), OT[t // 2 % 2][:], ACT.Copy)\
                           .then_inc(w2_h_done, 1)
                if st.kind == "wide":
                    act.wait_ge(stack_clear, cleared(s))
                fp = front_psum(st)
                ret = st.name == "ret1"

                def x_high(b):
                    wait, prev = in_stage(act, s, b)
                    wait("xT", 1)
                    prev({"ffn0": "y", "ffn1": "up"}.get(st.kind, "vp"))
                    if ret:
                        for t in range(CT):
                            act.activation(xT[0][:, t, :], fp[0][:, t * S:(t + 1) * S], ACT.Copy, scale=qkvn[:, t:t + 1])\
                               .then_inc(sig.sem["xh"], 1)
                    else:
                        act.activation(xT[0][:].rearrange("p a n -> p (a n)"), fp[0], ACT.Copy).then_inc(sig.sem["xh"], 1)

                def qk_high(b):
                    wait, prev = in_stage(act, s, b)
                    if st.kind == "tokens":
                        for dst, p, ps, done in ((qt, "qp", fp[1], "qev"), (kt_, "kp", fp[2], "kev")):
                            wait(p, 1)
                            if not (is_first(b)):
                                wait("prod", 2 * DEPTH1 - TT * PRODS)
                            act.activation(dst.rearrange("p t c -> p (t c)"), ps, ACT.Copy).then_inc(sig.sem[done], 1)
                        return
                    if st.kind in ("ffn0", "ffn1"):
                        return
                    for parts, p, ps, h, bias, free in ((QT, "qp", fp[1], "qh", bq, "qstore"), (KT, "kp", fp[2], "kh", bk, "kstore")):
                        wait(p, 1)
                        if st.kind == "narrow":
                            prev(free)
                            act.activation(parts[0][:].rearrange("p a n -> p (a n)"), ps, ACT.Copy, scale=qscale[:, 0:1] if ret else 1.0)\
                               .then_inc(sig.sem[h], 1)
                            continue
                        prev("scoresT")
                        if parts is QT:
                            for n in range(4):
                                t, r0 = n // 2, 64 * (n % 2)
                                act.activation(QM[0][r0:r0 + 64, n, :], ps[r0:r0 + 64, t * S:(t + 1) * S], ACT.Identity,
                                               bias=bias[r0:r0 + 64, t:t + 1]).then_inc(sig.sem[h], 1)
                        else:
                            for t in range(CT):
                                act.activation(parts[0][:, t, :], ps[:, t * S:(t + 1) * S], ACT.Identity, bias=bias[:, t:t + 1])\
                                   .then_inc(sig.sem[h], 1)

                def v_out(b):
                    wait, prev = in_stage(act, s, b)
                    if st.kind == "tokens":
                        wait("vp", 1)
                        if not (is_first(b)):
                            wait("prod", 2 * DEPTH1 + 2 * 4 + DEPTH1 - TT * PRODS)
                        act.activation(vt.rearrange("p t c -> p (t c)"), fp[3], ACT.Copy).then_inc(sig.sem["vev"], 1)
                    if st.kind == "narrow":
                        wait("vp", 1)
                        prev("pv")
                        act.activation(V[:, :, :, 0:16], fp[3].rearrange("p (t h d) -> p t h d", t=TT, h=16), ACT.Copy,
                                       scale=qscale[:, 0:1] if ret else 1.0).then_inc(sig.sem["vev"], 1)

                def back(i, ahead, last):
                    wait, prev = in_stage(act, s, i)
                    if st.kind == "ffn0":
                        ahead(0)
                    if st.kind == "ffn1":
                        for r in range(HT // 2):
                            wait("up", r + 1)
                            if r:
                                wait("hid", r)
                            else:
                                prev("hid")
                            act.activation(sg[:], SC[r % 2][:, 0:512], ACT.Silu).then_inc(sig.sem["silu"], 1)
                            if r == HT // 2 - 1:
                                ahead(0)
                            wait("hid", r + 1)
                            if r >= 2:
                                wait("down", r - 1)
                            else:
                                prev("down")
                            act.activation(hid[r % 2][0][:].rearrange("p a n -> p (a n)"), hf[:], ACT.Copy).then_inc(sig.sem["hh"], 1)
                    if st.kind == "tokens":
                        for t in range(TT):
                            wait("less", t + 1)
                            act.activation(sc1, sc1, ACT.Exp, scale=st.scale).then_inc(sig.sem["probs"], 1)
                            if t == 0:
                                ahead(0)
                                ahead(1)
                                prev("hn")
                            else:
                                ahead(2)
                            wait("summed", tile_sums(t, last))
                            act.activation(ON[:, t, :], OT[t][:, 0:C], ACT.Copy).then_inc(sig.sem["outT"], 1)
                    if st.kind in ("narrow", "wide"):
                        if st.n_max:
                            nh = 4 if st.kind == "wide" else st.groups * st.slots
                            wait("maxT", 1)
                            prev("maxrows" if st.kind == "narrow" else "scoresT")
                            act.activation(MT[0][0:nh, :], pa[0:nh, 0:S], ACT.Copy, scale=-1.0).then_inc(sig.sem["maxh"], 1)
                            if st.kind == "narrow":
                                ahead(0)
                                ahead(1)
                        for r in range(st.n_exp):
                            if st.n_max:
                                wait("scoresT", r + 1)
                                if r >= 2:
                                    wait("pv", (r - 1) * (2 if st.kind == "wide" else 1))
                                else:
                                    prev("pv")
                                act.activation(pr[r % 2][:], SC[r % 2][:], ACT.Exp, scale=st.scale).then_inc(sig.sem["probs"], 1)
                            if st.kind == "narrow" and r % 2 == 0 and r >= 2:
                                evac_out(act, st, wait, prev, (r - 2) // 2)
                        if st.kind == "wide":
                            ahead(0)
                            for o in range(4):
                                evac_out(act, st, wait, prev, o)
                            ahead(1)
                        else:
                            evac_out(act, st, wait, prev, st.n_out - 1)
                            if ret:
                                ahead(0)
                                ahead(1)
                            ahead(2)
                    if st.kind in ("narrow", "wide", "tokens"):
                        wait("aT", 1)
                        prev("y")
                        if ret:
                            for t in range(CT):
                                act.activation(aT[0][:, t, :], pa[:, t * S:(t + 1) * S], ACT.Copy, scale=projn[:, t:t + 1])\
                                   .then_inc(sig.sem["ah"], 1)
                        else:
                            act.activation(aT[0][:].rearrange("p a n -> p (a n)"), pa[:], ACT.Copy).then_inc(sig.sem["ah"], 1)

                sequences(act, [x_high, qk_high, v_out], back)

        @block.vector
        def _(dve):
            dve.wait_ge(primed, 1)
            dve.memset(ones[:], 1.0).then_inc(ones_done, 1)
            dve.memset(Ks[:].bitcast(F32), 0.0).then_inc(zeroed, 1)
            dve.memset(V[:], 0.0).then_inc(zeroed, 1)
            dve.memset(Vw[:, :, :, 64:65], 1.0).then_inc(ones_done, 1)
            dve.wait_ge(zeroed, 2)
            dve.memset(V[:, :, :, 16:17], 1.0).then_inc(ones_done, 1)
            for slot in range(ATTN_A0["slots"]):
                r = ATTN_A0["rows"] * slot
                dve.memset(Ks[r:r + 2, :, :].bitcast(F32), 1.0).then_inc(ones_done, 1)
            for s, st in enumerate(STAGES):
                stage_start(dve, s)
                fp = front_psum(st)
                ret = st.name == "ret1"
                if s == 1:
                    dve.wait_ge(const_in, n_const)
                    dve.tensor_copy(had[:], had_raw[:]).then_inc(had_done, 1)
                    dve.tensor_copy(sel[:].rearrange("a b c -> a (b c)"), sel_raw).then_inc(had_done, 1)
                    dve.wait_ge(had_done, 2)
                    lprod = sq[:, 0, 0:16].rearrange("p (a b) -> p a b", a=2)
                    dve.tensor_tensor(lprod, lamv[:, 0:4:2, :], lamv[:, 1:4:2, :], ALU.mult).then_inc(dve_setup, 1)
                    dve.wait_ge(dve_setup, 1)
                    dve.tensor_reduce(lamp[:, :, 0:1], lprod, AX.X, ALU.add).then_inc(dve_setup, 1)
                    dve.wait_ge(abs_in, 64)
                    for j, n in enumerate(("q", "k", "v", "o")):
                        dve.tensor_reduce(absum[:, j:j + 1], absw[:, j, :], AX.X, ALU.add, apply_absolute_value=True).then_inc(abs_rows, 1)
                    dve.wait_ge(act_setup, 1)
                    dve.tensor_tensor(lamt[:, 0:1], lamp[:, 1, 2:3], lamp[:, 0, 2:3], ALU.subtract).then_inc(dve_setup, 1)
                    dve.wait_ge(dve_setup, 3)
                    dve.tensor_scalar(lamt[:, 1:2], lamt[:, 0:1], -LAM_INIT, None, ALU.add).then_inc(dve_setup, 1)
                    dve.wait_ge(abs_ps, 1)
                    dve.tensor_reduce(qscale[:, 0:1], pb[:, 0:3], AX.X, ALU.add).then_inc(abs_sum, 1)
                    dve.tensor_copy(qscale[:, 1:2], pb[:, 3:4]).then_inc(abs_sum, 1)
                    dve.wait_ge(abs_sum, 2)
                    dve.tensor_scalar(qscale[:, 0:1], qscale[:, 0:1], 1.0 / (3 * C * C), 1e-5, ALU.mult, ALU.max).then_inc(abs_sum, 1)
                    dve.tensor_scalar(qscale[:, 1:2], qscale[:, 1:2], 1.0 / (C * C), 1e-5, ALU.mult, ALU.max).then_inc(abs_sum, 1)
                    dve.wait_ge(abs_sum, 4)
                    dve.reciprocal(qscale[:, 2:4], qscale[:, 0:2]).then_inc(q_scales, 2)
                if ret:
                    dve.wait_ge(mask_done, 1)
                if st.name == "ffn1" and s == 5:
                    for t in range(0, HT, 2):
                        dve.wait_ge(w2_h_done, t // 2 + 1)
                        dve.tensor_tensor(W["w2"][1][:, t:t + 2, :].rearrange("p a n -> p (a n)"), OT[t // 2 % 2][:],
                                          W["w2"][0][:, t:t + 2, :].rearrange("p a n -> p (a n)").bitcast(F32), ALU.subtract)\
                           .then_inc(w2_l_done, 1)

                def stats(b):
                    wait, prev = in_stage(dve, s, b)
                    if s == 0:
                        dve.wait_ge(x0_in, 16) if is_first(b) else dve.wait_ge(x_in, 16 * (B - 1))
                    for t in range(TT):
                        dve.bn_stats(bst[:, t, :], x[:, bass.ds(b, 1), t * C:(t + 1) * C]).then_inc(sig.sem["stats"], 1)
                    wait("stats", TT, alone=True)
                    for t in range(TT):
                        dve.bn_aggr(mv[:, t, :], bst[:, t, :]).then_inc(sig.sem["meanvar"], 1)

                def mean_square(b):
                    wait, prev = in_stage(dve, s, b)
                    if ret:
                        wait("rstd", 1)
                        dve.tensor_tensor(r2t[:], rstd[:], rstd[:], ALU.mult).then_inc(sig.sem["rstd_sq"], 1)
                        wait("rstd_sq", 1)
                        dve.tensor_tensor(ms2[:], r2t[:], mv[:, :, 1], ALU.mult).then_inc(sig.sem["ms2"], 1)

                def normalise(b):
                    wait, prev = in_stage(dve, s, b)
                    wait("rstd", 1)
                    scale_of = rstd
                    if ret:
                        wait("r2", 1)
                        dve.tensor_tensor(rr[:], r2[:], rstd[:], ALU.mult).then_inc(sig.sem["rr"], 1)
                        wait("rr", 1)
                        scale_of = rr
                    prev("xT")
                    for t in range(TT):
                        dve.tensor_scalar(xn[:, t, :], x[:, bass.ds(b, 1), t * C:(t + 1) * C], mv[:, t, 0:1], scale_of[:, t:t + 1],
                                          ALU.subtract, ALU.mult).then_inc(sig.sem["xn"], 1)

                def x_low(b):
                    wait, prev = in_stage(dve, s, b)
                    wait("xh", sig.per[s]["xh"])
                    if ret:
                        for t in range(CT):
                            ins = dve.scalar_tensor_tensor(out=xT[1][:, t, :], in0=fp[0][:, t * S:(t + 1) * S], scalar=qkvn[:, t:t + 1],
                                                           in1=xT[0][:, t, :].bitcast(F32), op0=ALU.mult, op1=ALU.subtract)
                        ins.then_inc(sig.sem["xl"], 1)
                    else:
                        dve.tensor_tensor(xT[1][:].rearrange("p a n -> p (a n)"), fp[0], xT[0][:].bitcast(F32).rearrange("p a n -> p (a n)"),
                                          ALU.subtract).then_inc(sig.sem["xl"], 1)

                def qk_low(b):
                    wait, prev = in_stage(dve, s, b)
                    if st.kind == "tokens":
                        return
                    for parts, ps, h, l, bias in ((QT, fp[1], "qh", "ql", bq), (KT, fp[2], "kh", "kl", bk)):
                        wait(h, sig.per[s][h])
                        if st.kind == "wide" and parts is QT:
                            for n in range(4):
                                t, r0 = n // 2, 64 * (n % 2)
                                dve.scalar_tensor_tensor(out=QM[1][r0:r0 + 64, n, :], in0=ps[r0:r0 + 64, t * S:(t + 1) * S],
                                                         scalar=bias[r0:r0 + 64, t:t + 1], in1=QM[0][r0:r0 + 64, n, :].bitcast(F32),
                                                         op0=ALU.add, op1=ALU.subtract).then_inc(sig.sem[l], 1)
                        elif st.kind == "wide":
                            for t in range(CT):
                                dve.scalar_tensor_tensor(out=parts[1][:, t, :], in0=ps[:, t * S:(t + 1) * S], scalar=bias[:, t:t + 1],
                                                         in1=parts[0][:, t, :].bitcast(F32), op0=ALU.add, op1=ALU.subtract)\
                                   .then_inc(sig.sem[l], 1)
                        else:
                            flat = [q[:].rearrange("p a n -> p (a n)") for q in parts]
                            a = qscale[:, 0:1] if ret else 1.0
                            dve.scalar_tensor_tensor(out=flat[1], in0=ps, scalar=a, in1=flat[0].bitcast(F32),
                                                     op0=ALU.mult, op1=ALU.subtract).then_inc(sig.sem[l], 1)
                    if st.kind == "wide":
                        wait("vp", 1)
                        prev("pv")
                        for t in range(TT):
                            ins = dve.tensor_tensor(Vw[:, t, :, 0:64], fp[3][:, t * C:(t + 1) * C].rearrange("p (h d) -> p h d", h=4),
                                                    bv[:].rearrange("p (h d) -> p h d", h=4), ALU.add)
                        ins.then_inc(sig.sem["vev"], 1)

                def products(wait, first, ring, pieces):
                    for u, (dst_of, in0, in1) in enumerate(pieces):
                        if not first or u >= 4:
                            wait("summed", ring + u - 3)
                        dve.tensor_tensor(dst_of(prods[u % 4]), in0, in1, ALU.mult).then_inc(sig.sem["prod"], 1)

                def score_products(wait, first, ring, t):
                    qv, kv = (q[:, t, :].rearrange("p (d q) -> p d q", d=DEPTH1) for q in (qt, kt_))
                    products(wait, first, ring, [
                        (lambda b: b.rearrange("p (q k) -> p q k", q=HALVES),
                         qv[:, d, :].rearrange("p (q a) -> p q a", a=1).to_broadcast([P, HALVES, HALVES]),
                         kv[:, d, :].rearrange("p (a k) -> p a k", a=1).to_broadcast([P, HALVES, HALVES])) for d in range(DEPTH1)])

                def first_tile(b):
                    wait, prev = in_stage(dve, s, b)
                    wait("kev", 1)
                    score_products(wait, is_first(b), 0 if is_first(b) else -4, 0)

                def masked(wait, prev, r):
                    wait("scoresT", r + 1)
                    if r >= 2:
                        wait("pv", r - 1)
                    else:
                        prev("pv")
                    heads = mask[:, r:16:8, :]
                    pv_, sv = (q[:].rearrange("p (k h t) -> p k h t", k=2, h=2) for q in (pr[r % 2], SC[r % 2]))
                    dve.tensor_tensor(pv_[:, 0], sv[:, 0], heads, ALU.mult)
                    dve.tensor_tensor(pv_[:, 1, :, P:S], sv[:, 1, :, P:S], heads[:, :, 0:P], ALU.mult).then_inc(sig.sem["probs"], 1)

                def heads_out(wait, prev, o):
                    wait("out_tok", o + 1)
                    ps = (pb, pa)[o % 2]
                    if o == 0:
                        prev("aT")
                    elif st.n_max:
                        wait("normed", o)
                    if st.kind == "wide":
                        pv_ = ps[:, 0:TT * 65].rearrange("p (t c) -> p t c", t=TT)
                        dve.reciprocal(rec[:, :, 0:1], pv_[:, :, 64:65]).then_inc(sig.sem["recip"], 1)
                        wait("recip", o + 1)
                        for t in range(TT):
                            ins = dve.tensor_scalar(ON[:, t, 64 * o:64 * o + 64], pv_[:, t, 0:64], rec[:, t, 0:1], None, ALU.mult)
                        ins.then_inc(sig.sem["normed"], 1)
                        return
                    pv_ = ps[:, 0:TT * P].rearrange("p (t h d) -> p t h d", t=TT, h=4)
                    if ret:
                        for t in range(TT):
                            ins = dve.tensor_scalar(ON[:, t, 64 * o:64 * o + 64].rearrange("p (h d) -> p h d", h=4),
                                                    pv_[:, t, :, 0:16], 0.25, None, ALU.mult)
                        ins.then_inc(sig.sem["normed"], 1)
                        return
                    dve.reciprocal(rec[:], pv_[:, :, :, 16]).then_inc(sig.sem["recip"], 1)
                    wait("recip", o + 1)
                    for t in range(TT):
                        ins = dve.tensor_tensor(ON[:, t, 64 * o:64 * o + 64].rearrange("p (h d) -> p h d", h=4), pv_[:, t, :, 0:16],
                                                rec[:, t, :].rearrange("p (h d) -> p h d", d=1).to_broadcast([P, 4, 16]), ALU.mult)
                    ins.then_inc(sig.sem["normed"], 1)

                def back(i, ahead, last):
                    wait, prev = in_stage(dve, s, i)
                    if st.kind == "ffn0":
                        ahead(0)
                        ahead(2)
                    if st.kind == "ffn1":
                        for r in range(HT // 2):
                            wait("silu", r + 1)
                            if r:
                                wait("hl", r)
                            else:
                                prev("hl")
                            dve.tensor_tensor(hf[:], SC[r % 2][:, 512:1024], sg[:], ALU.mult).then_inc(sig.sem["hid"], 1)
                            if r == HT // 2 - 1:
                                ahead(3)
                            wait("hh", r + 1)
                            dve.tensor_tensor(hid[r % 2][1][:].rearrange("p a n -> p (a n)"), hf[:],
                                              hid[r % 2][0][:].bitcast(F32).rearrange("p a n -> p (a n)"), ALU.subtract).then_inc(sig.sem["hl"], 1)
                            if r == 0:
                                ahead(0)
                            if r == 1:
                                ahead(2)
                    if st.kind in ("narrow", "wide"):
                        nr = st.n_max // 2
                        if st.n_max:
                            prev("maxT")
                        for r in range(st.n_max):
                            wait("scores", r + 1)
                            t, k = divmod(r, nr)
                            dve.tensor_reduce(mx[:, t, 4 * k:4 * k + 4], SC[r % 2][:].rearrange("p (h k) -> p h k", h=4), AX.X, ALU.max)\
                               .then_inc(sig.sem["rowmax"], 1)
                            if r == 0:
                                ahead(0)
                            if r == 4:
                                ahead(2)
                        if st.n_max:
                            nh = 4 * nr
                            wait("maxh", 1)
                            dve.scalar_tensor_tensor(out=MT[1][0:nh, :], in0=pa[0:nh, 0:S], scalar=-1.0, in1=MT[0][0:nh, :].bitcast(F32),
                                                     op0=ALU.mult, op1=ALU.subtract).then_inc(sig.sem["maxl"], 1)
                        if st.kind == "wide":
                            ahead(2)
                            ahead(3)
                        if st.name == "attn_a0":
                            ahead(3)
                            ahead(4)
                        for o in range(st.n_out):
                            if ret:
                                if o == 0:
                                    masked(wait, prev, 0)
                                    masked(wait, prev, 1)
                                    ahead(0)
                                if o < st.n_out - 1:
                                    masked(wait, prev, 2 * o + 2)
                                    ahead(1) if o == 0 else None
                                    masked(wait, prev, 2 * o + 3)
                                    ahead(2) if o == 1 else None
                            heads_out(wait, prev, o)
                        if st.kind == "wide":
                            ahead(4)
                        if ret:
                            wait("normed", st.n_out)
                            for src, dst, q, r, n in ((ON, ON2, "sq1", "rn1", "n1"), (ON2, ON, "sq2", "rn2", "n2")):
                                for t in range(TT):
                                    ins = dve.tensor_tensor_reduce(out=sq[:, t, :], in0=src[:, t, :], in1=src[:, t, :], scale=1.0, scalar=0.0,
                                                                   op0=ALU.mult, op1=ALU.add, accum_out=ssq[:, t:t + 1])
                                ins.then_inc(sig.sem[q], 1)
                                ahead(3 if q == "sq1" else 4)
                                wait(r, 1)
                                for t in range(TT):
                                    if q == "sq1":
                                        ins = dve.scalar_tensor_tensor(out=dst[:, t, :], in0=src[:, t, :], scalar=hr[:, t:t + 1], in1=nwb[:],
                                                                       op0=ALU.mult, op1=ALU.mult)
                                    else:
                                        ins = dve.tensor_scalar(dst[:, t, :], src[:, t, :], hr[:, t:t + 1], None, ALU.mult)
                                ins.then_inc(sig.sem[n], 1)
                                wait(n, 1)
                    if st.kind == "tokens":
                        s3 = sc1.rearrange("p (q k) -> p q k", q=HALVES)
                        HD = HALVES // 2
                        d3, e3 = (q.rearrange("p (a h) -> p a h", a=HD) for q in (dif, dif2))
                        ahead(0)
                        score_products(wait, False, DEPTH1, 1)
                        ahead(2)
                        for t in range(TT):
                            wait("summed", DEPTH1 * (t + 1))
                            if t:
                                wait("part2", t)
                            dve.tensor_scalar(sc1, SC[t][:], F32_MAX, -F32_MAX, ALU.min, ALU.max).then_inc(sig.sem["clamped"], 1)
                            wait("clamped", t + 1)
                            dve.tensor_reduce(m1[:], s3, AX.X, ALU.max).then_inc(sig.sem["smax"], 1)
                            wait("smax", t + 1)
                            dve.tensor_tensor(s3, s3, m1[:].rearrange("p (q a) -> p q a", a=1).to_broadcast([P, HALVES, HALVES]),
                                              ALU.subtract).then_inc(sig.sem["less"], 1)
                            if t == 0:
                                ahead(3)
                            wait("probs", t + 1)
                            dve.tensor_reduce(r1[:], s3, AX.X, ALU.add).then_inc(sig.sem["psum"], 1)
                            wait("psum", t + 1)
                            dve.reciprocal(m1[:], r1[:]).then_inc(sig.sem["recip"], 1)
                            wait("recip", t + 1)
                            dve.tensor_scalar(lr1[:], m1[:, HD:HALVES], lamt[:, 1:2], None, ALU.mult).then_inc(sig.sem["lamrec"], 1)
                            wait("lamrec", t + 1)
                            if t:
                                wait("prod", 2 * DEPTH1 + 4)
                            else:
                                wait("vev", 1)
                            dve.tensor_tensor(d3, s3[:, 0:HD, 0:HD], m1[:, 0:HD].rearrange("p (q a) -> p q a", a=1).to_broadcast([P, HD, HD]),
                                              ALU.mult).then_inc(sig.sem["part1"], 1)
                            dve.tensor_tensor(e3, s3[:, HD:HALVES, HD:HALVES], lr1[:].rearrange("p (q a) -> p q a", a=1).to_broadcast([P, HD, HD]),
                                              ALU.mult).then_inc(sig.sem["part2"], 1)
                            wait("part2", t + 1)
                            dve.tensor_tensor(dif, dif, dif2, ALU.add).then_inc(sig.sem["normed"], 1)
                            wait("normed", t + 1)
                            vv = vt[:, t, :].rearrange("p (h d) -> p h d", h=16)
                            products(wait, False, tile_sums(t, last) - 4, [
                                (lambda b: b.rearrange("p (h a d) -> p h a d", h=4, a=HD),
                                 d3[:, :, 4 * u:4 * u + 4].rearrange("p a (h o) -> p h a o", o=1).to_broadcast([P, 4, HD, 16]),
                                 vv[:, 4 * u:4 * u + 4, :].rearrange("p h (o d) -> p h o d", o=1).to_broadcast([P, 4, HD, 16])) for u in range(4)])
                            if t == 0:
                                ahead(5)
                        flat = ON[:].rearrange("p t c -> p (t c)")
                        wait("outT", TT)
                        prev("aT")
                        clipped = ON2[:].rearrange("p t c -> p (t c)")
                        dve.tensor_scalar(clipped, flat, SQRT_MAX, -SQRT_MAX, ALU.min, ALU.max).then_inc(sig.sem["clip"], 1)
                        wait("clip", 1)
                        dve.scalar_tensor_tensor(out=sq[:].rearrange("p t c -> p (t c)"), in0=clipped, scalar=1.0 / 16, in1=clipped,
                                                 op0=ALU.mult, op1=ALU.mult).then_inc(sig.sem["sq"], 1)
                        wait("sq", 1)
                        dve.tensor_reduce(ssq[:], sq[:].rearrange("p t (h d) -> p (t h) d", d=16), AX.X, ALU.add).then_inc(sig.sem["ssq"], 1)
                        wait("hr", 1)
                        dve.scalar_tensor_tensor(out=ON2[:].rearrange("p t (h d) -> p (t h) d", d=16), in0=ON[:].rearrange("p t (h d) -> p (t h) d", d=16),
                                                 scalar=1.0 - LAM_INIT, in1=hr[:].rearrange("p (h d) -> p h d", d=1).to_broadcast([P, 32, 16]),
                                                 op0=ALU.mult, op1=ALU.mult).then_inc(sig.sem["hn"], 1)
                    if st.kind in ("narrow", "wide", "tokens"):
                        wait("ah", sig.per[s]["ah"])
                        if ret:
                            for t in range(CT):
                                ins = dve.scalar_tensor_tensor(out=aT[1][:, t, :], in0=pa[:, t * S:(t + 1) * S], scalar=projn[:, t:t + 1],
                                                               in1=aT[0][:, t, :].bitcast(F32), op0=ALU.mult, op1=ALU.subtract)
                            ins.then_inc(sig.sem["al"], 1)
                        else:
                            dve.tensor_tensor(aT[1][:].rearrange("p a n -> p (a n)"), pa[:], aT[0][:].bitcast(F32).rearrange("p a n -> p (a n)"),
                                              ALU.subtract).then_inc(sig.sem["al"], 1)
                    if st.name in rowbias:
                        wait("xbias", 1)
                    if st.kind == "ffn1":
                        wait("down", HT // 2)
                        for t, ps in enumerate((pa, pb)):
                            xt = x[:, bass.ds(i, 1), t * C:(t + 1) * C]
                            dve.tensor_tensor(xt, xt, ps[:, 0:C].rearrange("p (a c) -> p a c", a=1), ALU.add).then_inc(sig.sem["xres"], 1)
                    else:
                        wait("y", 1)
                        xt, yv = x[:, bass.ds(i, 1), :], pb[:].rearrange("p (a c) -> p a c", a=1)
                        if ret:
                            ins = dve.scalar_tensor_tensor(out=xt, in0=yv, scalar=qscale[:, 1:2], in1=xt, op0=ALU.mult, op1=ALU.add)
                        else:
                            ins = dve.tensor_tensor(xt, xt, yv, ALU.add)
                        ins.then_inc(sig.sem["xres"], 1)
                    if st.kind == "ffn0":
                        ahead(3)

                pieces = [stats, mean_square, normalise, x_low]
                if st.kind in ("narrow", "wide"):
                    pieces.append(qk_low)
                if st.kind == "tokens":
                    pieces += [qk_low, first_tile]
                sequences(dve, pieces, back)

        @block.tensor
        def _(pe):
            pe.wait_ge(primed, 1)
            pe.wait_ge(first_in, 48)
            pe.wait_ge(ones_done, 3 + ATTN_A0["slots"])
            for s, st in enumerate(STAGES):
                stage_start(pe, s)
                split_done(pe, st.name)
                fp = front_psum(st)
                if s == 1:
                    pe.wait_ge(abs_rows, 4)
                    pe.matmul(pb[:, 0:4], ones[:], absum[:], start=True, stop=True).then_inc(abs_ps, 1)
                    pe.wait_ge(q_scales, 2)
                if st.kind == "wide":
                    pe.wait_ge(had_done, 2)
                if st.name == "ffn1" and s == 5:
                    for t in range(0, HT, 2):
                        if t >= 4:
                            pe.wait_ge(w2_l_done, t // 2 - 1)
                        for u in range(2):
                            for n, q in enumerate(w2_raw):
                                ins = pe.matmul(OT[t // 2 % 2][:, u * C:(u + 1) * C], had[:], q[:, t + u, :], start=n == 0, stop=n == 1)
                        ins.then_inc(had_ps, 1)
                    pe.wait_ge(w2_l_done, HT // 2)
                pre = {"attn_a0": "a0", "attn_b0": "b0", "ret1": "r1", "attn_b1": "b1"}.get(st.name)
                wq, wk, wv, wo = [W[f"{pre}_{n}"] for n in "qkvo"] if pre else [None] * 4

                def turn(src, ps, signal):
                    for c in range(CT):
                        for t in range(TT):
                            ins = pe.transpose(ps[:, c * S + t * P:c * S + t * P + P], src[:, t, c * P:c * P + P], ident[:])
                    ins.then_inc(sig.sem[signal], 1)

                def channels_out(ps, w, signal):
                    for o in range(CT):
                        ins = product(pe, ps[:, o * S:(o + 1) * S], lambda t: [q[:, t, o * P:(o + 1) * P] for q in w],
                                      lambda t: [q[:, t, :] for q in xT], CT)
                    ins.then_inc(sig.sem[signal], 1)

                def tokens_out(ps, act_, w, signal):
                    for o in range(TT):
                        ins = product(pe, ps[:, o * C:(o + 1) * C], lambda t: [q[:, t, o * P:(o + 1) * P] for q in act_],
                                      lambda t: [q[:, t, :] for q in w], CT)
                    ins.then_inc(sig.sem[signal], 1)

                def x_turned(b):
                    wait, prev = in_stage(pe, s, b)
                    wait("xn", TT)
                    if st.kind in ("ffn0", "ffn1"):
                        prev("xl")
                    turn(xn, fp[0], "xT")

                def qk(b):
                    wait, prev = in_stage(pe, s, b)
                    if pre:
                        wait("xl", 1)
                        out_of = (lambda ps, w, signal: tokens_out(ps, xT, w, signal)) if st.kind == "tokens" else channels_out
                        out_of(fp[1], wq, "qp")
                        out_of(fp[2], wk, "kp")

                def v(b):
                    wait, prev = in_stage(pe, s, b)
                    if pre:
                        if st.kind == "tokens":
                            wait("qev", 1)
                        tokens_out(fp[3], xT, wv, "vp")

                def read(b):
                    wait, prev = in_stage(pe, s, b)
                    if st.kind == "narrow":
                        wait("kl", 1)
                    if st.kind == "tokens":
                        wait("vev", 1)

                def sums(wait, ring, dst, width, terms):
                    for n in range(terms):
                        wait("prod", ring + n + 1)
                        for c in range(0, 1024, width):
                            ins = pe.matmul(dst(c), ident[:], prods[n % 4][:, c:c + width],
                                            start=n == 0 and (c == 0 or width == 512), stop=n == terms - 1 and (c == 1024 - width or width == 512))
                        ins.then_inc(sig.sem["summed"], 1)

                def first_scores(b):
                    wait, prev = in_stage(pe, s, b)
                    sums(wait, 0 if is_first(b) else -4, lambda c: SC[0][:, c:c + 512], 512, DEPTH1)

                def back(i, ahead, last):
                    wait, prev = in_stage(pe, s, i)
                    if st.kind == "ffn0":
                        wait("xl", 1)
                        prev("xres")
                        tokens_out(pb, xT, W["f0"], "y")
                        ahead(0)
                    if st.kind == "ffn1":
                        def up(r):
                            if r >= 2:
                                wait("hid", r - 1)
                            for u in range(2):
                                o = 2 * r + u
                                for w, at in ((W["w1"], 0), (W["w3"], 512)):
                                    ins = product(pe, SC[r % 2][:, at + u * S:at + (u + 1) * S],
                                                  lambda t: [q[:, t, o * P:(o + 1) * P] for q in w], lambda t: [q[:, t, :] for q in xT], CT)
                            ins.then_inc(sig.sem["up"], 1)

                        def down(r):
                            wait("hl", r + 1)
                            if r == 0:
                                prev("xres")
                            for u in range(2):
                                for t, ps in enumerate((pa, pb)):
                                    ins = three(pe, ps[:, 0:C], [q[:, u, t * P:(t + 1) * P] for q in hid[r % 2]],
                                                [q[:, 2 * r + u, :] for q in W["w2"]], r == 0 and u == 0, r == HT // 2 - 1 and u == 1)
                            return ins.then_inc(sig.sem["down"], 1)

                        wait("xl", 1)
                        up(0)
                        for r in range(1, HT // 2):
                            up(r)
                            if r == HT // 2 - 1:
                                ahead(0)
                            down(r - 1)
                        down(HT // 2 - 1)
                    if st.kind == "tokens":
                        sums(wait, DEPTH1, lambda c: SC[1][:, c:c + 512], 512, DEPTH1)
                        ahead(0)
                        ahead(1)
                        for t in range(TT):
                            prev("outT")
                            sums(wait, tile_sums(t, last) - 4, lambda c: OT[t][:, 0:C], C, 4)
                            if t == 0:
                                ahead(4)
                                ahead(2)
                        wait("hn", 1)
                        turn(ON2, pa, "aT")
                        wait("al", 1)
                        ahead(3)
                        tokens_out(pb, aT, W["b1_o"], "y")
                    if st.kind in ("narrow", "wide"):
                        wait("kl", sig.per[s]["kl"])
                        wait("vev", 1)
                        if st.kind == "narrow":
                            Qg = stack_q(st)
                            wait("qload", 16 * st.slots)
                            wait("kload", 16 * st.slots)
                            if st.n_max:
                                wait("maxzero", st.slots)
                        nr = st.n_max // 2
                        for r in range(st.n_max):
                            if r >= 2:
                                wait("rowmax", r - 1)
                            t, k = divmod(r, nr)
                            for u in range(4):
                                n = 4 * k + u
                                dst = SC[r % 2][:, u * S:(u + 1) * S]
                                if st.kind == "narrow":
                                    ins = pe.matmul(dst, Qg[:, n % 8, n // 8, t * P:(t + 1) * P], Ks[:, n % 8, :], start=True, stop=True)
                                else:
                                    ins = three(pe, dst, [q[:, n, t * P:(t + 1) * P] for q in QM], [q[:, n // 2, :] for q in KT], True, True)
                            ins.then_inc(sig.sem["scores"], 1)
                        if st.n_max:
                            nh = 4 * nr
                            wait("rowmax", st.n_max)
                            prev("xres")
                            for t in range(TT):
                                ins = pe.transpose(pa[0:nh, t * P:(t + 1) * P], mx[:, t, 0:nh], ident[:])
                            ins.then_inc(sig.sem["maxT"], 1)
                            if st.kind == "narrow":
                                ahead(0)
                                ahead(1)
                                ahead(3)
                                wait("maxrows", 32 * st.slots)
                            else:
                                wait("maxl", 1)

                        def scores_t(r):
                            if r >= 2:
                                wait("probs", r - 1)
                            for kt in range(TT):
                                dst = SC[r % 2][:, kt * 512:(kt + 1) * 512]
                                if st.kind == "narrow":
                                    ins = pe.matmul(dst.rearrange("p (s t) -> p s t", s=2), Ks[:, r, kt * P:(kt + 1) * P],
                                                    Qg[:, r, :, :], start=True, stop=True)
                                else:
                                    for u in range(2):
                                        n, d = 2 * r + u, dst[:, u * S:(u + 1) * S]
                                        three(pe, d, [q[:, r, kt * P:(kt + 1) * P] for q in KT], [q[:, n, :] for q in QM], True, False)
                                        pe.matmul(d, sel[:, n, :], MT[0][:], start=False, stop=False)
                                        ins = pe.matmul(d, sel[:, n, :], MT[1][:], start=False, stop=True)
                            ins.then_inc(sig.sem["scoresT"], 1)

                        def attend(r):
                            wait("probs", r + 1)
                            p = pr[r % 2][:].rearrange("p (k h t) -> p k h t", k=TT, h=2)
                            if st.kind == "wide":
                                for u in range(2):
                                    o = 2 * r + u
                                    if o >= 2:
                                        wait("outT", o - 1)
                                    for kt in range(TT):
                                        ins = pe.matmul(OT[o % 2][0:65, 0:S], Vw[:, kt, o, :], p[:, kt, u, :], start=kt == 0, stop=kt == 1)
                                    ins.then_inc(sig.sem["pv"], 1)
                                return
                            o = r // 2
                            if r % 2 == 0 and o >= 2:
                                wait("outT", o - 1)
                            for kt in range(TT):
                                for u in range(2):
                                    c = 32 * (2 * (r % 2) + u)
                                    head = 2 * r + u
                                    t0 = P * kt if st.name == "ret1" else 0
                                    ins = pe.matmul(OT[o % 2][c:c + 32, t0:S], V[:, kt, head, :], p[:, kt, u, t0:S],
                                                    start=kt == 0, stop=kt == 1, tile_position=(0, c), skip_group_check=True)
                            ins.then_inc(sig.sem["pv"], 1)

                        def to_tokens(o):
                            wait("outT", o + 1)
                            if o >= 2:
                                wait("normed", o - 1)
                            rows = 65 if st.kind == "wide" else P
                            for t in range(TT):
                                ins = pe.transpose((pb, pa)[o % 2][:, t * rows:(t + 1) * rows], OS[0:rows, t * P:(t + 1) * P], ident[0:rows, 0:rows])
                            ins.then_inc(sig.sem["out_tok"], 1)

                        scores_t(0)
                        scores_t(1)
                        if st.kind == "wide":
                            attend(0)
                            ahead(0)
                            to_tokens(0)
                            to_tokens(1)
                            attend(1)
                            ahead(1)
                            ahead(2)
                            to_tokens(2)
                            to_tokens(3)
                        else:
                            for r in range(st.n_exp):
                                attend(r)
                                if r + 2 < st.n_exp:
                                    scores_t(r + 2)
                                if r % 2 == 0 and r >= 2:
                                    if r == 2:
                                        prev("xres")
                                    to_tokens((r - 2) // 2)
                            if not st.n_max:
                                ahead(0)
                            else:
                                ahead(2)
                            to_tokens(st.n_out - 1)
                            if not st.n_max:
                                ahead(1)
                                ahead(2)
                        key = "n2" if st.name == "ret1" else "normed"
                        wait(key, sig.per[s][key])
                        turn(ON, pa, "aT")
                        wait("al", 1)
                        tokens_out(pb, aT, wo, "y")

                sequences(pe, [x_turned, qk, v, read] + ([first_scores] if st.kind == "tokens" else []), back)

_WEIGHTS = {
    "a0_q": "L0_attn_a_Wq", "a0_k": "L0_attn_a_Wk", "a0_v": "L0_attn_a_Wv", "a0_o": "L0_attn_a_Wo",
    "f0": "L0_ffn_weight", "f0_s": "L0_ffn_scale_weight", "f0_b": "L0_ffn_bias",
    "b0_q": "L0_attn_b_Wq", "b0_bq": "L0_attn_b_bq", "b0_k": "L0_attn_b_Wk", "b0_bk": "L0_attn_b_bk",
    "b0_v": "L0_attn_b_Wv", "b0_bv": "L0_attn_b_bv", "b0_o": "L0_attn_b_Wo", "b0_bo": "L0_attn_b_bo",
    "r1_qkvn": "L1_attn_a_qkv_norm_w", "r1_projn": "L1_attn_a_proj_norm_w", "r1_nw": "L1_attn_a_norm_w", "r1_s": "L1_attn_a_s",
    "b1_q": "L1_attn_b_Wq", "b1_k": "L1_attn_b_Wk", "b1_v": "L1_attn_b_Wv", "b1_o": "L1_attn_b_Wo", "b1_bo": "L1_attn_b_bo",
    "lq1": "L1_attn_b_lq1", "lq2": "L1_attn_b_lq2", "lk1": "L1_attn_b_lk1", "lk2": "L1_attn_b_lk2",
    "w1": "L1_ffn_W1", "w2": "L1_ffn_W2", "w3": "L1_ffn_W3",
}

_OUT = (8, 256, 256)


def _layouts(inputs):
    import numpy as np

    a = {k: np.asarray(inputs[v]) for k, v in _WEIGHTS.items()}
    half, d, j = np.meshgrid(np.arange(2), np.arange(16), np.arange(8), indexing="ij")
    qk16 = ((half * 8 + j) * 16 + d).ravel()
    d, half, j = np.meshgrid(np.arange(8), np.arange(2), np.arange(16), indexing="ij")
    qk8 = (j * 16 + 2 * d + half).ravel()
    g, half, d = np.meshgrid(np.arange(8), np.arange(2), np.arange(16), indexing="ij")
    v16 = ((half * 8 + g) * 16 + d).ravel()
    qkv = np.asarray(inputs["L1_attn_a_qkv_w"])
    proj = np.asarray(inputs["L1_attn_a_proj_w"])
    a["a0_q"], a["a0_k"] = a["a0_q"].T[:, qk16], a["a0_k"].T[:, qk16]
    a["a0_v"], a["a0_o"] = a["a0_v"].T[:, v16], a["a0_o"].T[v16]
    a["r1_q"], a["r1_k"], a["r1_v"] = qkv[:256].T[:, qk16], qkv[256:512].T[:, qk16], qkv[512:].T[:, v16]
    a["r1_o"] = proj.T[v16]
    a["r1_nw"], a["r1_projn"] = a["r1_nw"][v16], a["r1_projn"][v16]
    a["b1_q"], a["b1_k"] = a["b1_q"].T[:, qk8], a["b1_k"].T[:, qk8]
    for n in ("b1_v", "b1_o", "f0", "w1", "w2", "w3"):
        a[n] = a[n].T
    for n in ("b0_bq", "b0_bk", "r1_qkvn", "r1_projn"):
        a[n] = a[n].reshape(2, 128).T
    a["hidden"] = np.asarray(inputs["L0_attn_a_hidden_states"])
    a["ident"] = np.eye(128, dtype=np.float32)
    h = np.ones((1, 1), np.float32)
    while h.shape[0] < 128:
        h = np.block([[h, h], [h, -h]])
    a["had"] = h.astype(np.float32)
    t, k = np.arange(256)[None, :], np.arange(128)[:, None]
    a["caus"] = (t >= k).astype(np.float32)
    a["diff"] = np.maximum(t - k, 0).astype(np.float32)
    a["sel"] = np.repeat(np.eye(128, 4, dtype=np.float32), 128, axis=1)
    return {k: np.ascontiguousarray(v) for k, v in a.items()}


def kernel(**inputs):
    import numpy as _np
    import concourse.bacc as _bacc
    from concourse.bass_utils import run_bass_kernel_spmd as _run

    nc = _bacc.Bacc("TRN2", target_bir_lowering=False, num_devices=1)
    arrays, T = {}, {}
    for name, a in _layouts(inputs).items():
        arrays[f"in_{name}"] = a
        T[name] = nc.dram_tensor(f"in_{name}", a.shape, mybir.dt.from_np(a.dtype), kind="ExternalInput").ap()
    out = nc.dram_tensor("out_0_dram", _OUT, F32, kind="ExternalOutput").ap()
    build(nc, T, out)
    r = _run(nc, [arrays], core_ids=[0])
    return r.results[0]["out_0_dram"]
```

```python
from contextlib import ExitStack

import concourse.bass as bass
from concourse import mybir

F32 = mybir.dt.float32
F32R = mybir.dt.float32r
ALU = mybir.AluOpType
ACT = mybir.ActivationFunctionType
AX = mybir.AxisListType

P = 128
B = 8
S = 256
C = 256
CT = C // P
TT = S // P
HID = 1024
HT = HID // P
LN_EPS = 1e-5
F32_EPS = 2.0 ** -23
LAM_INIT = 0.8 - 0.6 * 2.718281828459045 ** (-0.3 * 12)
ROUND_MAGIC = 1.5 * 2.0 ** 23
F32_MAX = 3.4028234663852886e38
SQRT_MAX = 1.8446742e19


HALVES, DEPTH1 = 32, 8
PAIRS = (0, 3)
SCORE_SUMS = DEPTH1 - len(PAIRS)
PRODS = SCORE_SUMS + 4


class Stage:

    def __init__(self, name, kind, slots=0, rows=0, groups=0, depth=0, n_max=0, n_exp=0, n_out=0, scale=1.0):
        self.name, self.kind = name, kind
        self.slots, self.rows, self.groups, self.depth = slots, rows, groups, depth
        self.n_max, self.n_exp, self.n_out, self.scale = n_max, n_exp, n_out, scale


ATTN_A0 = dict(slots=2, rows=64, groups=8, depth=16, n_max=8, n_exp=8, n_out=4, scale=0.25)
RET1 = dict(slots=2, rows=64, groups=8, depth=16, n_max=0, n_exp=8, n_out=4)
ATTN_B0 = dict(n_max=2, n_exp=2, n_out=4, scale=0.5)
STAGES = [
    Stage("attn_a0", "narrow", **ATTN_A0),
    Stage("ffn0", "ffn0"),
    Stage("attn_b0", "wide", **ATTN_B0),
    Stage("ffn0", "ffn0"),
    Stage("ret1", "narrow", **RET1),
    Stage("ffn1", "ffn1"),
    Stage("attn_b1", "tokens", scale=8.0 ** -0.5),
    Stage("ffn1", "ffn1"),
]


def increments(st):
    n = dict(stats=TT, meanvar=TT, vareps=1, rstd=1, xn=TT, xT=1, xh=1, xl=1, y=1, xres=1)
    if st.name == "ret1":
        n.update(rstd_sq=1, ms2=1, ms2e=1, r2=1, rr=1, xh=CT)
    if st.name in ("ffn0", "attn_b0", "attn_b1"):
        n.update(xbias=1)
    if st.kind == "ffn1":
        n.update(y=0, up=HT // 2, silu=HT // 2, hid=HT // 2, hh=HT // 2, hl=HT // 2, down=HT // 2, xres=TT)
    if st.kind in ("narrow", "wide"):
        n.update(qp=1, kp=1, vp=1, qh=1, ql=1, kh=1, kl=1, vev=1)
        n.update(scoresT=st.n_exp, probs=st.n_exp, pv=st.n_exp, outT=st.n_out, out_tok=st.n_out,
                 normed=st.n_out, aT=1, ah=1, al=1)
        if st.n_max:
            n.update(scores=st.n_max, rowmax=st.n_max, maxT=1, maxh=1, maxl=1, recip=st.n_out)
    if st.kind == "wide":
        n.update(qh=4, ql=4, kh=CT, kl=CT, pv=4)
    if st.kind == "narrow":
        n.update(qstore=48, kstore=48, qload=16 * st.slots, kload=16 * st.slots)
        if st.n_max:
            n.update(maxrows=32 * st.slots, maxzero=st.slots)
    if st.kind == "tokens":
        n.update(qp=1, kp=1, vp=1, qev=1, kev=1, vev=1, halves=TT * 2 * len(PAIRS), prod=TT * PRODS,
                 summed=TT * PRODS, clamped=TT, smax=TT, less=TT, probs=TT, psum=TT, recip=TT, lamrec=TT, part1=TT, part2=TT, normed=TT, outT=TT,
                 clip=1, sq=1, ssq=1, ssqe=1, hpow=1, inrange=1, hr=1, hn=1, aT=1, ah=1, al=1)
    if st.name == "ret1":
        n.update(n1=1, n2=1, sq1=1, sq2=1, e1=1, e2=1, rn1=1, rn2=1)
        n.update(ah=CT)
    if st is STAGES[-1]:
        n.update(stored=16)
    return n


class Signals:

    def __init__(self, ctx, nc):
        self.per = [increments(st) for st in STAGES]
        names = list(dict.fromkeys(k for n in self.per for k in n))
        self.sem = {k: ctx.enter_context(nc.semaphore(f"s_{k}")) for k in names}
        self.base, total = [], {k: 1 for k in names}
        for n in self.per:
            self.base.append(dict(total))
            for k, v in n.items():
                total[k] += B * v
        self.total = total


def build(nc, T, out):
    ctx = ExitStack()
    with ctx:
        def sb(name, shape, dt=F32):
            return ctx.enter_context(nc.sbuf_tensor(name, shape, dt))

        def sem(name):
            return ctx.enter_context(nc.semaphore(name))

        sig = Signals(ctx, nc)

        x = sb("x", [P, B, TT * C])
        ident = sb("ident", [P, P])
        caus = sb("caus", [P, S])
        diff = sb("diff", [P, S])
        negs = sb("negs", [P, 16])
        half_pow = sb("half_pow", [P, 32])
        with nc.sbuf_tensor("below", [P, 1024], F32), nc.sbuf_tensor("w2_staged", [P, 2, HT, C], F32R) as w2_staged:
            w2_raw = (w2_staged[:, 0], w2_staged[:, 1])
        scratch = sb("scratch", [P, 5120])
        tmpw = scratch[:, 3072:5120]
        W = {}
        for n, cols in dict(a0_q=C, a0_k=C, a0_v=C, a0_o=C, f0=C, b0_q=C, b0_k=C, b0_v=C, b0_o=C, w1=HID, w3=HID).items():
            W[n] = (sb(f"{n}_h", [P, CT, cols], F32R), sb(f"{n}_l", [P, CT, cols], F32R))
        with nc.sbuf_tensor("mask", [P, 16, S], F32) as mask:
            pass
        w2_tile = sb("w2", [P, 2, HT, C], F32R)
        W["w2"] = (w2_tile[:, 0], w2_tile[:, 1])
        for n in "qkvo":
            W[f"b1_{n}"] = W[f"a0_{n}"]
            W[f"r1_{n}"] = (sb(f"r1_{n}_w", [P, CT, C], F32R),)
        had = sb("had", [P, P], F32R)
        sel = sb("sel", [P, 4, P], F32R)
        had_raw = sb("had_raw", [P, P])
        bq, bk = sb("bq", [P, CT]), sb("bk", [P, CT])
        bv, bo0, bo1, bf = sb("bv", [P, C]), sb("bo0", [P, C]), sb("bo1", [P, C]), sb("bf", [P, C])
        rowbias = {"ffn0": bf, "attn_b0": bo0, "attn_b1": bo1}
        qkvn, projn, nwb = sb("qkvn", [P, CT]), sb("projn", [P, CT]), sb("nwb", [P, C])
        lamv = sb("lamv", [P, 4, 8])
        lamt = sb("lamt", [P, 8])
        lamp = sb("lamp", [P, 2, 8])
        absum = sb("absum", [P, 4])
        qscale = sb("qscale", [P, 4])
        ones = sb("ones", [P, P])

        bn_parts = sb("bst", [P, TT, 6])
        mean_var = sb("mv", [P, TT, 2])
        var_eps, rstd = sb("ve", [P, TT]), sb("rstd", [P, TT])
        ms2, ms2e, r2, rr = sb("ms2", [P, TT]), sb("ms2e", [P, TT]), sb("r2", [P, TT]), sb("rr", [P, TT])
        xn = sb("xn", [P, TT, C])
        xT = (sb("xT_h", [P, CT, S], F32R), sb("xT_l", [P, CT, S], F32R))
        QT = (sb("QT_h", [P, CT, S], F32R), sb("QT_l", [P, CT, S], F32R))
        KT = (sb("KT_h", [P, CT, S], F32R), sb("KT_l", [P, CT, S], F32R))
        V = sb("V", [P, TT, 16, 32])
        Vw = sb("Vw", [P, TT, 4, 65])
        Qs = sb("Qs", [P, 8 * 2 * S], F32R)
        Ks = sb("Ks", [P, 8, S], F32R)
        mx = sb("mx", [P, TT, 32])
        MT = (sb("MT_h", [P, S], F32R), sb("MT_l", [P, S], F32R))
        prob_bufs = [sb(f"pr{i}", [P, TT * 512]) for i in range(2)]
        OS = sb("OS", [P, S])
        qt, kt_, vt = (scratch[:, 2048 + n * 512:2560 + n * 512].rearrange("p (t c) -> p t c", t=TT) for n in range(3))
        prods = [prob_bufs[0][:], prob_bufs[1][:], scratch[:, 0:1024], scratch[:, 1024:2048]]
        tok_scores = scratch[:, 3584:4608]
        tok_weights, tok_weights2 = scratch[:, 4608:4864], scratch[:, 4864:5120]
        tok_max, weight_sum, lam_recip = sb("m1", [P, HALVES]), sb("r1", [P, HALVES]), sb("lr1", [P, HALVES // 2])
        rec = sb("rec", [P, TT, 4])
        silu_first = sb("silu_first", [P, 1])
        ON = sb("ON", [P, TT, C])
        ON2 = sb("ON2", [P, TT, C])
        sq = sb("sq", [P, TT, C])
        sel_raw = sq[:].rearrange("p t c -> p (t c)")
        swb = ON2[:, 0, :]
        ssq, ssqe, hr = sb("ssq", [P, 32]), sb("ssqe", [P, 32]), sb("hr", [P, 32])
        aT = (sb("aT_h", [P, CT, S], F32R), sb("aT_l", [P, CT, S], F32R))
        silu_gate, hidden_f = (q[:].rearrange("p t c -> p (t c)") for q in (ON, ON2))
        hid = [tuple(Qs[:, 512 * n:512 * n + 512].rearrange("p (a t) -> p a t", a=2) for n in (2 * k, 2 * k + 1))
               for k in range(2)]
        r2t, hr0 = sb("r2t", [P, TT]), sb("hr0", [P, 32])
        absw = tmpw.rearrange("p (j n) -> p j n", j=4)

        q_dram = nc.dram_tensor("q_stack", [2, 3, P, S], F32, kind="Internal").ap()
        k_dram = nc.dram_tensor("k_stack", [2, 3, P, S], F32, kind="Internal").ap()

        SC = [ctx.enter_context(nc.psum_tensor(f"SC{i}", [P, 1024], F32)) for i in range(2)]
        OT = [ctx.enter_context(nc.psum_tensor(f"OT{i}", [P, 512], F32)) for i in range(2)]
        pa = ctx.enter_context(nc.psum_tensor("pa", [P, 512], F32))
        pb = ctx.enter_context(nc.psum_tensor("pb", [P, 512], F32))

        x0_in, x_in, first_in, const_in = sem("x0_in"), sem("x_in"), sem("first_in"), sem("const_in")
        a0_in, a0_high, a0_low = sem("a0_in"), sem("a0_high"), sem("a0_low")
        negs_done, ones_done, zeroed, had_done = sem("negs_done"), sem("ones_done"), sem("zeroed"), sem("had_done")
        primed = sem("primed")
        passed = sem("passed")
        raw_first, raw_in = ([sem(f"{q}{n}") for n in range(3)] for q in ("raw_first", "raw_in"))
        w_split, w_step = sem("w_split"), sem("w_step")
        had_ps, w2_h_done, w2_l_done = sem("had_ps"), sem("w2_h_done"), sem("w2_l_done")
        dve_setup, act_setup, abs_ps, q_scales = sem("dve_setup"), sem("act_setup"), sem("abs_ps"), sem("q_scales")
        abs_in, abs_rows, abs_sum = sem("abs_in"), sem("abs_rows"), sem("abs_sum")
        mask_exp, mask_done, stack_clear = sem("mask_exp"), sem("mask_done"), sem("stack_clear")

        ORDER = ["f0", "b0_q", "b0_k", "b0_v", "b0_o", "w1", "w3", "r1_q", "r1_k", "r1_v", "r1_o",
                 "b1_q", "b1_k", "b1_v", "b1_o", "w2"]
        LARGE = ("w1", "w3", "w2")
        NEEDS = {"ffn0": "f0", "attn_b0": "b0_o", "ret1": "r1_o", "ffn1": "w2", "attn_b1": "b1_o"}

        def raw_part(n):
            return 2 if n in LARGE else [m for m in ORDER if m not in LARGE].index(n) % 2

        def raw_view(n):
            at, size = ((0, 512), (512, 512), (1024, 2048))[raw_part(n)]
            return scratch[:, at:at + size].rearrange("p (t n) -> p t n", t=HT if n == "w2" else CT)

        def load_raw(eng, n, arrived):
            eng.dma_start(raw_view(n), T[n].rearrange("(t p) n -> p t n", p=P)).then_inc(arrived[raw_part(n)], 16)

        A0 = ("a0_q", "a0_k", "a0_v", "a0_o")
        a0_raw = {n: prob_bufs[k // 2][:, k % 2 * 512:k % 2 * 512 + 512].rearrange("p (t n) -> p t n", t=CT) for k, n in enumerate(A0)}

        def split_done(eng, name):
            if name == "attn_a0":
                eng.wait_ge(a0_low, len(A0))
                return
            eng.wait_ge(w_split, ORDER.index(NEEDS[name]) + 1)

        quarter = [SC[n // 2][:, n % 2 * 512:n % 2 * 512 + 512] for n in range(4)]

        def front_psum(st):
            if st.name == "attn_a0":
                return [pb[:], OT[0][:], OT[1][:], quarter[3]]
            if st.name == "ret1":
                return [quarter[n] for n in (2, 3, 2, 3)]
            if st.kind in ("narrow", "wide"):
                return quarter
            return [q[:] for q in ((pa, pb, pa, OT[0]) if st.kind == "tokens" else (OT[0],))]

        def sequences(eng, pieces, back, parts=(), between=None):
            for piece in pieces:
                piece(0)
            cuts = [0, *parts, B - 1]
            for n in range(len(cuts) - 1):
                with eng.Fori(cuts[n], cuts[n + 1]) as i:
                    back(i, lambda k: pieces[k](i + 1))
                if between and n < len(parts):
                    between(n)
            back(B - 1, lambda k: None)

        def is_first(b):
            return isinstance(b, int) and b == 0

        def in_stage(eng, s, i):
            per, base = sig.per[s], sig.base[s]

            apart = eng.engine in (mybir.EngineType.Pool, mybir.EngineType.SP)

            def wait(name, k, alone=apart):
                eng.wait_ge(sig.sem[name], i * per[name] + (base[name] + k))
                if alone:
                    eng.sem_inc(passed, 1)

            def prev(name, alone=apart):
                if name in per:
                    eng.wait_ge(sig.sem[name], i * per[name] + base[name])
                    if alone:
                        eng.sem_inc(passed, 1)
            return wait, prev

        def stage_start(eng, s):
            if s:
                eng.wait_ge(sig.sem["xres"], sig.base[s]["xres"])

        def three(pe, out_ap, left, right, first, last):
            terms = [(a, b) for a in range(len(left)) for b in range(len(right)) if a + b < 2]
            for n, (a, b) in enumerate(terms):
                ins = pe.matmul(out_ap, left[a], right[b], start=first and n == 0, stop=last and n == len(terms) - 1)
            return ins

        def product(pe, out_ap, left, right, tiles):
            for t in range(tiles):
                ins = three(pe, out_ap, left(t), right(t), t == 0, t == tiles - 1)
            return ins

        QM = tuple(Qs[:, n * 4 * S:(n + 1) * 4 * S].rearrange("p (h t) -> p h t", h=4) for n in range(2))

        EARLY = 2

        def stack_q(st):
            return Qs[:, 0:st.groups * st.slots * S].rearrange("p (g s t) -> p g s t", g=st.groups, s=st.slots)

        def cleared(s):
            return 1 + sum(t.kind in ("narrow", "wide") for t in STAGES[:s])

        def made(kind, t):
            return SCORE_SUMS * (t + 1) if kind == "scores" else TT * SCORE_SUMS + 4 * (t + 1)

        n_const = 16 * (3 + 4 + 6 + 4)
        block = ctx.enter_context(nc.Block())

        @block.sync
        def _(sp):
            for b in range(B):
                sp.dma_start(x[:, b, :].rearrange("p (t c) -> p t c", t=TT),
                             T["hidden"][b].rearrange("(t p) c -> p t c", p=P)).then_inc(x_in if b else x0_in, 16)
                if b == 0:
                    for n in A0:
                        sp.dma_start(a0_raw[n], T[n].rearrange("(t p) n -> p t n", p=P)).then_inc(a0_in, 16)
                    for dst, src in ((ident[:], T["ident"]), (negs[:], T["r1_s"].rearrange("(a n) -> a n", a=1).to_broadcast([P, 16])),
                                     (diff[:], T["diff"])):
                        sp.dma_start(dst, src).then_inc(first_in, 16)
            for dst, src in ((caus[:], T["caus"]), (had_raw[:], T["had"]), (sel_raw, T["sel"])):
                sp.dma_start(dst, src).then_inc(const_in, 16)
            for dst, n in ((bq, "b0_bq"), (bk, "b0_bk"), (qkvn, "r1_qkvn"), (projn, "r1_projn")):
                sp.dma_start(dst[:], T[n]).then_inc(const_in, 16)
            for dst, n in ((bv[:], "b0_bv"), (bo0[:], "b0_bo"), (bo1[:], "b1_bo"), (bf[:], "f0_b"), (swb, "f0_s"), (nwb[:], "r1_nw")):
                sp.dma_start(dst, T[n].rearrange("(a n) -> a n", a=1).to_broadcast([P, C])).then_inc(const_in, 16)
            for j, n in enumerate(("lq1", "lk1", "lq2", "lk2")):
                sp.dma_start(lamv[:, j, :], T[n].rearrange("(a n) -> a n", a=1).to_broadcast([P, 8])).then_inc(const_in, 16)
            for n in ("f0", "b0_q", "w1"):
                load_raw(sp, n, raw_first)
            for j, n in enumerate(("r1_q", "r1_k", "r1_v", "r1_o")):
                sp.dma_start(absw[:, j, :].rearrange("p (t n) -> p t n", t=CT), T[n].rearrange("(t p) n -> p t n", p=P)).then_inc(abs_in, 16)

            sp.wait_ge(primed, 1)
            for s, st in enumerate(STAGES):
                if st.kind == "narrow":
                    stage_start(sp, s)
                    sp.wait_ge(stack_clear, cleared(s))
                    D, Qg = st.depth, stack_q(st)

                    def stores(b):
                        wait, prev = in_stage(sp, s, b)
                        for parts, dram, low, store, load in ((QT, q_dram, "ql", "qstore", "qload"), (KT, k_dram, "kl", "kstore", "kload")):
                            wait(low, 1)
                            prev(load)
                            for t in range(3):
                                part = (0, 0, 1)[t] if dram is q_dram else (0, 1, 0)[t]
                                sp.dma_start(dram[:, t, :, :].rearrange("h p t -> p h t"),
                                             parts[part][:].bitcast(F32)).then_inc(sig.sem[store], 16)

                    def loads(b):
                        wait, prev = in_stage(sp, s, b)
                        prev("scoresT")
                        for slot in range(st.slots):
                            r0 = st.rows * slot + 2
                            if slot == 0:
                                wait("qstore", 48)
                            sp.dma_start(Qg[r0:r0 + 3 * D, :, slot, :].bitcast(F32),
                                         q_dram[slot].rearrange("t (d j) n -> (t d) j n", j=P // D)).then_inc(sig.sem["qload"], 16)
                            if slot == 0:
                                wait("kstore", 48)
                            sp.dma_start(Ks[r0:r0 + 3 * D, :, :].bitcast(F32),
                                         k_dram[slot].rearrange("t (d j) n -> (t d) j n", j=P // D)).then_inc(sig.sem["kload"], 16)

                    def back(i, ahead):
                        wait, prev = in_stage(sp, s, i)
                        if st.n_max:
                            wait("maxl", 1)
                            wait("scores", st.n_max)
                            for slot in range(st.slots):
                                for part in range(2):
                                    r = st.rows * slot + part
                                    sp.dma_start(Qg[r:r + 1, :, slot, :].bitcast(F32),
                                                 MT[part][8 * slot:8 * slot + 8, :].bitcast(F32)).then_inc(sig.sem["maxrows"], 16)
                        ahead(0)
                        ahead(1)

                    sequences(sp, [stores, loads], back)
                if s == len(STAGES) - 1:
                    with sp.Fori(0, B) as i:
                        wait, prev = in_stage(sp, s, i)
                        wait("xres", sig.per[s]["xres"])
                        sp.dma_start(out[bass.ds(i, 1)].rearrange("a (t p) c -> p (a t) c", p=P),
                                     x[:, bass.ds(i, 1), :].rearrange("p a (t c) -> p (a t) c", t=TT)).then_inc(sig.sem["stored"], 16)
                    sp.wait_ge(sig.sem["stored"], sig.total["stored"])

        @block.gpsimd
        def _(pool):
            steps = 0

            def step(ins):
                nonlocal steps
                steps += 1
                ins.then_inc(w_step, 1)
                pool.wait_ge(w_step, steps)

            step(pool.memset(half_pow[:], -0.5))

            def clear_stack():
                step(pool.memset(Qs[:].bitcast(F32), 0.0))
                pool.sem_inc(stack_clear, 1)

            def prepare(names):
                for n in names:
                    v = raw_view(n)
                    same = [m for m in ORDER if raw_part(m) == raw_part(n)]
                    if n == same[0]:
                        pool.wait_ge(raw_first[raw_part(n)], 16)
                    else:
                        pool.wait_ge(raw_in[raw_part(n)], 16 * same.index(n))
                    h = W[n][0]
                    low = len(W[n]) > 1 and W[n][1]
                    if n == "f0":
                        pool.wait_ge(const_in, n_const)
                        for t in range(CT):
                            step(pool.tensor_tensor(v[:, t, :], v[:, t, :], swb, ALU.mult))
                    if n.startswith("r1"):
                        a = qscale[:, 3:4] if n == "r1_o" else qscale[:, 2:3]
                        pool.wait_ge(q_scales, 2)
                        step(pool.tensor_scalar(v, v, a, 1.0, ALU.mult, ALU.min))
                        step(pool.tensor_scalar(v, v, -1.0, ROUND_MAGIC, ALU.max, ALU.add))
                        step(pool.tensor_scalar(v, v, -ROUND_MAGIC, None, ALU.add))
                    if n == "w2":
                        v = tmpw.rearrange("p (t n) -> p t n", t=HT)
                        h, low = w2_raw
                        step(pool.tensor_scalar(v, v, float(HID) ** -0.5, None, ALU.mult))
                    step(pool.tensor_copy(h[:], v))
                    if low:
                        step(pool.tensor_tensor(low[:], v, h[:].bitcast(F32), ALU.subtract))
                    pool.sem_inc(w_split, 1)
                    if n != same[-1]:
                        load_raw(pool, same[same.index(n) + 1], raw_in)

            def butterflies():
                pool.wait_ge(raw_in[raw_part("w2")], 16 * 2)
                src, dst = raw_view("w2"), tmpw.rearrange("p (t n) -> p t n", t=HT)
                for stride in (1, 2, 4):
                    sv = src.rearrange("p (a two b) n -> p a two (b n)", two=2, b=stride)
                    dv = dst.rearrange("p (a two b) n -> p a two (b n)", two=2, b=stride)
                    step(pool.tensor_tensor(dv[:, :, 0, :], sv[:, :, 0, :], sv[:, :, 1, :], ALU.add))
                    step(pool.tensor_tensor(dv[:, :, 1, :], sv[:, :, 0, :], sv[:, :, 1, :], ALU.subtract))
                    src, dst = dst, src

            def cut_mask():
                for h in range(16):
                    pool.wait_ge(mask_exp, h + 1)
                    step(pool.tensor_tensor(mask[:, h, :], mask[:, h, :], caus[:], ALU.mult))
                pool.sem_inc(mask_done, 1)

            def clear_wide():
                for q in (QM[0], QM[1], MT[0][:], MT[1][:]):
                    step(pool.memset(q.bitcast(F32), 0.0))
                pool.sem_inc(stack_clear, 1)

            jobs = {0: [lambda: prepare(ORDER[0:3]), lambda: prepare(ORDER[3:5]), cut_mask, lambda: prepare(ORDER[5:6]),
                        lambda: prepare(ORDER[6:7])],
                    1: [clear_wide],
                    2: [lambda: prepare(ORDER[7:9]), lambda: prepare(ORDER[9:11]), lambda: prepare(ORDER[11:15]),
                        butterflies, lambda: prepare(ORDER[15:])],
                    3: [clear_stack]}

            clear_stack()
            step(pool.memset(Ks[:].bitcast(F32), 0.0))
            for slot in range(ATTN_A0["slots"]):
                r = ATTN_A0["rows"] * slot
                step(pool.memset(Ks[r:r + 2, :, :].bitcast(F32), 1.0))
                pool.sem_inc(ones_done, 1)
            pool.wait_ge(first_in, 48)
            pool.tensor_scalar(negs[:], negs[:], -1.0, None, ALU.mult).then_inc(negs_done, 1)
            pool.wait_ge(primed, 1)
            for s, st in enumerate(STAGES):
                stage_start(pool, s)

                def rstd_of(b):
                    wait, prev = in_stage(pool, s, b)
                    wait("meanvar", TT)
                    pool.tensor_scalar(var_eps[:], mean_var[:, :, 1], LN_EPS, None, ALU.add).then_inc(sig.sem["vareps"], 1)
                    wait("vareps", 1)
                    pool.tensor_tensor(rstd[:], var_eps[:], half_pow[:, 0:TT], ALU.pow).then_inc(sig.sem["rstd"], 1)
                    if st.name == "ret1":
                        wait("ms2", 1)
                        pool.tensor_scalar(ms2e[:], ms2[:], F32_EPS, None, ALU.add).then_inc(sig.sem["ms2e"], 1)
                        wait("ms2e", 1)
                        pool.tensor_tensor(r2[:], ms2e[:], half_pow[:, 0:TT], ALU.pow).then_inc(sig.sem["r2"], 1)
                    if st.name in rowbias:
                        wait("xn", TT)
                        xv = x[:, bass.ds(b, 1), :].rearrange("p a (t c) -> p (a t) c", t=TT)
                        bb = rowbias[st.name][:].rearrange("p (a c) -> p a c", a=1).to_broadcast([P, TT, C])
                        pool.tensor_tensor(xv, xv, bb, ALU.add).then_inc(sig.sem["xbias"], 1)

                def back(i, ahead):
                    wait, prev = in_stage(pool, s, i)
                    if st.kind == "narrow" and st.n_max:
                        prev("scoresT")
                        Qg = stack_q(st)
                        for slot in range(st.slots):
                            r = st.rows * slot
                            pool.memset(Qg[r:r + 2, :, slot, :].bitcast(F32), 0.0).then_inc(sig.sem["maxzero"], 1)
                            wait("maxzero", slot + 1)
                    ahead(0)
                    if st.name == "attn_b1":
                        wait("outT", TT)
                        prev("aT")
                        flat, clipped = (q[:].rearrange("p t c -> p (t c)") for q in (ON, ON2))
                        pool.tensor_scalar(clipped, flat, SQRT_MAX, -SQRT_MAX, ALU.min, ALU.max).then_inc(sig.sem["clip"], 1)
                        wait("ssq", 1)
                        pool.tensor_scalar(ssqe[:], ssq[:], 1e-5, None, ALU.add).then_inc(sig.sem["ssqe"], 1)
                        wait("ssqe", 1)
                        pool.tensor_tensor(hr0[:], ssqe[:], half_pow[:], ALU.pow).then_inc(sig.sem["hpow"], 1)
                        wait("hpow", 1)
                        pool.tensor_scalar(ssqe[:], ssq[:], F32_MAX / 16, 1.0 - LAM_INIT, ALU.is_lt, ALU.mult).then_inc(sig.sem["inrange"], 1)
                        wait("inrange", 1)
                        pool.tensor_tensor(hr[:], hr0[:], ssqe[:], ALU.mult).then_inc(sig.sem["hr"], 1)
                        wait("hr", 1)
                        wait("sq", 1)
                        heads = [q[:].rearrange("p t (h d) -> p (t h) d", d=16) for q in (ON, ON2)]
                        pool.tensor_tensor(heads[1], heads[0], hr[:].rearrange("p (h d) -> p h d", d=1).to_broadcast([P, 32, 16]),
                                           ALU.mult).then_inc(sig.sem["hn"], 1)
                    if st.name == "ret1":
                        for q, e, r, eps in (("sq1", "e1", "rn1", 1e-6), ("sq2", "e2", "rn2", F32_EPS)):
                            wait(q, 1)
                            pool.tensor_scalar(ssqe[:, 0:TT], ssq[:, 0:TT], 1.0 / C, eps, ALU.mult, ALU.add).then_inc(sig.sem[e], 1)
                            wait(e, 1)
                            pool.tensor_tensor(hr[:, 0:TT], ssqe[:, 0:TT], half_pow[:, 0:TT], ALU.pow).then_inc(sig.sem[r], 1)

                todo = jobs.get(s, [])
                sequences(pool, [rstd_of], back, range(1, len(todo) + 1), lambda n: todo[n]())

        def evac_out(act, st, wait, prev, o):
            rows = 65 if st.kind == "wide" else P
            wait("pv", o + 1 if st.kind == "wide" else 2 * o + 2)
            if o:
                wait("out_tok", o)
            else:
                prev("out_tok")
            act.activation(OS[0:rows, :], OT[o % 2][0:rows, 0:S], ACT.Copy).then_inc(sig.sem["outT"], 1)

        @block.scalar
        def _(act):
            for signal in sig.sem.values():
                act.sem_inc(signal, 1)
            act.sem_inc(primed, 1)
            act.wait_ge(a0_in, 16 * len(A0))
            for n in A0:
                act.activation(W[n][0][:], a0_raw[n], ACT.Copy).then_inc(a0_high, 1)
            act.wait_ge(negs_done, 1)
            for h in range(16):
                act.activation(mask[:, h, :], diff[:], ACT.Exp, scale=negs[:, h:h + 1]).then_inc(mask_exp, 1)
            for s, st in enumerate(STAGES):
                stage_start(act, s)
                if s == 1:
                    act.wait_ge(dve_setup, 2)
                    act.activation(lamp[:, :, 2:3], lamp[:, :, 0:1], ACT.Exp).then_inc(act_setup, 1)
                if st.kind == "ffn1" and s == 5:
                    for t in range(0, HT, 2):
                        act.wait_ge(had_ps, t // 2 + 1)
                        act.activation(W["w2"][0][:, t:t + 2, :].rearrange("p a n -> p (a n)"), OT[t // 2 % 2][:], ACT.Copy)\
                           .then_inc(w2_h_done, 1)
                if st.kind == "wide":
                    act.wait_ge(stack_clear, cleared(s))
                if st.kind == "ffn1":
                    act.activation(silu_first[:], ident[:, 0:1], ACT.Silu)
                fp = front_psum(st)
                ret = st.name == "ret1"

                def x_high(b):
                    wait, prev = in_stage(act, s, b)
                    wait("xT", 1)
                    prev({"ffn0": "y", "ffn1": "up"}.get(st.kind, "vp"))
                    if ret:
                        for t in range(CT):
                            act.activation(xT[0][:, t, :], fp[0][:, t * S:(t + 1) * S], ACT.Copy, scale=qkvn[:, t:t + 1])\
                               .then_inc(sig.sem["xh"], 1)
                    else:
                        act.activation(xT[0][:].rearrange("p a n -> p (a n)"), fp[0], ACT.Copy).then_inc(sig.sem["xh"], 1)

                def qk_high(b):
                    wait, prev = in_stage(act, s, b)
                    if st.kind == "tokens":
                        for dst, p, ps, done in ((qt, "qp", fp[1], "qev"), (kt_, "kp", fp[2], "kev")):
                            wait(p, 1)
                            if not is_first(b):
                                wait("prod", made("scores", 1) - TT * PRODS)
                            act.activation(dst.rearrange("p t c -> p (t c)"), ps, ACT.Copy).then_inc(sig.sem[done], 1)
                        return
                    if st.kind in ("ffn0", "ffn1"):
                        return
                    for parts, p, ps, h, bias, free in ((QT, "qp", fp[1], "qh", bq, "qstore"), (KT, "kp", fp[2], "kh", bk, "kstore")):
                        wait(p, 1)
                        if st.kind == "narrow":
                            prev(free)
                            act.activation(parts[0][:].rearrange("p a n -> p (a n)"), ps, ACT.Copy, scale=qscale[:, 0:1] if ret else 1.0)\
                               .then_inc(sig.sem[h], 1)
                            continue
                        prev("scoresT")
                        if parts is QT:
                            for n in range(4):
                                t, r0 = n // 2, 64 * (n % 2)
                                act.activation(QM[0][r0:r0 + 64, n, :], ps[r0:r0 + 64, t * S:(t + 1) * S], ACT.Identity,
                                               bias=bias[r0:r0 + 64, t:t + 1]).then_inc(sig.sem[h], 1)
                        else:
                            for t in range(CT):
                                act.activation(parts[0][:, t, :], ps[:, t * S:(t + 1) * S], ACT.Identity, bias=bias[:, t:t + 1])\
                                   .then_inc(sig.sem[h], 1)

                def v_out(b):
                    wait, prev = in_stage(act, s, b)
                    if st.kind == "tokens":
                        wait("vp", 1)
                        prev("prod")
                        act.activation(vt.rearrange("p t c -> p (t c)"), fp[3], ACT.Copy).then_inc(sig.sem["vev"], 1)
                    if st.kind == "narrow":
                        wait("vp", 1)
                        prev("pv")
                        act.activation(V[:, :, :, 0:16], fp[3].rearrange("p (t h d) -> p t h d", t=TT, h=16), ACT.Copy,
                                       scale=qscale[:, 0:1] if ret else 1.0).then_inc(sig.sem["vev"], 1)

                def token_probs(wait, t):
                    wait("less", t + 1)
                    act.activation(tok_scores, tok_scores, ACT.Exp, scale=st.scale).then_inc(sig.sem["probs"], 1)

                def first_probs(b):
                    token_probs(in_stage(act, s, b)[0], 0)

                def back(i, ahead):
                    wait, prev = in_stage(act, s, i)
                    if st.kind == "ffn0":
                        ahead(0)
                    if st.kind == "ffn1":
                        for r in range(HT // 2):
                            wait("up", r + 1)
                            if r:
                                wait("hid", r)
                            else:
                                prev("hid")
                            act.activation(silu_gate[:], SC[r % 2][:, 0:512], ACT.Silu).then_inc(sig.sem["silu"], 1)
                            if r == HT // 2 - 1:
                                ahead(0)
                            wait("hid", r + 1)
                            if r >= 2:
                                wait("down", r - 1)
                            else:
                                prev("down")
                            act.activation(hid[r % 2][0][:].rearrange("p a n -> p (a n)"), hidden_f[:], ACT.Copy).then_inc(sig.sem["hh"], 1)
                    if st.kind == "tokens":
                        prev("hn")
                        token_probs(wait, 1)
                        for t in range(TT):
                            if t:
                                ahead(0)
                                ahead(1)
                            wait("summed", made("values", t))
                            act.activation(ON[:, t, :], OT[t][:, 0:C], ACT.Copy).then_inc(sig.sem["outT"], 1)
                        wait("clip", 1)
                        act.activation(sq[:].rearrange("p t c -> p (t c)"), ON2[:].rearrange("p t c -> p (t c)"), ACT.Square,
                                       scale=1.0 / 4).then_inc(sig.sem["sq"], 1)
                        ahead(3)
                    if st.kind in ("narrow", "wide"):
                        if st.n_max:
                            nh = 4 if st.kind == "wide" else st.groups * st.slots
                            if st.kind == "narrow":
                                ahead(0)
                            wait("maxT", 1)
                            prev("maxrows" if st.kind == "narrow" else "scoresT")
                            act.activation(MT[0][0:nh, :], pa[0:nh, 0:S], ACT.Copy, scale=-1.0).then_inc(sig.sem["maxh"], 1)
                            if st.kind == "narrow":
                                ahead(1)
                        for r in range(st.n_exp):
                            if st.n_max:
                                wait("scoresT", r + 1)
                                if r >= 2:
                                    wait("pv", (r - 1) * (2 if st.kind == "wide" else 1))
                                else:
                                    prev("pv")
                                act.activation(prob_bufs[r % 2][:], SC[r % 2][:], ACT.Exp, scale=st.scale).then_inc(sig.sem["probs"], 1)
                            if st.kind == "narrow" and r % 2 == 0 and r >= 2:
                                if ret and r == 4:
                                    ahead(0)
                                evac_out(act, st, wait, prev, (r - 2) // 2)
                                if ret and r == 4:
                                    ahead(1)
                        if st.kind == "wide":
                            ahead(0)
                            for o in range(4):
                                evac_out(act, st, wait, prev, o)
                                if o == 1:
                                    ahead(1)
                        else:
                            evac_out(act, st, wait, prev, st.n_out - 1)
                            ahead(2)
                    if st.kind in ("narrow", "wide", "tokens"):
                        wait("aT", 1)
                        prev("y")
                        if ret:
                            for t in range(CT):
                                act.activation(aT[0][:, t, :], pa[:, t * S:(t + 1) * S], ACT.Copy, scale=projn[:, t:t + 1])\
                                   .then_inc(sig.sem["ah"], 1)
                        else:
                            act.activation(aT[0][:].rearrange("p a n -> p (a n)"), pa[:], ACT.Copy).then_inc(sig.sem["ah"], 1)
                    if st.kind == "tokens":
                        ahead(2)

                sequences(act, [x_high, qk_high, v_out] + ([first_probs] if st.kind == "tokens" else []), back)

        @block.vector
        def _(dve):
            dve.memset(ones[:], 1.0).then_inc(ones_done, 1)
            dve.memset(V[:], 0.0).then_inc(zeroed, 1)
            dve.memset(Vw[:, :, :, 64:65], 1.0).then_inc(ones_done, 1)
            dve.wait_ge(zeroed, 1)
            dve.memset(V[:, :, :, 16:17], 1.0).then_inc(ones_done, 1)
            dve.wait_ge(primed, 1)
            for s, st in enumerate(STAGES):
                stage_start(dve, s)
                fp = front_psum(st)
                ret = st.name == "ret1"
                if s == 1:
                    dve.wait_ge(const_in, n_const)
                    dve.tensor_copy(had[:], had_raw[:]).then_inc(had_done, 1)
                    dve.tensor_copy(sel[:].rearrange("a b c -> a (b c)"), sel_raw).then_inc(had_done, 1)
                    dve.wait_ge(had_done, 2)
                    lprod = sq[:, 0, 0:16].rearrange("p (a b) -> p a b", a=2)
                    dve.tensor_tensor(lprod, lamv[:, 0:4:2, :], lamv[:, 1:4:2, :], ALU.mult).then_inc(dve_setup, 1)
                    dve.wait_ge(dve_setup, 1)
                    dve.tensor_reduce(lamp[:, :, 0:1], lprod, AX.X, ALU.add).then_inc(dve_setup, 1)
                    dve.wait_ge(abs_in, 64)
                    for j, n in enumerate(("q", "k", "v", "o")):
                        dve.tensor_reduce(absum[:, j:j + 1], absw[:, j, :], AX.X, ALU.add, apply_absolute_value=True).then_inc(abs_rows, 1)
                    dve.wait_ge(act_setup, 1)
                    dve.tensor_tensor(lamt[:, 0:1], lamp[:, 1, 2:3], lamp[:, 0, 2:3], ALU.subtract).then_inc(dve_setup, 1)
                    dve.wait_ge(dve_setup, 3)
                    dve.tensor_scalar(lamt[:, 1:2], lamt[:, 0:1], -LAM_INIT, None, ALU.add).then_inc(dve_setup, 1)
                    dve.wait_ge(abs_ps, 1)
                    dve.tensor_reduce(qscale[:, 0:1], pb[:, 0:3], AX.X, ALU.add).then_inc(abs_sum, 1)
                    dve.tensor_copy(qscale[:, 1:2], pb[:, 3:4]).then_inc(abs_sum, 1)
                    dve.wait_ge(abs_sum, 2)
                    dve.tensor_scalar(qscale[:, 0:1], qscale[:, 0:1], 1.0 / (3 * C * C), 1e-5, ALU.mult, ALU.max).then_inc(abs_sum, 1)
                    dve.tensor_scalar(qscale[:, 1:2], qscale[:, 1:2], 1.0 / (C * C), 1e-5, ALU.mult, ALU.max).then_inc(abs_sum, 1)
                    dve.wait_ge(abs_sum, 4)
                    dve.reciprocal(qscale[:, 2:4], qscale[:, 0:2]).then_inc(q_scales, 2)
                if ret:
                    dve.wait_ge(mask_done, 1)
                if st.name == "ffn1" and s == 5:
                    for t in range(0, HT, 2):
                        dve.wait_ge(w2_h_done, t // 2 + 1)
                        dve.tensor_tensor(W["w2"][1][:, t:t + 2, :].rearrange("p a n -> p (a n)"), OT[t // 2 % 2][:],
                                          W["w2"][0][:, t:t + 2, :].rearrange("p a n -> p (a n)").bitcast(F32), ALU.subtract)\
                           .then_inc(w2_l_done, 1)

                def low_a0():
                    for k, n in enumerate(A0):
                        dve.wait_ge(a0_high, k + 1)
                        dve.tensor_tensor(W[n][1][:], a0_raw[n], W[n][0][:].bitcast(F32), ALU.subtract).then_inc(a0_low, 1)

                def stats(b):
                    wait, prev = in_stage(dve, s, b)
                    if s == 0:
                        dve.wait_ge(x0_in, 16) if is_first(b) else dve.wait_ge(x_in, 16 * (B - 1))
                    for t in range(TT):
                        dve.bn_stats(bn_parts[:, t, :], x[:, bass.ds(b, 1), t * C:(t + 1) * C]).then_inc(sig.sem["stats"], 1)
                    wait("stats", TT, alone=True)
                    for t in range(TT):
                        dve.bn_aggr(mean_var[:, t, :], bn_parts[:, t, :]).then_inc(sig.sem["meanvar"], 1)
                    if s == 0 and is_first(b):
                        low_a0()

                def mean_square(b):
                    wait, prev = in_stage(dve, s, b)
                    if ret:
                        wait("rstd", 1)
                        dve.tensor_tensor(r2t[:], rstd[:], rstd[:], ALU.mult).then_inc(sig.sem["rstd_sq"], 1)
                        wait("rstd_sq", 1)
                        dve.tensor_tensor(ms2[:], r2t[:], mean_var[:, :, 1], ALU.mult).then_inc(sig.sem["ms2"], 1)

                def normalise(b):
                    wait, prev = in_stage(dve, s, b)
                    wait("rstd", 1)
                    scale_of = rstd
                    if ret:
                        wait("r2", 1)
                        dve.tensor_tensor(rr[:], r2[:], rstd[:], ALU.mult).then_inc(sig.sem["rr"], 1)
                        wait("rr", 1)
                        scale_of = rr
                    prev("xT")
                    for t in range(TT):
                        dve.tensor_scalar(xn[:, t, :], x[:, bass.ds(b, 1), t * C:(t + 1) * C], mean_var[:, t, 0:1], scale_of[:, t:t + 1],
                                          ALU.subtract, ALU.mult).then_inc(sig.sem["xn"], 1)

                def x_low(b):
                    wait, prev = in_stage(dve, s, b)
                    wait("xh", sig.per[s]["xh"])
                    if ret:
                        for t in range(CT):
                            ins = dve.scalar_tensor_tensor(out=xT[1][:, t, :], in0=fp[0][:, t * S:(t + 1) * S], scalar=qkvn[:, t:t + 1],
                                                           in1=xT[0][:, t, :].bitcast(F32), op0=ALU.mult, op1=ALU.subtract)
                        ins.then_inc(sig.sem["xl"], 1)
                    else:
                        dve.tensor_tensor(xT[1][:].rearrange("p a n -> p (a n)"), fp[0], xT[0][:].bitcast(F32).rearrange("p a n -> p (a n)"),
                                          ALU.subtract).then_inc(sig.sem["xl"], 1)

                def qk_low(b):
                    wait, prev = in_stage(dve, s, b)
                    if st.kind == "tokens":
                        return
                    for parts, ps, h, l, bias in ((QT, fp[1], "qh", "ql", bq), (KT, fp[2], "kh", "kl", bk)):
                        wait(h, sig.per[s][h])
                        if st.kind == "wide" and parts is QT:
                            for n in range(4):
                                t, r0 = n // 2, 64 * (n % 2)
                                dve.scalar_tensor_tensor(out=QM[1][r0:r0 + 64, n, :], in0=ps[r0:r0 + 64, t * S:(t + 1) * S],
                                                         scalar=bias[r0:r0 + 64, t:t + 1], in1=QM[0][r0:r0 + 64, n, :].bitcast(F32),
                                                         op0=ALU.add, op1=ALU.subtract).then_inc(sig.sem[l], 1)
                        elif st.kind == "wide":
                            for t in range(CT):
                                dve.scalar_tensor_tensor(out=parts[1][:, t, :], in0=ps[:, t * S:(t + 1) * S], scalar=bias[:, t:t + 1],
                                                         in1=parts[0][:, t, :].bitcast(F32), op0=ALU.add, op1=ALU.subtract)\
                                   .then_inc(sig.sem[l], 1)
                        else:
                            flat = [q[:].rearrange("p a n -> p (a n)") for q in parts]
                            a = qscale[:, 0:1] if ret else 1.0
                            dve.scalar_tensor_tensor(out=flat[1], in0=ps, scalar=a, in1=flat[0].bitcast(F32),
                                                     op0=ALU.mult, op1=ALU.subtract).then_inc(sig.sem[l], 1)

                def v_wide(b):
                    wait, prev = in_stage(dve, s, b)
                    if st.kind == "wide":
                        wait("vp", 1)
                        prev("pv")
                        for t in range(TT):
                            ins = dve.tensor_tensor(Vw[:, t, :, 0:64], fp[3][:, t * C:(t + 1) * C].rearrange("p (h d) -> p h d", h=4),
                                                    bv[:].rearrange("p (h d) -> p h d", h=4), ALU.add)
                        ins.then_inc(sig.sem["vev"], 1)

                s3 = tok_scores.rearrange("p (q k) -> p q k", q=HALVES)
                HD = HALVES // 2
                d3, e3 = (q.rearrange("p (a h) -> p a h", a=HD) for q in (tok_weights, tok_weights2))

                def buffer(b, kind, t, u):
                    n = made(kind, t) - (4 if kind == "values" else SCORE_SUMS) + u
                    if not is_first(b) or n >= 4:
                        in_stage(dve, s, b)[0]("summed", n - 3)
                    return prods[n % 4]

                def score_products(b, t):
                    wait, prev = in_stage(dve, s, b)
                    qv, kv = (q[:, t, :].rearrange("p (d q) -> p d q", d=DEPTH1) for q in (qt, kt_))

                    def product_of(dst, d):
                        return dve.tensor_tensor(dst.rearrange("p (q k) -> p q k", q=HALVES),
                                                 qv[:, d, :].rearrange("p (q a) -> p q a", a=1).to_broadcast([P, HALVES, HALVES]),
                                                 kv[:, d, :].rearrange("p (a k) -> p a k", a=1).to_broadcast([P, HALVES, HALVES]), ALU.mult)
                    d = pairs = 0
                    for u in range(SCORE_SUMS):
                        dst = buffer(b, "scores", t, u)
                        if d in PAIRS:
                            product_of(dst, d).then_inc(sig.sem["halves"], 1)
                            if pairs or t:
                                wait("prod", made("scores", t) - SCORE_SUMS + u)
                            product_of(tok_scores, d + 1).then_inc(sig.sem["halves"], 1)
                            pairs += 1
                            wait("halves", 2 * (len(PAIRS) * t + pairs))
                            dve.tensor_tensor(dst, dst, tok_scores, ALU.add).then_inc(sig.sem["prod"], 1)
                            d += 2
                        else:
                            product_of(dst, d).then_inc(sig.sem["prod"], 1)
                            d += 1

                def value_products(b, t):
                    vv = vt[:, t, :].rearrange("p (h d) -> p h d", h=16)
                    for u in range(4):
                        dst = buffer(b, "values", t, u)
                        dve.tensor_tensor(dst.rearrange("p (h a d) -> p h a d", h=4, a=HD),
                                          d3[:, :, 4 * u:4 * u + 4].rearrange("p a (h o) -> p h a o", o=1).to_broadcast([P, 4, HD, 16]),
                                          vv[:, 4 * u:4 * u + 4, :].rearrange("p h (o d) -> p h o d", o=1).to_broadcast([P, 4, HD, 16]),
                                          ALU.mult).then_inc(sig.sem["prod"], 1)

                def token_softmax(b, t, between):
                    wait, prev = in_stage(dve, s, b)
                    if t:
                        wait("part2", t)
                    else:
                        wait("prod", made("scores", 1))
                    wait("summed", made("scores", t))
                    dve.tensor_scalar(tok_scores, SC[t][:], F32_MAX, -F32_MAX, ALU.min, ALU.max).then_inc(sig.sem["clamped"], 1)
                    wait("clamped", t + 1)
                    dve.tensor_reduce(tok_max[:], s3, AX.X, ALU.max).then_inc(sig.sem["smax"], 1)
                    wait("smax", t + 1)
                    dve.tensor_tensor(s3, s3, tok_max[:].rearrange("p (q a) -> p q a", a=1).to_broadcast([P, HALVES, HALVES]),
                                      ALU.subtract).then_inc(sig.sem["less"], 1)
                    wait("probs", t + 1)
                    dve.tensor_reduce(weight_sum[:], s3, AX.X, ALU.add).then_inc(sig.sem["psum"], 1)
                    between()
                    wait("psum", t + 1)
                    dve.reciprocal(tok_max[:], weight_sum[:]).then_inc(sig.sem["recip"], 1)
                    wait("recip", t + 1)
                    dve.tensor_scalar(lam_recip[:], tok_max[:, HD:HALVES], lamt[:, 1:2], None, ALU.mult).then_inc(sig.sem["lamrec"], 1)
                    wait("lamrec", t + 1)
                    if t:
                        wait("prod", made("values", 0))
                    elif not is_first(b):
                        wait("prod", made("values", 1) - TT * PRODS)
                    dve.tensor_tensor(d3, s3[:, 0:HD, 0:HD], tok_max[:, 0:HD].rearrange("p (q a) -> p q a", a=1).to_broadcast([P, HD, HD]),
                                      ALU.mult).then_inc(sig.sem["part1"], 1)
                    dve.tensor_tensor(e3, s3[:, HD:HALVES, HD:HALVES], lam_recip[:].rearrange("p (q a) -> p q a", a=1).to_broadcast([P, HD, HD]),
                                      ALU.mult).then_inc(sig.sem["part2"], 1)
                    wait("part2", t + 1)
                    dve.tensor_tensor(tok_weights, tok_weights, tok_weights2, ALU.add).then_inc(sig.sem["normed"], 1)
                    wait("normed", t + 1)

                def first_tile(b):
                    in_stage(dve, s, b)[0]("kev", 1)
                    score_products(b, 0)

                def second_tile(b):
                    score_products(b, 1)

                def first_softmax(b):
                    token_softmax(b, 0, lambda: None)

                def masked(b, r):
                    wait, prev = in_stage(dve, s, b)
                    wait("scoresT", r + 1)
                    if r >= 2:
                        wait("pv", r - 1)
                    else:
                        prev("pv")
                    heads = mask[:, r:16:8, :]
                    pv_, sv = (q[:].rearrange("p (k h t) -> p k h t", k=2, h=2) for q in (prob_bufs[r % 2], SC[r % 2]))
                    dve.tensor_tensor(pv_[:, 0], sv[:, 0], heads, ALU.mult)
                    dve.tensor_tensor(pv_[:, 1, :, P:S], sv[:, 1, :, P:S], heads[:, :, 0:P], ALU.mult).then_inc(sig.sem["probs"], 1)

                def maximum(b, r):
                    wait, prev = in_stage(dve, s, b)
                    if r == 0:
                        prev("maxT")
                    wait("scores", r + 1)
                    t, k = divmod(r, st.n_max // 2)
                    dve.tensor_reduce(mx[:, t, 4 * k:4 * k + 4], SC[r % 2][:].rearrange("p (h k) -> p h k", h=4), AX.X, ALU.max)\
                       .then_inc(sig.sem["rowmax"], 1)

                def early(b):
                    for r in range(EARLY):
                        if ret:
                            masked(b, r)
                        else:
                            maximum(b, r)

                def heads_out(wait, prev, o):
                    wait("out_tok", o + 1)
                    ps = (pb, pa)[o % 2]
                    if o == 0:
                        prev("aT")
                    elif st.n_max:
                        wait("normed", o)
                    if st.kind == "wide":
                        pv_ = ps[:, 0:TT * 65].rearrange("p (t c) -> p t c", t=TT)
                        dve.reciprocal(rec[:, :, 0:1], pv_[:, :, 64:65]).then_inc(sig.sem["recip"], 1)
                        wait("recip", o + 1)
                        for t in range(TT):
                            ins = dve.tensor_scalar(ON[:, t, 64 * o:64 * o + 64], pv_[:, t, 0:64], rec[:, t, 0:1], None, ALU.mult)
                        ins.then_inc(sig.sem["normed"], 1)
                        return
                    pv_ = ps[:, 0:TT * P].rearrange("p (t h d) -> p t h d", t=TT, h=4)
                    if ret:
                        for t in range(TT):
                            ins = dve.tensor_scalar(ON[:, t, 64 * o:64 * o + 64].rearrange("p (h d) -> p h d", h=4),
                                                    pv_[:, t, :, 0:16], 0.25, None, ALU.mult)
                        ins.then_inc(sig.sem["normed"], 1)
                        return
                    dve.reciprocal(rec[:], pv_[:, :, :, 16]).then_inc(sig.sem["recip"], 1)
                    wait("recip", o + 1)
                    for t in range(TT):
                        ins = dve.tensor_tensor(ON[:, t, 64 * o:64 * o + 64].rearrange("p (h d) -> p h d", h=4), pv_[:, t, :, 0:16],
                                                rec[:, t, :].rearrange("p (h d) -> p h d", d=1).to_broadcast([P, 4, 16]), ALU.mult)
                    ins.then_inc(sig.sem["normed"], 1)

                def back(i, ahead):
                    wait, prev = in_stage(dve, s, i)
                    if st.kind == "ffn0":
                        ahead(0)
                        ahead(2)
                    if st.kind == "ffn1":
                        for r in range(HT // 2):
                            wait("silu", r + 1)
                            if r:
                                wait("hl", r)
                            else:
                                prev("hl")
                            dve.tensor_tensor(hidden_f[:], SC[r % 2][:, 512:1024], silu_gate[:], ALU.mult).then_inc(sig.sem["hid"], 1)
                            if r == HT // 2 - 1:
                                ahead(3)
                            wait("hh", r + 1)
                            dve.tensor_tensor(hid[r % 2][1][:].rearrange("p a n -> p (a n)"), hidden_f[:],
                                              hid[r % 2][0][:].bitcast(F32).rearrange("p a n -> p (a n)"), ALU.subtract).then_inc(sig.sem["hl"], 1)
                            if r == 0:
                                ahead(0)
                            if r == 1:
                                ahead(2)
                    if st.kind in ("narrow", "wide"):
                        for r in range(EARLY, st.n_max):
                            maximum(i, r)
                            if r == 2:
                                ahead(0)
                            if r == 4:
                                ahead(2)
                            if r == 6:
                                ahead(3)
                        if st.kind == "wide":
                            ahead(0)
                        if st.n_max:
                            nh = 2 * st.n_max
                            wait("maxh", 1)
                            dve.scalar_tensor_tensor(out=MT[1][0:nh, :], in0=pa[0:nh, 0:S], scalar=-1.0, in1=MT[0][0:nh, :].bitcast(F32),
                                                     op0=ALU.mult, op1=ALU.subtract).then_inc(sig.sem["maxl"], 1)
                        if st.kind == "wide":
                            ahead(2)
                            ahead(3)
                        if st.name == "attn_a0":
                            ahead(4)
                        for o in range(st.n_out):
                            if ret and o == 0:
                                ahead(0)
                                masked(i, 2)
                                ahead(1)
                                masked(i, 3)
                            if ret and o == 1:
                                ahead(2)
                                masked(i, 4)
                                ahead(3)
                            if ret and o == 2:
                                ahead(4)
                                for r in (5, 6, 7):
                                    masked(i, r)
                            if st.kind == "wide" and o == 2:
                                ahead(4)
                            heads_out(wait, prev, o)
                        ahead(5)
                        if ret:
                            wait("normed", st.n_out)
                            for src, dst, q, r, n in ((ON, ON2, "sq1", "rn1", "n1"), (ON2, ON, "sq2", "rn2", "n2")):
                                for t in range(TT):
                                    ins = dve.tensor_tensor_reduce(out=sq[:, t, :], in0=src[:, t, :], in1=src[:, t, :], scale=1.0, scalar=0.0,
                                                                   op0=ALU.mult, op1=ALU.add, accum_out=ssq[:, t:t + 1])
                                ins.then_inc(sig.sem[q], 1)
                                wait(r, 1)
                                for t in range(TT):
                                    if q == "sq1":
                                        ins = dve.scalar_tensor_tensor(out=dst[:, t, :], in0=src[:, t, :], scalar=hr[:, t:t + 1], in1=nwb[:],
                                                                       op0=ALU.mult, op1=ALU.mult)
                                    else:
                                        ins = dve.tensor_scalar(dst[:, t, :], src[:, t, :], hr[:, t:t + 1], None, ALU.mult)
                                ins.then_inc(sig.sem[n], 1)
                                wait(n, 1)
                    if st.kind == "tokens":
                        ahead(0)
                        wait("vev", 1)
                        value_products(i, 0)
                        ahead(2)
                        token_softmax(i, 1, lambda: ahead(3))
                        value_products(i, 1)
                        ahead(5)
                        wait("sq", 1)
                        dve.tensor_reduce(ssq[:], sq[:].rearrange("p t (h d) -> p (t h) d", d=16), AX.X, ALU.add).then_inc(sig.sem["ssq"], 1)
                        ahead(6)
                        ahead(7)
                    if st.kind in ("narrow", "wide", "tokens"):
                        wait("ah", sig.per[s]["ah"])
                        if ret:
                            for t in range(CT):
                                ins = dve.scalar_tensor_tensor(out=aT[1][:, t, :], in0=pa[:, t * S:(t + 1) * S], scalar=projn[:, t:t + 1],
                                                               in1=aT[0][:, t, :].bitcast(F32), op0=ALU.mult, op1=ALU.subtract)
                            ins.then_inc(sig.sem["al"], 1)
                        else:
                            dve.tensor_tensor(aT[1][:].rearrange("p a n -> p (a n)"), pa[:], aT[0][:].bitcast(F32).rearrange("p a n -> p (a n)"),
                                              ALU.subtract).then_inc(sig.sem["al"], 1)
                    if st.kind in ("narrow", "wide"):
                        ahead(6)
                    if st.name in rowbias:
                        wait("xbias", 1)
                    if st.kind == "ffn1":
                        wait("down", HT // 2)
                        for t, ps in enumerate((pa, pb)):
                            xt = x[:, bass.ds(i, 1), t * C:(t + 1) * C]
                            dve.tensor_tensor(xt, xt, ps[:, 0:C].rearrange("p (a c) -> p a c", a=1), ALU.add).then_inc(sig.sem["xres"], 1)
                    else:
                        wait("y", 1)
                        xt, yv = x[:, bass.ds(i, 1), :], pb[:].rearrange("p (a c) -> p a c", a=1)
                        if ret:
                            ins = dve.scalar_tensor_tensor(out=xt, in0=yv, scalar=qscale[:, 1:2], in1=xt, op0=ALU.mult, op1=ALU.add)
                        else:
                            ins = dve.tensor_tensor(xt, xt, yv, ALU.add)
                        ins.then_inc(sig.sem["xres"], 1)
                    if st.kind == "ffn0":
                        ahead(3)

                pieces = [stats, mean_square, normalise, x_low]
                if st.kind in ("narrow", "wide"):
                    pieces += [qk_low, v_wide, early]
                if st.kind == "tokens":
                    pieces += [qk_low, first_tile, second_tile, first_softmax]
                sequences(dve, pieces, back)

        @block.tensor
        def _(pe):
            pe.wait_ge(primed, 1)
            pe.wait_ge(first_in, 48)
            pe.wait_ge(ones_done, 3 + ATTN_A0["slots"])
            for s, st in enumerate(STAGES):
                stage_start(pe, s)
                split_done(pe, st.name)
                fp = front_psum(st)
                if s == 1:
                    pe.wait_ge(abs_rows, 4)
                    pe.matmul(pb[:, 0:4], ones[:], absum[:], start=True, stop=True).then_inc(abs_ps, 1)
                    pe.wait_ge(q_scales, 2)
                if st.kind == "wide":
                    pe.wait_ge(had_done, 2)
                if st.name == "ffn1" and s == 5:
                    for t in range(0, HT, 2):
                        if t >= 4:
                            pe.wait_ge(w2_l_done, t // 2 - 1)
                        for u in range(2):
                            for n, q in enumerate(w2_raw):
                                ins = pe.matmul(OT[t // 2 % 2][:, u * C:(u + 1) * C], had[:], q[:, t + u, :], start=n == 0, stop=n == 1)
                        ins.then_inc(had_ps, 1)
                    pe.wait_ge(w2_l_done, HT // 2)
                pre = {"attn_a0": "a0", "attn_b0": "b0", "ret1": "r1", "attn_b1": "b1"}.get(st.name)
                wq, wk, wv, wo = [W[f"{pre}_{n}"] for n in "qkvo"] if pre else [None] * 4

                if st.kind == "narrow":
                    Qg = stack_q(st)

                def turn(src, ps, signal):
                    for c in range(CT):
                        for t in range(TT):
                            ins = pe.transpose(ps[:, c * S + t * P:c * S + t * P + P], src[:, t, c * P:c * P + P], ident[:])
                    ins.then_inc(sig.sem[signal], 1)

                def channels_out(ps, w, signal):
                    for o in range(CT):
                        ins = product(pe, ps[:, o * S:(o + 1) * S], lambda t: [q[:, t, o * P:(o + 1) * P] for q in w],
                                      lambda t: [q[:, t, :] for q in xT], CT)
                    ins.then_inc(sig.sem[signal], 1)

                def tokens_out(ps, act_, w, signal):
                    for o in range(TT):
                        ins = product(pe, ps[:, o * C:(o + 1) * C], lambda t: [q[:, t, o * P:(o + 1) * P] for q in act_],
                                      lambda t: [q[:, t, :] for q in w], CT)
                    ins.then_inc(sig.sem[signal], 1)

                def x_turned(b):
                    wait, prev = in_stage(pe, s, b)
                    wait("xn", TT)
                    if st.kind in ("ffn0", "ffn1"):
                        prev("xl")
                    turn(xn, fp[0], "xT")

                def qk(b):
                    wait, prev = in_stage(pe, s, b)
                    if pre:
                        wait("xl", 1)
                        out_of = (lambda ps, w, signal: tokens_out(ps, xT, w, signal)) if st.kind == "tokens" else channels_out
                        out_of(fp[1], wq, "qp")
                        out_of(fp[2], wk, "kp")

                def v(b):
                    wait, prev = in_stage(pe, s, b)
                    if pre:
                        if st.name == "ret1":
                            wait("kl", 1)
                        tokens_out(fp[3], xT, wv, "vp")

                def read(b):
                    wait, prev = in_stage(pe, s, b)
                    if st.kind == "narrow":
                        wait("kl", 1)
                def sums(b, kind, t):
                    wait, prev = in_stage(pe, s, b)
                    terms, width, ps = (SCORE_SUMS, 512, SC[t]) if kind == "scores" else (4, C, OT[t])
                    for n in range(terms):
                        m = made(kind, t) - terms + n
                        wait("prod", m + 1)
                        for c in range(0, 1024, width):
                            dst = ps[:, c:c + width] if kind == "scores" else ps[:, 0:C]
                            ins = pe.matmul(dst, ident[:], prods[m % 4][:, c:c + width],
                                            start=n == 0 and (c == 0 or kind == "scores"),
                                            stop=n == terms - 1 and (c == 1024 - width or kind == "scores"))
                        ins.then_inc(sig.sem["summed"], 1)

                def scores(b, r):
                    wait, prev = in_stage(pe, s, b)
                    if r >= 2:
                        wait("rowmax", r - 1)
                    t, k = divmod(r, st.n_max // 2)
                    for u in range(4):
                        n = 4 * k + u
                        dst = SC[r % 2][:, u * S:(u + 1) * S]
                        if st.kind == "narrow":
                            ins = pe.matmul(dst, Qg[:, n % 8, n // 8, t * P:(t + 1) * P], Ks[:, n % 8, :], start=True, stop=True)
                        else:
                            ins = three(pe, dst, [q[:, n, t * P:(t + 1) * P] for q in QM], [q[:, n // 2, :] for q in KT], True, True)
                    ins.then_inc(sig.sem["scores"], 1)

                def scores_t(b, r):
                    wait, prev = in_stage(pe, s, b)
                    if r >= 2:
                        wait("probs", r - 1)
                    for kt in range(TT):
                        dst = SC[r % 2][:, kt * 512:(kt + 1) * 512]
                        if st.kind == "narrow":
                            ins = pe.matmul(dst.rearrange("p (s t) -> p s t", s=2), Ks[:, r, kt * P:(kt + 1) * P],
                                            Qg[:, r, :, :], start=True, stop=True)
                        else:
                            for u in range(2):
                                n, d = 2 * r + u, dst[:, u * S:(u + 1) * S]
                                three(pe, d, [q[:, r, kt * P:(kt + 1) * P] for q in KT], [q[:, n, :] for q in QM], True, False)
                                pe.matmul(d, sel[:, n, :], MT[0][:], start=False, stop=False)
                                ins = pe.matmul(d, sel[:, n, :], MT[1][:], start=False, stop=True)
                    ins.then_inc(sig.sem["scoresT"], 1)

                def early(b):
                    wait, prev = in_stage(pe, s, b)
                    if st.kind not in ("narrow", "wide"):
                        return
                    wait("kl", sig.per[s]["kl"])
                    wait("vev", 1)
                    if st.kind == "narrow":
                        wait("qload", 16 * st.slots)
                        wait("kload", 16 * st.slots)
                        if st.n_max:
                            wait("maxzero", st.slots)
                    for r in range(EARLY):
                        (scores_t if st.name == "ret1" else scores)(b, r)

                def back(i, ahead):
                    wait, prev = in_stage(pe, s, i)
                    if st.kind == "ffn0":
                        wait("xl", 1)
                        prev("xres")
                        tokens_out(pb, xT, W["f0"], "y")
                        ahead(0)
                    if st.kind == "ffn1":
                        def up(r):
                            if r >= 2:
                                wait("hid", r - 1)
                            for u in range(2):
                                o = 2 * r + u
                                for w, at in ((W["w1"], 0), (W["w3"], 512)):
                                    ins = product(pe, SC[r % 2][:, at + u * S:at + (u + 1) * S],
                                                  lambda t: [q[:, t, o * P:(o + 1) * P] for q in w], lambda t: [q[:, t, :] for q in xT], CT)
                            ins.then_inc(sig.sem["up"], 1)

                        def down(r):
                            wait("hl", r + 1)
                            if r == 0:
                                prev("xres")
                            for u in range(2):
                                for t, ps in enumerate((pa, pb)):
                                    ins = three(pe, ps[:, 0:C], [q[:, u, t * P:(t + 1) * P] for q in hid[r % 2]],
                                                [q[:, 2 * r + u, :] for q in W["w2"]], r == 0 and u == 0, r == HT // 2 - 1 and u == 1)
                            return ins.then_inc(sig.sem["down"], 1)

                        wait("xl", 1)
                        up(0)
                        for r in range(1, HT // 2):
                            up(r)
                            if r == HT // 2 - 1:
                                ahead(0)
                            down(r - 1)
                        down(HT // 2 - 1)
                    if st.kind == "tokens":
                        prev("outT")
                        sums(i, "values", 0)
                        ahead(0)
                        ahead(1)
                        sums(i, "values", 1)
                        ahead(4)
                        ahead(5)
                        wait("hn", 1)
                        turn(ON2, pa, "aT")
                        ahead(2)
                        wait("al", 1)
                        tokens_out(pb, aT, W["b1_o"], "y")
                    if st.kind in ("narrow", "wide"):
                        for r in range(EARLY, st.n_max):
                            scores(i, r)
                            if r == 5:
                                prev("xres")
                                ahead(0)
                        if st.n_max:
                            nh = 2 * st.n_max
                            wait("rowmax", st.n_max)
                            prev("xres")
                            for t in range(TT):
                                ins = pe.transpose(pa[0:nh, t * P:(t + 1) * P], mx[:, t, 0:nh], ident[:])
                            ins.then_inc(sig.sem["maxT"], 1)
                            if st.kind == "narrow":
                                ahead(1)
                                wait("maxrows", 32 * st.slots)
                            else:
                                wait("maxl", 1)

                        def attend(r):
                            wait("probs", r + 1)
                            p = prob_bufs[r % 2][:].rearrange("p (k h t) -> p k h t", k=TT, h=2)
                            if st.kind == "wide":
                                for u in range(2):
                                    o = 2 * r + u
                                    if o >= 2:
                                        wait("outT", o - 1)
                                    for kt in range(TT):
                                        ins = pe.matmul(OT[o % 2][0:65, 0:S], Vw[:, kt, o, :], p[:, kt, u, :], start=kt == 0, stop=kt == 1)
                                    ins.then_inc(sig.sem["pv"], 1)
                                return
                            o = r // 2
                            if r % 2 == 0 and o >= 2:
                                wait("outT", o - 1)
                            for kt in range(TT):
                                for u in range(2):
                                    c = 32 * (2 * (r % 2) + u)
                                    head = 2 * r + u
                                    t0 = P * kt if st.name == "ret1" else 0
                                    ins = pe.matmul(OT[o % 2][c:c + 32, t0:S], V[:, kt, head, :], p[:, kt, u, t0:S],
                                                    start=kt == 0, stop=kt == 1, tile_position=(0, c), skip_group_check=True)
                            ins.then_inc(sig.sem["pv"], 1)

                        def to_tokens(o):
                            wait("outT", o + 1)
                            if o >= 2:
                                wait("normed", o - 1)
                            rows = 65 if st.kind == "wide" else P
                            for t in range(TT):
                                ins = pe.transpose((pb, pa)[o % 2][:, t * rows:(t + 1) * rows], OS[0:rows, t * P:(t + 1) * P], ident[0:rows, 0:rows])
                            ins.then_inc(sig.sem["out_tok"], 1)

                        if st.n_max:
                            scores_t(i, 0)
                            scores_t(i, 1)
                        if st.name == "attn_a0":
                            ahead(3)
                        if st.kind == "wide":
                            attend(0)
                            ahead(0)
                            to_tokens(0)
                            wait("probs", 2)
                            ahead(1)
                            to_tokens(1)
                            attend(1)
                            ahead(2)
                            to_tokens(2)
                            to_tokens(3)
                        else:
                            for r in range(st.n_exp):
                                attend(r)
                                if not st.n_max and r == 3:
                                    ahead(0)
                                elif not st.n_max and r == 4:
                                    ahead(1)
                                    to_tokens(1)
                                    ahead(3)
                                    scores_t(i, 5)
                                    scores_t(i, 6)
                                elif r + 2 < st.n_exp:
                                    scores_t(i, r + 2)
                                if r % 2 == 0 and r >= 2 and (st.n_max or r != 4):
                                    if r == 2:
                                        prev("xres")
                                    to_tokens((r - 2) // 2)
                            ahead(2)
                            to_tokens(st.n_out - 1)
                        key = "n2" if st.name == "ret1" else "normed"
                        wait(key, sig.per[s][key])
                        turn(ON, pa, "aT")
                        ahead(4)
                        wait("al", 1)
                        tokens_out(pb, aT, wo, "y")

                pieces = [x_turned, qk, v, read]
                if st.kind in ("narrow", "wide"):
                    pieces += [early]
                if st.kind == "tokens":
                    pieces += [lambda b: sums(b, "scores", 0), lambda b: sums(b, "scores", 1)]
                sequences(pe, pieces, back)

_WEIGHTS = {
    "a0_q": "L0_attn_a_Wq", "a0_k": "L0_attn_a_Wk", "a0_v": "L0_attn_a_Wv", "a0_o": "L0_attn_a_Wo",
    "f0": "L0_ffn_weight", "f0_s": "L0_ffn_scale_weight", "f0_b": "L0_ffn_bias",
    "b0_q": "L0_attn_b_Wq", "b0_bq": "L0_attn_b_bq", "b0_k": "L0_attn_b_Wk", "b0_bk": "L0_attn_b_bk",
    "b0_v": "L0_attn_b_Wv", "b0_bv": "L0_attn_b_bv", "b0_o": "L0_attn_b_Wo", "b0_bo": "L0_attn_b_bo",
    "r1_qkvn": "L1_attn_a_qkv_norm_w", "r1_projn": "L1_attn_a_proj_norm_w", "r1_nw": "L1_attn_a_norm_w", "r1_s": "L1_attn_a_s",
    "b1_q": "L1_attn_b_Wq", "b1_k": "L1_attn_b_Wk", "b1_v": "L1_attn_b_Wv", "b1_o": "L1_attn_b_Wo", "b1_bo": "L1_attn_b_bo",
    "lq1": "L1_attn_b_lq1", "lq2": "L1_attn_b_lq2", "lk1": "L1_attn_b_lk1", "lk2": "L1_attn_b_lk2",
    "w1": "L1_ffn_W1", "w2": "L1_ffn_W2", "w3": "L1_ffn_W3",
}

_OUT = (8, 256, 256)


def _layouts(inputs):
    import numpy as np

    a = {k: np.asarray(inputs[v]) for k, v in _WEIGHTS.items()}
    half, d, j = np.meshgrid(np.arange(2), np.arange(16), np.arange(8), indexing="ij")
    qk16 = ((half * 8 + j) * 16 + d).ravel()
    d, half, j = np.meshgrid(np.arange(8), np.arange(2), np.arange(16), indexing="ij")
    qk8 = (j * 16 + 2 * d + half).ravel()
    g, half, d = np.meshgrid(np.arange(8), np.arange(2), np.arange(16), indexing="ij")
    v16 = ((half * 8 + g) * 16 + d).ravel()
    qkv = np.asarray(inputs["L1_attn_a_qkv_w"])
    proj = np.asarray(inputs["L1_attn_a_proj_w"])
    a["a0_q"], a["a0_k"] = a["a0_q"].T[:, qk16], a["a0_k"].T[:, qk16]
    a["a0_v"], a["a0_o"] = a["a0_v"].T[:, v16], a["a0_o"].T[v16]
    a["r1_q"], a["r1_k"], a["r1_v"] = qkv[:256].T[:, qk16], qkv[256:512].T[:, qk16], qkv[512:].T[:, v16]
    a["r1_o"] = proj.T[v16]
    a["r1_nw"], a["r1_projn"] = a["r1_nw"][v16], a["r1_projn"][v16]
    a["b1_q"], a["b1_k"] = a["b1_q"].T[:, qk8], a["b1_k"].T[:, qk8]
    for n in ("b1_v", "b1_o", "f0", "w1", "w2", "w3"):
        a[n] = a[n].T
    for n in ("b0_bq", "b0_bk", "r1_qkvn", "r1_projn"):
        a[n] = a[n].reshape(2, 128).T
    a["hidden"] = np.asarray(inputs["L0_attn_a_hidden_states"])
    a["ident"] = np.eye(128, dtype=np.float32)
    h = np.ones((1, 1), np.float32)
    while h.shape[0] < 128:
        h = np.block([[h, h], [h, -h]])
    a["had"] = h.astype(np.float32)
    t, k = np.arange(256)[None, :], np.arange(128)[:, None]
    a["caus"] = (t >= k).astype(np.float32)
    a["diff"] = np.maximum(t - k, 0).astype(np.float32)
    a["sel"] = np.repeat(np.eye(128, 4, dtype=np.float32), 128, axis=1)
    return {k: np.ascontiguousarray(v) for k, v in a.items()}


def kernel(**inputs):
    import numpy as _np
    import concourse.bacc as _bacc
    from concourse.bass_utils import run_bass_kernel_spmd as _run

    nc = _bacc.Bacc("TRN2", target_bir_lowering=False, num_devices=1)
    arrays, T = {}, {}
    for name, a in _layouts(inputs).items():
        arrays[f"in_{name}"] = a
        T[name] = nc.dram_tensor(f"in_{name}", a.shape, mybir.dt.from_np(a.dtype), kind="ExternalInput").ap()
    out = nc.dram_tensor("out_0_dram", _OUT, F32, kind="ExternalOutput").ap()
    build(nc, T, out)
    r = _run(nc, [arrays], core_ids=[0])
    return r.results[0]["out_0_dram"]
```
